# Optimizing a Trainium2 kernel written in Bass

```python
import numpy as np
import jax
import jax.numpy as jnp

def _softmax(x, axis=-1):
    return jax.nn.softmax(x, axis=axis)
def _gelu(x):
    return jax.nn.gelu(x, approximate=True)
def _silu(x):
    return jax.nn.silu(x)
def _sigmoid(x):
    return jax.nn.sigmoid(x)
def _layernorm(x, axis=-1, eps=1e-5):
    m = jnp.mean(x, axis=axis, keepdims=True)
    v = jnp.var(x, axis=axis, keepdims=True)
    return (x - m) / jnp.sqrt(v + eps)
def _scatter_add(tgt, idx, src, axis=0):
    return tgt.at[idx].add(src)
def _segment_sum(src, seg, n):
    return jax.ops.segment_sum(src, seg, n)

kernel_name = 'mk_conv_preact_d4_conv_nchw256_781671'

def setup_inputs(seed: int = 0):
    np.random.seed(seed)
    _w = jnp.asarray
    def _rec_inputs():
        import jax
        import jax.numpy as jnp
        _gk = jax.random.key(seed)
        x = -0.0002928 + 1 * jax.random.normal(jax.random.fold_in(_gk, 1), (4, 256, 64, 64), jnp.float32)
        return x
    x = _rec_inputs()
    def _L0_conv_setup():
        import jax, jax.numpy as jnp
        import numpy as np
        INC, OUTC, NHEADS, KSIZE = (256, 256, 8, 5)
        key = jax.random.key(seed)
        k1, k2 = jax.random.split(key, 2)
        x = jax.random.normal(k1, (4, INC, 64, 64), dtype=jnp.float32)
        w_qkv = jax.random.normal(k2, (3 * OUTC, INC), dtype=jnp.float32) * 0.02
        b_qkv = jnp.zeros((3 * OUTC,), dtype=jnp.float32)
        return {'x': x, 'w_qkv': w_qkv, 'b_qkv': b_qkv}
    _L0_conv_all = _L0_conv_setup()
    _L0_conv_in = {k: v for k, v in _L0_conv_all.items() if k in ('w_qkv', 'b_qkv', )}
    del _L0_conv_all

    def _L1_conv_setup():
        import jax, jax.numpy as jnp
        import numpy as np
        from jax import lax
        DIM = 8
        HEADS = 32
        SCALE = 5
        EPS = 1e-15

        def _conv2d(x, w, groups=1, pad=0):
            return lax.conv_general_dilated(x, w, window_strides=(1, 1), padding=[(pad, pad), (pad, pad)], dimension_numbers=('NCHW', 'OIHW', 'NCHW'), feature_group_count=groups)
        key = jax.random.key(seed)
        ks = jax.random.split(key, 5)
        B, C, H, W = (8, 256, 64, 64)
        td = HEADS * DIM
        x = jax.random.normal(ks[0], (B, C, H, W), jnp.float32)
        w_qkv = jax.random.normal(ks[1], (3 * td, C, 1, 1), jnp.float32) * 0.05
        w_dw = jax.random.normal(ks[2], (3 * td, 1, SCALE, SCALE), jnp.float32) * 0.05
        w_pw = jax.random.normal(ks[3], (3 * td, 3 * td // (3 * HEADS), 1, 1), jnp.float32) * 0.1
        w_proj = jax.random.normal(ks[4], (C, td * 2, 1, 1), jnp.float32) * 0.05
        return {'x': x, 'w_qkv': w_qkv, 'w_dw': w_dw, 'w_pw': w_pw, 'w_proj': w_proj}
    _L1_conv_all = _L1_conv_setup()
    _L1_conv_in = {k: v for k, v in _L1_conv_all.items() if k in ('w_qkv', 'w_dw', 'w_pw', 'w_proj', )}
    del _L1_conv_all

    def _L2_conv_setup():
        import jax, jax.numpy as jnp
        import numpy as np
        K = 7
        PAD = 3
        CIN = 256
        COUT = 256
        B, H, W = (2, 48, 48)

        def _unfold2d(x, k):
            Hout = x.shape[2] - k + 1
            Wout = x.shape[3] - k + 1
            rows = jnp.stack([x[:, :, i:i + Hout, :] for i in range(k)], axis=-1)
            return jnp.stack([rows[:, :, :, j:j + Wout, :] for j in range(k)], axis=-1)
        key = jax.random.key(seed)
        ks = jax.random.split(key, 6)
        s = 1.0 / np.sqrt(CIN)
        return {'x': jax.random.normal(ks[0], (B, CIN, H, W), jnp.float32), 'w_q': jax.random.normal(ks[1], (COUT, CIN), jnp.float32) * s, 'w_k': jax.random.normal(ks[2], (COUT, CIN), jnp.float32) * s, 'w_v': jax.random.normal(ks[3], (COUT, CIN), jnp.float32) * s, 'rel_h': jax.random.normal(ks[4], (COUT // 2, 1, 1, K, 1), jnp.float32), 'rel_w': jax.random.normal(ks[5], (COUT // 2, 1, 1, 1, K), jnp.float32)}
    _L2_conv_all = _L2_conv_setup()
    _L2_conv_in = {k: v for k, v in _L2_conv_all.items() if k in ('w_q', 'w_k', 'w_v', 'rel_h', 'rel_w', )}
    del _L2_conv_all

    def _L3_conv_setup():
        import jax, jax.numpy as jnp
        import numpy as np
        K = 4
        TEMP = 0.5
        PAD = 1

        def _dyn_conv(x, w1, w2, b2, weight):
            B, C, H, W = x.shape
            Kk, O = (weight.shape[0], weight.shape[1])
            pooled = jnp.mean(x, axis=(2, 3))
            h = jax.nn.relu(pooled @ w1.T)
            logits = (h @ w2.T + b2).reshape(B, Kk, O)
            attn = jax.nn.softmax(logits / TEMP, axis=1)
            agg_w = jnp.einsum('bko,kocij->bocij', attn, weight)

            def conv1(xi, wi):
                return jax.lax.conv_general_dilated(xi[None], wi, window_strides=(1, 1), padding=[(PAD, PAD), (PAD, PAD)], dimension_numbers=('NCHW', 'OIHW', 'NCHW'))[0]
            return jax.vmap(conv1)(x, agg_w)
        key = jax.random.key(seed)
        ks = jax.random.split(key, 5)
        B, C, H, W = (32, 256, 64, 64)
        O, HID = (256, 65)
        x = jax.random.normal(ks[0], (B, C, H, W), dtype=jnp.float32)
        w1 = jax.random.normal(ks[1], (HID, C), dtype=jnp.float32) * 0.05
        w2 = jax.random.normal(ks[2], (K * O, HID), dtype=jnp.float32) * 0.05
        b2 = jnp.zeros((K * O,), dtype=jnp.float32)
        weight = jax.random.normal(ks[3], (K, O, C, 3, 3), dtype=jnp.float32) * 0.05
        return {'x': x, 'w1': w1, 'w2': w2, 'b2': b2, 'weight': weight}
    _L3_conv_all = _L3_conv_setup()
    _L3_conv_in = {k: v for k, v in _L3_conv_all.items() if k in ('w1', 'w2', 'b2', 'weight', )}
    del _L3_conv_all

    return {
        "x": x,
        "L0_conv_w_qkv": _L0_conv_in["w_qkv"],
        "L0_conv_b_qkv": _L0_conv_in["b_qkv"],
        "L1_conv_w_qkv": _L1_conv_in["w_qkv"],
        "L1_conv_w_dw": _L1_conv_in["w_dw"],
        "L1_conv_w_pw": _L1_conv_in["w_pw"],
        "L1_conv_w_proj": _L1_conv_in["w_proj"],
        "L2_conv_w_q": _L2_conv_in["w_q"],
        "L2_conv_w_k": _L2_conv_in["w_k"],
        "L2_conv_w_v": _L2_conv_in["w_v"],
        "L2_conv_rel_h": _L2_conv_in["rel_h"],
        "L2_conv_rel_w": _L2_conv_in["rel_w"],
        "L3_conv_w1": _L3_conv_in["w1"],
        "L3_conv_w2": _L3_conv_in["w2"],
        "L3_conv_b2": _L3_conv_in["b2"],
        "L3_conv_weight": _L3_conv_in["weight"],
    }

def reference(x, L0_conv_w_qkv, L0_conv_b_qkv, L1_conv_w_qkv, L1_conv_w_dw, L1_conv_w_pw, L1_conv_w_proj, L2_conv_w_q, L2_conv_w_k, L2_conv_w_v, L2_conv_rel_h, L2_conv_rel_w, L3_conv_w1, L3_conv_w2, L3_conv_b2, L3_conv_weight):
    import jax
    import jax.numpy as jnp
    def _L0_conv_ref(x, w_qkv, b_qkv):
        import jax, jax.numpy as jnp
        import numpy as np
        INC, OUTC, NHEADS, KSIZE = (256, 256, 8, 5)
        N, Cin, H, W = x.shape
        hd = OUTC // NHEADS
        ofs = KSIZE // 2
        K2 = KSIZE * KSIZE
        qkv = jnp.einsum('nchw,dc->ndhw', x, w_qkv) + b_qkv[None, :, None, None]
        Q = qkv[:, :OUTC]
        K = qkv[:, OUTC:2 * OUTC]
        V = qkv[:, 2 * OUTC:]
        Kp = jnp.pad(K, ((0, 0), (0, 0), (ofs, ofs), (ofs, ofs)))
        Vp = jnp.pad(V, ((0, 0), (0, 0), (ofs, ofs), (ofs, ofs)))
        valid = jnp.pad(jnp.ones((H, W), dtype=bool), ((ofs, ofs), (ofs, ofs)))
        k_win = jnp.stack([Kp[:, :, dy:dy + H, dx:dx + W] for dy in range(KSIZE) for dx in range(KSIZE)], axis=-1)
        v_win = jnp.stack([Vp[:, :, dy:dy + H, dx:dx + W] for dy in range(KSIZE) for dx in range(KSIZE)], axis=-1)
        m_win = jnp.stack([valid[dy:dy + H, dx:dx + W] for dy in range(KSIZE) for dx in range(KSIZE)], axis=-1)
        qh = Q.reshape(N, NHEADS, hd, H, W)
        kh = k_win.reshape(N, NHEADS, hd, H, W, K2)
        vh = v_win.reshape(N, NHEADS, hd, H, W, K2)
        scores = jnp.einsum('ngdhw,ngdhwk->nghwk', qh, kh)
        scores = jnp.where(m_win[None, None], scores, -jnp.inf)
        att = jax.nn.softmax(scores, axis=-1)
        out = jnp.einsum('nghwk,ngdhwk->ngdhw', att, vh)
        return out.reshape(N, OUTC, H, W)

    def _L1_conv_ref(x, w_qkv, w_dw, w_pw, w_proj):
        import jax, jax.numpy as jnp
        import numpy as np
        from jax import lax
        DIM = 8
        HEADS = 32
        SCALE = 5
        EPS = 1e-15

        def _conv2d(x, w, groups=1, pad=0):
            return lax.conv_general_dilated(x, w, window_strides=(1, 1), padding=[(pad, pad), (pad, pad)], dimension_numbers=('NCHW', 'OIHW', 'NCHW'), feature_group_count=groups)
        B, C, H, W = x.shape
        td = HEADS * DIM
        qkv = _conv2d(x, w_qkv)
        agg = _conv2d(qkv, w_dw, groups=3 * td, pad=SCALE // 2)
        agg = _conv2d(agg, w_pw, groups=3 * HEADS)
        ms = jnp.concatenate([qkv, agg], axis=1)
        ms = ms.reshape(B, -1, 3 * DIM, H * W).transpose(0, 1, 3, 2)
        q, k, v = jnp.split(ms, 3, axis=-1)
        q = jax.nn.relu(q)
        k = jax.nn.relu(k)
        v = jnp.pad(v, ((0, 0), (0, 0), (0, 0), (0, 1)), constant_values=1.0)
        kv = jnp.einsum('bgnd,bgne->bgde', k, v)
        out = jnp.einsum('bgnd,bgde->bgne', q, kv)
        out = out[..., :-1] / (out[..., -1:] + EPS)
        out = out.transpose(0, 1, 3, 2).reshape(B, -1, H, W)
        return _conv2d(out, w_proj)

    def _L2_conv_ref(x, w_q, w_k, w_v, rel_h, rel_w):
        import jax, jax.numpy as jnp
        import numpy as np
        K = 7
        PAD = 3
        CIN = 256
        COUT = 256
        B, H, W = (2, 48, 48)

        def _unfold2d(x, k):
            Hout = x.shape[2] - k + 1
            Wout = x.shape[3] - k + 1
            rows = jnp.stack([x[:, :, i:i + Hout, :] for i in range(k)], axis=-1)
            return jnp.stack([rows[:, :, :, j:j + Wout, :] for j in range(k)], axis=-1)
        b, cin, h, w = x.shape
        cout = w_q.shape[0]
        half = cout // 2
        x_pad = jnp.pad(x, ((0, 0), (0, 0), (PAD, PAD), (PAD, PAD)))
        q = jnp.einsum('bchw,oc->bohw', x, w_q)
        kmap = jnp.einsum('bchw,oc->bohw', x_pad, w_k)
        vmap = jnp.einsum('bchw,oc->bohw', x_pad, w_v)
        kwin = _unfold2d(kmap, K)
        vwin = _unfold2d(vmap, K)
        kwin = jnp.concatenate([kwin[:, :half] + rel_h, kwin[:, half:] + rel_w], axis=1)
        kwin = kwin.reshape(b, cout, h, w, K * K)
        vwin = vwin.reshape(b, cout, h, w, K * K)
        attn = jax.nn.softmax(q[..., None] * kwin, axis=-1)
        out = jnp.sum(attn * vwin, axis=-1)
        return out

    def _L3_conv_ref(x, w1, w2, b2, weight):
        import jax, jax.numpy as jnp
        import numpy as np
        K = 4
        TEMP = 0.5
        PAD = 1

        def _dyn_conv(x, w1, w2, b2, weight):
            B, C, H, W = x.shape
            Kk, O = (weight.shape[0], weight.shape[1])
            pooled = jnp.mean(x, axis=(2, 3))
            h = jax.nn.relu(pooled @ w1.T)
            logits = (h @ w2.T + b2).reshape(B, Kk, O)
            attn = jax.nn.softmax(logits / TEMP, axis=1)
            agg_w = jnp.einsum('bko,kocij->bocij', attn, weight)

            def conv1(xi, wi):
                return jax.lax.conv_general_dilated(xi[None], wi, window_strides=(1, 1), padding=[(PAD, PAD), (PAD, PAD)], dimension_numbers=('NCHW', 'OIHW', 'NCHW'))[0]
            return jax.vmap(conv1)(x, agg_w)
        return _dyn_conv(x, w1, w2, b2, weight)

    def _gn(v, G=32, eps=1e-5):
        B_, C_, H_, W_ = v.shape
        g = v.reshape(B_, G, C_ // G, H_, W_)
        m = jnp.mean(g, axis=(2, 3, 4), keepdims=True)
        s = jnp.var(g, axis=(2, 3, 4), keepdims=True)
        return ((g - m) / jnp.sqrt(s + eps)).reshape(v.shape)

    def _ln_c(v, eps=1e-6):
        m = jnp.mean(v, axis=1, keepdims=True)
        s = jnp.var(v, axis=1, keepdims=True)
        return (v - m) / jnp.sqrt(s + eps)

    def _ln_t(v, eps=1e-5):
        m = jnp.mean(v, axis=-1, keepdims=True)
        s = jnp.var(v, axis=-1, keepdims=True)
        return (v - m) / jnp.sqrt(s + eps)

    def _to_tokens(v):
        B_, C_, H_, W_ = v.shape
        return v.reshape(B_, C_, H_ * W_).transpose(0, 2, 1)
    def _from_tokens(t, like):
        B_, C_, H_, W_ = like.shape
        return t.transpose(0, 2, 1).reshape(B_, C_, H_, W_)

    x = x + _L0_conv_ref(_gn(x), L0_conv_w_qkv, L0_conv_b_qkv)
    x = x + _L1_conv_ref(_gn(x), L1_conv_w_qkv, L1_conv_w_dw, L1_conv_w_pw, L1_conv_w_proj)
    x = x + _L2_conv_ref(_gn(x), L2_conv_w_q, L2_conv_w_k, L2_conv_w_v, L2_conv_rel_h, L2_conv_rel_w)
    x = x + _L3_conv_ref(_gn(x), L3_conv_w1, L3_conv_w2, L3_conv_b2, L3_conv_weight)
    return x


_drawn_inputs = setup_inputs


def setup_inputs(seed=0):
    import zlib

    import numpy as np

    out = dict(_drawn_inputs(seed))
    spreads = {'L0_conv_b_qkv': (0.0, 0.1), 'L3_conv_b2': (0.0, 0.1)}
    factors = {'L1_conv_w_dw': 8.0, 'L1_conv_w_pw': 8.0}
    for name, (base, spread) in spreads.items():
        noise = np.random.default_rng([zlib.crc32(name.encode()), seed]).standard_normal(out[name].shape)
        drawn = base * np.exp(spread * noise) if base else spread * noise
        out[name] = jnp.asarray(drawn.astype(out[name].dtype))
    for name, factor in factors.items():
        out[name] = (out[name] * factor).astype(out[name].dtype)
    return out
```

```python
import concourse.bass as bass
from concourse import mybir
from concourse.alu_op_type import AluOpType as ALU
from contextlib import ExitStack, contextmanager
import numpy as np

ACT = mybir.ActivationFunctionType
AX = mybir.AxisListType
F32 = mybir.dt.float32
F32R = mybir.dt.float32r

B, C, HH, WW = 4, 256, 64, 64
NPX = HH * WW
PART = 128
HALVES = C // PART
PAD = 3
PW = WW + 2 * PAD
PPX = (HH + 2 * PAD) * PW
EPS = 1e-5


NORM_PAIRS = ("x_loaded", "stats_ready", "group_ready", "var_ready", "std_ready", "coef_ready", "norm_done",
              "xn_stored", "pooled_stored")


def norm_semaphores(nc):
    sems = {n: [nc.alloc_semaphore(name=f"n_{n}{h}") for h in range(HALVES)] for n in NORM_PAIRS}
    return sems | {n: nc.alloc_semaphore(name=f"n_{n}") for n in ("gm_loaded", "border_zero", "chain")}


def group_norm(nc, sems, call, x_in, xn_out, mean_matrix, pooled=None):
    tag = f"n{call}"
    before = call * B
    (x_loaded, stats_ready, group_ready, var_ready, std_ready, coef_ready, norm_done, xn_stored,
     pooled_stored) = (sems[n] for n in NORM_PAIRS)
    gm_loaded, border_zero, chain = sems["gm_loaded"], sems["border_zero"], sems["chain"]
    ctx = ExitStack()
    with ctx:
        sb = lambda n, s, dt=F32: ctx.enter_context(nc.sbuf_tensor(f"{tag}_{n}", s, dt))
        xt = [sb(f"xt{h}", [PART, NPX]) for h in range(HALVES)]
        xnp = [sb(f"xnp{h}", [PART, PPX]) for h in range(HALVES)]
        stats = [sb(f"stats{h}", [PART, NPX // 512, 6]) for h in range(HALVES)]
        ms = [sb(f"ms{h}", [PART, 2]) for h in range(HALVES)]
        gs = [sb(f"gs{h}", [PART, 2]) for h in range(HALVES)]
        var = [sb(f"var{h}", [PART, 1]) for h in range(HALVES)]
        std = [sb(f"std{h}", [PART, 1]) for h in range(HALVES)]
        coef = [sb(f"coef{h}", [PART, 2]) for h in range(HALVES)]
        pool_t = [sb(f"pool{h}", [PART, 1]) for h in range(HALVES)]
        wait_taker = sb("wait_taker", [PART, 1])
        gm = sb("gm", [PART, PART])
        psum = ctx.enter_context(nc.psum_tensor(f"{tag}_psum", [PART, HALVES, 512], F32))
        block = ctx.enter_context(nc.Block())

        @block.sync
        def _(sp):
            sp.dma_start(gm[:], mean_matrix).then_inc(gm_loaded, 16)
            with sp.Fori(0, B) as b:
                for h in range(HALVES):
                    sp.wait_ge(norm_done[h], before + b)
                    sp.dma_start(xt[h][:], x_in[bass.ds(b, 1), h * PART:(h + 1) * PART, :]
                                 .rearrange("b p n -> (b p) n")).then_inc(x_loaded[h], 16)

        @block.gpsimd
        def _(pool):
            pool.memset(xnp[0][:], 0.0).then_inc(border_zero, 1)
            pool.memset(xnp[1][:], 0.0).then_inc(border_zero, 1)
            with pool.Fori(0, B) as b:
                for h in range(HALVES):
                    pool.wait_ge(norm_done[h], before + b + 1)
                    pool.dma_start(xn_out[bass.ds(b, 1), h * PART:(h + 1) * PART, :]
                                   .rearrange("b p n -> (b p) n"), xnp[h][:]).then_inc(xn_stored[h], 16)
                    if pooled is not None:
                        pool.wait_ge(coef_ready[h], before + b + 1)
                        pool.dma_start(pooled[bass.ds(b, 1), h * PART:(h + 1) * PART]
                                       .rearrange("b p -> p b"), pool_t[h][:]).then_inc(pooled_stored[h], 16)
            for h in range(HALVES):
                pool.wait_ge(xn_stored[h], 16 * (before + B))
                if pooled is not None:
                    pool.wait_ge(pooled_stored[h], 16 * B)

        @block.vector
        def _(dve):
            STEPS0 = 1 + 4 * HALVES
            STEPS = STEPS0 + (HALVES if pooled is not None else 0)
            with dve.Fori(0, B) as b:
                n = [0]

                def link(ins):
                    n[0] += 1
                    ins.then_inc(chain, 1)
                    dve.wait_ge(chain, before * STEPS0 + b * STEPS + n[0])

                for h in range(HALVES):
                    dve.wait_ge(x_loaded[h], (before + b + 1) * 16)
                    for k in range(NPX // 512):
                        ins = nc.vector.bn_stats(stats[h][:, k, :], xt[h][:, k * 512:(k + 1) * 512])
                    link(ins)
                nc.vector.memset(wait_taker[:], 0.0)
                for h in range(HALVES):
                    ins = nc.vector.bn_aggr(ms[h][:], stats[h][:])
                link(ins)
                for h in range(HALVES):
                    nc.vector.scalar_tensor_tensor(ms[h][:, 1:2], ms[h][:, 0:1], ms[h][:, 0:1], ms[h][:, 1:2],
                                                   ALU.mult, ALU.add).then_inc(stats_ready[h], 1)
                for h in range(HALVES):
                    dve.wait_ge(group_ready[h], before + b + 1)
                    link(nc.vector.tensor_copy(gs[h][:], psum[:, h, 0:2]))
                    link(nc.vector.scalar_tensor_tensor(var[h][:], gs[h][:, 0:1], gs[h][:, 0:1], gs[h][:, 1:2],
                                                        ALU.mult, ALU.subtract))
                    nc.vector.tensor_scalar(var[h][:], var[h][:], -1.0, EPS, ALU.mult, ALU.add)\
                        .then_inc(var_ready[h], 1)
                for h in range(HALVES):
                    dve.wait_ge(std_ready[h], before + b + 1)
                    link(nc.vector.reciprocal(coef[h][:, 0:1], std[h][:]))
                    if pooled is not None:
                        dve.wait_ge(pooled_stored[h], b * 16)
                        link(nc.vector.tensor_scalar(pool_t[h][:], ms[h][:, 0:1], gs[h][:, 0:1],
                                                     coef[h][:, 0:1], ALU.subtract, ALU.mult))
                    nc.vector.tensor_scalar(coef[h][:, 1:2], gs[h][:, 0:1], coef[h][:, 0:1], -1.0,
                                            ALU.mult, ALU.mult).then_inc(coef_ready[h], 1)

        @block.tensor
        def _(pe):
            pe.wait_ge(gm_loaded, (call + 1) * 16)
            with pe.Fori(0, B) as b:
                for h in range(HALVES):
                    pe.wait_ge(stats_ready[h], before + b + 1)
                    nc.tensor.matmul(psum[:, h, 0:2], lhsT=gm[:], rhs=ms[h][:], start=True, stop=True)\
                        .then_inc(group_ready[h], 1)

        @block.scalar
        def _(act):
            act.wait_ge(border_zero, (call + 1) * 2)
            with act.Fori(0, B) as b:
                for h in range(HALVES):
                    act.wait_ge(var_ready[h], before + b + 1)
                    nc.scalar.activation(std[h][:], var[h][:], ACT.Sqrt).then_inc(std_ready[h], 1)
                for h in range(HALVES):
                    act.wait_ge(coef_ready[h], before + b + 1)
                    act.wait_ge(xn_stored[h], (before + b) * 16)
                    inner = xnp[h][:].rearrange("p (r c) -> p r c", c=PW)[:, PAD:PAD + HH, PAD:PAD + WW]
                    nc.scalar.activation(inner, xt[h][:].rearrange("p (r c) -> p r c", c=WW), ACT.Identity,
                                         bias=coef[h][:, 1:2], scale=coef[h][:, 0:1]).then_inc(norm_done[h], 1)


def group_mean():
    g = np.arange(PART) // (C // 32)
    return (g[:, None] == g[None, :]).astype(np.float32) / np.float32(C // 32)


HEADS0, HD0, K0 = 8, 32, 5
TR, TC = 8, 16
TQ = TR * TC
KR, KC = TR + K0 - 1, TC + K0 - 1
NK = KR * KC
KCH = NK // 2
TILES = WW // TC
BROWS = TR + K0 - 1
BAND0 = TR * WW


def attention_masks():
    qr, qc = np.divmod(np.arange(TQ), TC)
    kr, kc = np.divmod(np.arange(NK), KC)
    near = (np.abs(kr[None] - qr[:, None] - K0 // 2) <= K0 // 2) & (np.abs(kc[None] - qc[:, None] - K0 // 2) <= K0 // 2)
    out = np.zeros((HH // TR, TQ, TILES, NK), np.float32)
    for r in range(HH // TR):
        for c in range(TILES):
            y, x = r * TR + kr - K0 // 2, c * TC + kc - K0 // 2
            inside = (y >= 0) & (y < HH) & (x >= 0) & (x < WW)
            out[r, :, c] = np.where(near & inside[None], 0.0, -1e30)
    return out


def window_attention(nc, xn, x_in, x_out, w_qkv_t, b_qkv, masks, ident_in):
    ctx = ExitStack()
    with ctx:
        sb = lambda n, s, dt=F32: ctx.enter_context(nc.sbuf_tensor(f"a_{n}", s, dt))
        pb = lambda n, s: ctx.enter_context(nc.psum_tensor(f"a_{n}", s, F32))
        sem = lambda n: nc.alloc_semaphore(name=f"a_{n}")
        wt = sb("wt", [PART, HALVES, 3 * C])
        bias = sb("bias", [PART, 3 * HALVES])
        wait_taker = sb("wait_taker", [PART, 2])
        ident = sb("ident", [PART, PART])
        xb = [sb(f"xb{u}", [PART, HALVES, BROWS * PW]) for u in range(2)]
        xr = [sb(f"xr{u}", [PART, HALVES, BAND0]) for u in range(2)]
        mk = [sb(f"mk{u}", [TQ, TILES, NK]) for u in range(2)]
        xk = [sb(f"xk{u}", [PART, HALVES, NK]) for u in range(2)]
        qk = [sb(f"qk{u}", [PART, HALVES, TQ + NK]) for u in range(2)]
        vt = [sb(f"vt{u}", [KCH, 2, C]) for u in range(2)]
        ms = [sb(f"ms{i}", [TQ, 2, NK]) for i in range(3)]
        pr = [sb(f"pr{i}", [TQ, 2, NK]) for i in range(3)]
        nmax = [sb(f"nmax{i}", [TQ, 2]) for i in range(3)]
        den = [sb(f"den{u}", [TQ, HEADS0]) for u in range(2)]
        rden = sb("rden", [TQ, HEADS0])
        pt = [sb(f"pt{i}", [KCH, 4, TQ]) for i in range(2)]
        on = [sb(f"on{u}", [TQ, C]) for u in range(2)]
        pqk = pb("pqk", [PART, 2, 512])
        pv = pb("pv", [PART, 512])
        ps = pb("ps", [PART, 2, 512])
        ppt = pb("ppt", [PART, 512])
        po = pb("po", [PART, 512])
        pot = pb("pot", [PART, 512])
        consts_in = sem("consts_in")
        band_in = [sem(f"band_in{u}") for u in range(2)]
        rest_in = [sem(f"rest_in{u}") for u in range(2)]
        out_stored = [sem(f"out_stored{u}") for u in range(2)]
        taker_ready = sem("taker_ready")
        area_ready = sem("area_ready")
        projected = sem("projected")
        qk_copied = sem("qk_copied")
        v_copied = sem("v_copied")
        scored = sem("scored")
        masked = [sem(f"masked{u}") for u in range(2)]
        max_ready = sem("max_ready")
        exp_done = sem("exp_done")
        turned = sem("turned")
        turned_copied = sem("turned_copied")
        weighted = sem("weighted")
        recip_ready = sem("recip_ready")
        normalised = sem("normalised")
        turned_back = sem("turned_back")
        added = sem("added")

        NT = 2 * TILES
        NP = HEADS0 // 2
        BP = TILES * NP
        TURNS = HH // TR // 2
        LAG = 2
        block = ctx.enter_context(nc.Block())

        @contextmanager
        def turn(eng):
            with eng.Fori(0, B) as b, eng.Fori(0, TURNS) as r:
                yield b, r, b * TURNS + r

        @block.sync
        def _(sp):
            sp.dma_start(wt[:], w_qkv_t.rearrange("(h p) o -> p h o", p=PART)).then_inc(consts_in, 16)
            sp.dma_start(bias[:], b_qkv.rearrange("(m p) -> p m", p=PART), allow_slow_non_contiguous=True).then_inc(consts_in, 16)
            sp.dma_start(ident[:], ident_in).then_inc(consts_in, 16)
            with turn(sp) as (b, rr, n):
                for u in range(2):
                    sp.wait_ge(area_ready, n * NT)
                    first = (PAD - K0 // 2 + u * TR) * PW
                    sp.dma_start(xb[u][:], xn[bass.ds(b, 1), :, bass.ds(rr * (2 * TR * PW) + first, BROWS * PW)]
                                 .rearrange("b (h p) n -> p (b h) n", p=PART)).then_inc(band_in[u], 16)
                    sp.wait_ge(masked[u], n * BP)
                    sp.dma_start(mk[u][:], masks[bass.ds(rr * 2 + u, 1)]
                                 .rearrange("r q c k -> (r q) c k")).then_inc(rest_in[u], 16)
                    sp.wait_ge(out_stored[u], n * 16)
                    sp.dma_start(xr[u][:], x_in[bass.ds(b, 1), :, bass.ds(rr * (2 * BAND0) + u * BAND0, BAND0)]
                                 .rearrange("b (h p) n -> p (b h) n", p=PART)).then_inc(rest_in[u], 16)

        @block.gpsimd
        def _(pool):
            nc.gpsimd.memset(wait_taker[:], 0.0).then_inc(taker_ready, 1)
            pool.wait_ge(taker_ready, 1)
            with turn(pool) as (b, rr, n):
                for t in range(NT):
                    u, c = divmod(t, TILES)
                    if c == 0:
                        pool.wait_ge(band_in[u], n * 16 + 16)
                    pool.wait_ge(projected, n * NT + max(t - 1, 0))
                    pool.wait_ge(area_ready, n * NT + t)
                    nc.gpsimd.tensor_tensor(wait_taker[:, 0:1], wait_taker[:, 1:2], wait_taker[:, 1:2], ALU.add)
                    k0 = PAD - K0 // 2 + c * TC
                    for h in range(HALVES):
                        last = nc.gpsimd.tensor_copy(xk[t % 2][:, h, :].rearrange("p (r c) -> p r c", c=KC),
                                                     xb[u][:, h, :].rearrange("p (r c) -> p r c", c=PW)[:, :, k0:k0 + KC])
                    last.then_inc(area_ready, 1)
                for u in range(2):
                    pool.wait_ge(added, n * NT + (u + 1) * TILES)
                    pool.dma_start(x_out[bass.ds(b, 1), :, bass.ds(rr * (2 * BAND0) + u * BAND0, BAND0)]
                                   .rearrange("b (h p) n -> p (b h) n", p=PART), xr[u][:]).then_inc(out_stored[u], 16)
            for u in range(2):
                pool.wait_ge(out_stored[u], 16 * B * TURNS)

        @block.tensor
        def _(pe):
            pe.wait_ge(consts_in, 48)
            with turn(pe) as (b, rr, n):
                def project(t):
                    u, c = divmod(t, TILES)
                    pe.wait_ge(area_ready, n * NT + t + 1)
                    pe.wait_ge(qk_copied, n * NT + t)
                    pe.wait_ge(v_copied, n * NT + t)
                    area = xk[t % 2]
                    grid = area[:].rearrange("p h (r c) -> p h r c", c=KC)
                    own = grid[:, :, K0 // 2:K0 // 2 + TR, K0 // 2:K0 // 2 + TC]
                    for m in range(HALVES):
                        for h in range(HALVES):
                            nc.tensor.matmul(pqk[:, m, 0:TQ].rearrange("p (r c) -> p r c", c=TC),
                                             lhsT=wt[:, h, m * PART:(m + 1) * PART], rhs=own[:, h],
                                             start=h == 0, stop=h == HALVES - 1)
                        for h in range(HALVES):
                            nc.tensor.matmul(pqk[:, m, TQ:TQ + NK], lhsT=wt[:, h, C + m * PART:C + (m + 1) * PART],
                                             rhs=area[:, h, :], start=h == 0, stop=h == HALVES - 1)
                    for j in range(2):
                        for h in range(HALVES):
                            last = nc.tensor.matmul(pv[0:KCH, j * C:(j + 1) * C],
                                                    lhsT=area[:, h, j * KCH:(j + 1) * KCH],
                                                    rhs=wt[:, h, 2 * C:3 * C], start=h == 0, stop=h == HALVES - 1)
                    last.then_inc(projected, 1)

                def scores(P):
                    t, p = divmod(P, NP)
                    if p == 0:
                        pe.wait_ge(qk_copied, n * NT + t + 1)
                    if P >= 2:
                        pe.wait_ge(masked[(P - 2) // BP], n * BP + (P - 2) % BP + 1)
                    else:
                        pe.wait_ge(masked[1], n * BP)
                    for e in range(2):
                        s = slice(p * HD0, (p + 1) * HD0)
                        last = nc.tensor.matmul(ps[0:TQ, P % 2, e * NK:(e + 1) * NK], lhsT=qk[t % 2][s, e, 0:TQ],
                                                rhs=qk[t % 2][s, e, TQ:TQ + NK], start=True, stop=True)
                    last.then_inc(scored, 1)

                def turned_exps(P):
                    pe.wait_ge(exp_done, n * NT * NP + P + 1)
                    pe.wait_ge(turned_copied, n * NT * NP + P)
                    for e in range(2):
                        for j in range(2):
                            k = 2 * e + j
                            last = nc.tensor.transpose(ppt[0:KCH, k * TQ:(k + 1) * TQ],
                                                       pr[P % 3][:, e, j * KCH:(j + 1) * KCH], ident[:])
                    last.then_inc(turned, 1)

                def weigh(P):
                    t, p = divmod(P, NP)
                    pe.wait_ge(turned_copied, n * NT * NP + P + 1)
                    if p == 0:
                        pe.wait_ge(v_copied, n * NT + t + 1)
                        pe.wait_ge(normalised, n * NT + t)
                    for e in range(2):
                        s = slice((e * NP + p) * HD0, (e * NP + p + 1) * HD0)
                        for j in range(2):
                            last = nc.tensor.matmul(po[0:TQ, s], lhsT=pt[P % 2][:, 2 * e + j, :],
                                                    rhs=vt[t % 2][:, j, s], start=j == 0, stop=j == 1)
                    last.then_inc(weighted, 1)

                def back(t):
                    pe.wait_ge(normalised, n * NT + t + 1)
                    pe.wait_ge(added, n * NT + t)
                    for m in range(HALVES):
                        last = nc.tensor.transpose(pot[:, m * TQ:(m + 1) * TQ],
                                                   on[t % 2][:, m * PART:(m + 1) * PART], ident[:])
                    last.then_inc(turned_back, 1)

                project(0)
                for P in range(NT * NP + LAG + 3):
                    if P < NT * NP:
                        scores(P)
                        if P % NP == 1 and P // NP + 1 < NT:
                            project(P // NP + 1)
                    if 0 <= P - LAG < NT * NP:
                        turned_exps(P - LAG)
                    if 0 <= P - LAG - 1 < NT * NP:
                        weigh(P - LAG - 1)
                    if P - LAG - 2 >= 0 and (P - LAG - 2) % NP == NP - 1:
                        back((P - LAG - 2) // NP)

        @block.scalar
        def _(act):
            act.wait_ge(consts_in, 48)
            with turn(act) as (b, rr, n):
                def copy_qkv(t):
                    act.wait_ge(projected, n * NT + t + 1)
                    act.wait_ge(weighted, (n * NT + max(t - 1, 0)) * NP)
                    for m in range(HALVES):
                        nc.scalar.activation(qk[t % 2][:, m, 0:TQ], pqk[:, m, 0:TQ], ACT.Identity,
                                             bias=bias[:, m:m + 1])
                        last = nc.scalar.activation(qk[t % 2][:, m, TQ:TQ + NK], pqk[:, m, TQ:TQ + NK], ACT.Identity,
                                                    bias=bias[:, HALVES + m:HALVES + m + 1])
                    last.then_inc(qk_copied, 1)
                    nc.scalar.activation(vt[t % 2][:].rearrange("p j c -> p (j c)"), pv[0:KCH, :], ACT.Copy)\
                        .then_inc(v_copied, 1)

                copy_qkv(0)
                for P in range(NT * NP):
                    t, p = divmod(P, NP)
                    if p == 2 and t + 1 < NT:
                        copy_qkv(t + 1)
                    act.wait_ge(max_ready, n * NT * NP + P + 1)
                    act.wait_ge(turned, n * NT * NP + max(P - 2, 0))
                    if p == 0:
                        act.wait_ge(recip_ready, n * NT + max(t - 1, 0))
                    for e in range(2):
                        last = nc.scalar.activation(pr[P % 3][:, e, :], ms[P % 3][:, e, :], ACT.Exp,
                                                    bias=nmax[P % 3][:, e:e + 1],
                                                    accum_out=den[t % 2][:, e * NP + p:e * NP + p + 1])
                    last.then_inc(exp_done, 1)

        @block.vector
        def _(dve):
            dve.wait_ge(consts_in, 48)
            with turn(dve) as (b, rr, n):
                def mask(P):
                    t, p = divmod(P, NP)
                    u, c = divmod(t, TILES)
                    if c == 0 and p == 0:
                        dve.wait_ge(rest_in[u], n * 32 + 32)
                    dve.wait_ge(scored, n * NT * NP + P + 1)
                    dve.wait_ge(exp_done, n * NT * NP + max(P - 2, 0))
                    ins = nc.vector.tensor_tensor(ms[P % 3][:], ps[0:TQ, P % 2, 0:2 * NK].rearrange("p (e k) -> p e k", e=2),
                                                  mk[u][:, c:c + 1, :].to_broadcast([TQ, 2, NK]), ALU.add)
                    ins.then_inc(masked[u], 1)

                def maximum(P):
                    dve.wait_ge(masked[P // BP], n * BP + P % BP + 1)
                    nc.vector.tensor_reduce(nmax[P % 3][:], ms[P % 3][:], AX.X, ALU.max, negate=True).then_inc(max_ready, 1)

                def copy_turned(P):
                    dve.wait_ge(turned, n * NT * NP + P + 1)
                    dve.wait_ge(weighted, n * NT * NP + max(P - 1, 0))
                    nc.vector.tensor_copy(pt[P % 2][:].rearrange("p k q -> p (k q)"), ppt[0:KCH, :]).then_inc(turned_copied, 1)

                def normalise(t):
                    dve.wait_ge(exp_done, (n * NT + t + 1) * NP)
                    dve.wait_ge(normalised, n * NT + t)
                    nc.vector.reciprocal(rden[:], den[t % 2][:]).then_inc(recip_ready, 1)
                    dve.wait_ge(weighted, (n * NT + t + 1) * NP)
                    dve.wait_ge(recip_ready, n * NT + t + 1)
                    dve.wait_ge(turned_back, n * NT + max(t - 1, 0))
                    nc.vector.tensor_tensor(on[t % 2][:].rearrange("p (g d) -> p g d", d=HD0),
                                            po[0:TQ, 0:C].rearrange("p (g d) -> p g d", d=HD0),
                                            rden[:].rearrange("p (g o) -> p g o", o=1).to_broadcast([TQ, HEADS0, HD0]),
                                            ALU.mult).then_inc(normalised, 1)

                def add(t):
                    u, c = divmod(t, TILES)
                    dve.wait_ge(turned_back, n * NT + t + 1)
                    for m in range(HALVES):
                        res = xr[u][:, m, :].rearrange("p (r c) -> p r c", c=WW)[:, :, c * TC:(c + 1) * TC]
                        last = nc.vector.scalar_tensor_tensor(
                            res, pot[:, m * TQ:(m + 1) * TQ].rearrange("p (r c) -> p r c", c=TC),
                            bias[:, 2 * HALVES + m:2 * HALVES + m + 1], res, ALU.add, ALU.add)
                    last.then_inc(added, 1)

                for P in range(NT * NP + LAG + 3):
                    if P < NT * NP:
                        mask(P)
                    if 0 <= P - LAG < NT * NP:
                        copy_turned(P - LAG)
                    if P < NT * NP:
                        maximum(P)
                    if P - LAG - 1 >= 0 and (P - LAG - 1) % NP == NP - 1:
                        normalise((P - LAG - 1) // NP)
                    if P - LAG - 2 >= 0 and (P - LAG - 2) % NP == NP - 1:
                        add((P - LAG - 2) // NP)


G8 = 8
C3 = 3 * C
GROUPS = C3 // G8
GPX = HH * G8 * WW
TG = PART // G8
CHUNK = 512
CROWS = CHUNK // WW


def qkv_project(nc, xn, qkv, w_t):
    ctx = ExitStack()
    with ctx:
        sb = lambda n, s, dt=F32: ctx.enter_context(nc.sbuf_tensor(f"b_{n}", s, dt))
        sem = lambda n: nc.alloc_semaphore(name=f"b_{n}")
        MT = C3 // PART
        NC = NPX // CHUNK
        wt = sb("wt", [PART, HALVES, C3])
        xi = [sb(f"xi{u}", [PART, HALVES, PPX]) for u in range(2)]
        ot = [sb(f"ot{u}", [PART, NPX]) for u in range(2)]
        pq = ctx.enter_context(nc.psum_tensor("b_pq", [PART, 8, 512], F32))
        w_in = sem("w_in")
        image_in = [sem(f"image_in{u}") for u in range(2)]
        product = sem("product")
        copied = [sem("copied_act"), sem("copied_dve")]
        stored = [sem(f"stored{u}") for u in range(2)]
        block = ctx.enter_context(nc.Block())
        TURNS = B // 2
        T = 2 * MT

        @block.gpsimd
        def _(pool):
            with pool.Fori(0, TURNS) as n:
                for u in range(2):
                    pool.wait_ge(product, n * (T * NC))
                    pool.dma_start(xi[u][:], xn[bass.ds(n * 2 + u, 1)].rearrange("b (h p) n -> p (b h) n", p=PART))\
                        .then_inc(image_in[u], 16)

        @block.sync
        def _(sp):
            sp.dma_start(wt[:], w_t.rearrange("(h p) o -> p h o", p=PART)).then_inc(w_in, 16)
            with sp.Fori(0, TURNS) as n:
                for t in range(T):
                    u, m = divmod(t, MT)
                    for k in range(2):
                        sp.wait_ge(copied[k], (n * T + t + 1) * (NC // 2))
                    dst = qkv[bass.ds(n * 2 + u, 1), m * TG:(m + 1) * TG, :].rearrange("b g (r i c) -> i (b g) r c", i=G8, c=WW)
                    src = ot[t % 2][:].rearrange("p (r c) -> p r c", c=WW)
                    for i in range(G8):
                        sp.dma_start(dst[i], src[i * TG:(i + 1) * TG]).then_inc(stored[t % 2], 16)
            for k in range(2):
                sp.wait_ge(stored[k], TURNS * T // 2 * G8 * 16)

        @block.tensor
        def _(pe):
            pe.wait_ge(w_in, 16)
            with pe.Fori(0, TURNS) as n:
                for t in range(T):
                    u, m = divmod(t, MT)
                    if m == 0:
                        pe.wait_ge(image_in[u], n * 16 + 16)
                    rows = xi[u][:].rearrange("p h (r c) -> p h r c", c=PW)
                    for k in range(NC):
                        pe.wait_ge(copied[k % 2], (n * T + max(t - 1, 0)) * (NC // 2) + (k // 2 + 1 if t else 0))
                        for h in range(HALVES):
                            last = nc.tensor.matmul(pq[:, k, :].rearrange("p (r c) -> p r c", c=WW),
                                                    lhsT=wt[:, h, m * PART:(m + 1) * PART],
                                                    rhs=rows[:, h, PAD + k * CROWS:PAD + (k + 1) * CROWS, PAD:PAD + WW],
                                                    start=h == 0, stop=h == HALVES - 1)
                        last.then_inc(product, 1)

        def copy_chunks(eng, copy, which):
            with eng.Fori(0, TURNS) as n:
                for t in range(T):
                    eng.wait_ge(stored[t % 2], (n * (T // 2) + t // 2) * (G8 * 16))
                    for k in range(which, NC, 2):
                        eng.wait_ge(product, (n * T + t) * NC + k + 1)
                        copy(ot[t % 2][:, k * CHUNK:(k + 1) * CHUNK], pq[:, k, :]).then_inc(copied[which], 1)

        @block.scalar
        def _(act):
            copy_chunks(act, lambda o, i: nc.scalar.activation(o, i, ACT.Copy), 0)

        @block.vector
        def _(dve):
            copy_chunks(dve, nc.vector.tensor_copy, 1)


def permuted_channels():
    return np.arange(C3).reshape(C3 // PART, TG, G8).transpose(0, 2, 1).reshape(-1)


K1 = 5
BLK = 16
STEP = BLK - K1 + 1
NBLK = (HH - BLK) // STEP + 1
TW = WW + K1 - 1


def grouped_conv(nc, qkv, agg, w_dw, w_pw, row_masks):
    ctx = ExitStack()
    with ctx:
        sb = lambda n, s, dt=F32: ctx.enter_context(nc.sbuf_tensor(f"c_{n}", s, dt))
        sem = lambda n: nc.alloc_semaphore(name=f"c_{n}")
        dw = sb("dw", [PART, GROUPS, K1, K1])
        pw = sb("pw", [PART, GROUPS, G8])
        band = sb("band", [PART, GROUPS, K1, BLK])
        rm = sb("rm", [PART, BLK])
        NB_IN = 2
        xt = [sb(f"xt{u}", [PART, B, NBLK, TW]) for u in range(NB_IN)]
        wm = [sb(f"wm{u}", [PART, K1, BLK, G8]) for u in range(2)]
        ot = [sb(f"ot{u}", [PART, B, NBLK, WW]) for u in range(2)]
        pa = ctx.enter_context(nc.psum_tensor("c_pa", [PART, 2, B, 512], F32))
        consts_in = sem("consts_in")
        border_zero = sem("border_zero")
        band_step = sem("band_step")
        group_in = [sem(f"group_in{u}") for u in range(2)]
        weights_ready = sem("weights_ready")
        product = [sem(f"product{u}") for u in range(2)]
        copied = [[sem(f"copied_{k}{u}") for u in range(2)] for k in ("act", "dve")]
        stored = [sem(f"stored{u}") for u in range(2)]
        STORES = B + 2
        TURNS = GROUPS // 2
        block = ctx.enter_context(nc.Block())

        @block.gpsimd
        def _(pool):
            for y in range(BLK):
                pool.dma_start(dw[y * G8:(y + 1) * G8].rearrange("p g a b -> p (g a b)"), w_dw).then_inc(consts_in, 16)
                pool.dma_start(pw[y * G8:(y + 1) * G8].rearrange("p g o -> p (g o)"), w_pw).then_inc(consts_in, 16)
            pool.dma_start(rm[:], row_masks).then_inc(consts_in, 16)
            with pool.Fori(0, TURNS) as n:
                for u in range(2):
                    g = n * 2 + u
                    for k in range(2):
                        pool.wait_ge(copied[k][u], (n + 1) * (B // 2))
                    rows = agg[:, bass.ds(g, 1), :].rearrange("b g (r c) -> (g r) b c", c=WW)
                    for b in range(B):
                        dst = agg[b:b + 1, bass.ds(g, 1), 2 * G8 * WW:(2 + NBLK * STEP) * G8 * WW]\
                            .rearrange("b g (k r c) -> (b g r) k c", k=NBLK, c=WW)
                        pool.dma_start(dst, ot[u][2 * G8:(2 + STEP) * G8, b]).then_inc(stored[u], 16)
                    pool.dma_start(rows[0:2 * G8], ot[u][0:2 * G8, :, 0, :]).then_inc(stored[u], 16)
                    pool.dma_start(rows[(HH - 2) * G8:HH * G8], ot[u][(BLK - 2) * G8:BLK * G8, :, NBLK - 1, :])\
                        .then_inc(stored[u], 16)
            for u in range(2):
                pool.wait_ge(stored[u], TURNS * STORES * 16)

        @block.sync
        def _(sp):
            sp.wait_ge(border_zero, 2)
            with sp.Fori(0, TURNS) as n:
                for u in range(2):
                    g = n * 2 + u
                    sp.wait_ge(product[u], n * B)
                    for b in range(B):
                        one = qkv[b:b + 1, bass.ds(g, 1), :]
                        src = bass.AP(tensor=one.tensor, offset=one.offset,
                                      ap=[[WW, PART], [STEP * G8 * WW, NBLK], [1, WW]])
                        sp.dma_start(xt[u][:, b, :, K1 // 2:K1 // 2 + WW], src).then_inc(group_in[u], 16)

        @block.tensor
        def _(pe):
            with pe.Fori(0, TURNS) as n:
                for u in range(2):
                    g = n * 2 + u
                    pe.wait_ge(group_in[u], (n + 1) * (B * 16))
                    pe.wait_ge(weights_ready, g + 1)
                    for b in range(B):
                        pe.wait_ge(copied[b % 2][u], n * (B // 2))
                        for dx in range(K1):
                            last = nc.tensor.matmul(pa[:, u, b, 0:NBLK * WW].rearrange("p (k c) -> p k c", c=WW),
                                                    lhsT=wm[u][:, dx].rearrange("p y o -> p (y o)"),
                                                    rhs=xt[u][:, b, :, dx:dx + WW], start=dx == 0, stop=dx == K1 - 1)
                        last.then_inc(product[u], 1)

        def copy_out(eng, copy, which):
            with eng.Fori(0, TURNS) as n:
                for u in range(2):
                    g = n * 2 + u
                    if which == 1:
                        make_weights(eng, n, u)
                    eng.wait_ge(stored[u], n * (STORES * 16))
                    for b in range(which, B, 2):
                        eng.wait_ge(product[u], n * B + b + 1)
                        copy(ot[u][:, b].rearrange("p k c -> p (k c)"), pa[:, u, b, 0:NBLK * WW]).then_inc(copied[which][u], 1)

        def make_weights(dve, n, u):
            g = n * 2 + u
            dve.wait_ge(product[u], n * B)
            nc.vector.tensor_tensor(
                wm[u][:].rearrange("p d y o -> p (d y) o"),
                band[:, bass.ds(g, 1)].rearrange("p g d (y o) -> p (g d y) o", o=1).to_broadcast([PART, K1 * BLK, G8]),
                pw[:, bass.ds(g, 1), :].to_broadcast([PART, K1 * BLK, G8]), ALU.mult).then_inc(weights_ready, 1)

        @block.scalar
        def _(act):
            copy_out(act, lambda o, i: nc.scalar.activation(o, i, ACT.Copy), 0)

        @block.vector
        def _(dve):
            for u in range(2):
                nc.vector.memset(xt[u][:], 0.0).then_inc(border_zero, 1)
            dve.wait_ge(consts_in, (2 * BLK + 1) * 16)
            nc.vector.memset(band[:], 0.0).then_inc(band_step, 1)
            dve.wait_ge(band_step, 1)
            done = 1
            for dy in range(K1):
                first = done
                for y in range(BLK):
                    j = y + dy - K1 // 2
                    if 0 <= j < BLK:
                        to = band[:, :, :, y]
                        nc.vector.scalar_tensor_tensor(to, dw[:, :, dy, :], rm[:, j:j + 1], to, ALU.mult, ALU.add)\
                            .then_inc(band_step, 1)
                        done += 1
                dve.wait_ge(band_step, done)
            copy_out(dve, nc.vector.tensor_copy, 1)


def row_masks():
    return (np.arange(PART)[:, None] // G8 == np.arange(BLK)[None]).astype(np.float32)


HEADS1 = C // G8
SCALES = 2
ST = SCALES * HEADS1 // TG
EPS1 = 1e-15


def linear_attention(nc, scales, x_in, x_out, w_proj_t, head_mask, ident_in):
    ctx = ExitStack()
    with ctx:
        sb = lambda n, s, dt=F32: ctx.enter_context(nc.sbuf_tensor(f"d_{n}", s, dt))
        pb = lambda n, s: ctx.enter_context(nc.psum_tensor(f"d_{n}", s, F32))
        sem = lambda n: nc.alloc_semaphore(name=f"d_{n}")
        TPS = ST // SCALES
        NCH = NPX // PART
        PC = 512
        NPC = NPX // PC
        kt = [sb(f"kt{u}", [PART, NPX]) for u in range(2)]
        vt = [sb(f"vt{u}", [PART, NPX]) for u in range(2)]
        qt = sb("qt", [PART, ST, NPX])
        kvp = [sb(f"kvp{u}", [PART, 2, 2 * PART + 1]) for u in range(2)]
        kvm = sb("kvm", [PART, ST, PART])
        ksm = sb("ksm", [PART, ST, PART])
        wp = sb("wp", [PART, ST, C])
        hm = sb("hm", [PART, PART])
        ident = sb("ident", [PART, PART])
        den = [sb(f"den{u}", [PART, PC]) for u in range(2)]
        att = [sb(f"att{i}", [PART, PC]) for i in range(3)]
        xr = [sb(f"xr{u}", [PART, HALVES, PC]) for u in range(2)]
        work = pb("work", [PART, 2, 2, 512])
        pkv = pb("pkv", [PART, 512])
        pp = pb("pp", [PART, 2, 512])
        wait_taker = sb("wait_taker", [PART, 2])
        taken = sem("taken")
        consts_in = sem("consts_in")
        ones_ready = sem("ones_ready")
        kv_in = [sem(f"kv_in{u}") for u in range(2)]
        q_in = [sem(f"q_in{st}") for st in range(ST)]
        q_positive = sem("q_positive")
        turned = sem("turned")
        keys_copied = sem("keys_copied")
        values_copied = sem("values_copied")
        summed = sem("summed")
        kv_masked = sem("kv_masked")
        ks_masked = sem("ks_masked")
        ratio_parts = sem("ratio_parts")
        den_guarded = sem("den_guarded")
        den_inverted = sem("den_inverted")
        attended = sem("attended")
        projected = sem("projected")
        added = sem("added")
        x_loaded = [sem(f"x_loaded{u}") for u in range(2)]
        stored = [sem(f"stored{u}") for u in range(2)]
        block = ctx.enter_context(nc.Block())
        PAIRS = NCH // 2

        def heads_of(b, st, kind):
            s, t = divmod(st, TPS)
            first = 3 * TG * t
            return scales[s][bass.ds(b, 1), first:first + 3 * TG, :]\
                .rearrange("b (h k) (r i c) -> k i (b h) r c", k=3, i=G8, c=WW)[kind]

        @block.sync
        def _(sp):
            sp.dma_start(wp[:], w_proj_t.rearrange("(s p) o -> p s o", p=PART)).then_inc(consts_in, 16)
            sp.dma_start(hm[:], head_mask).then_inc(consts_in, 16)
            sp.dma_start(ident[:], ident_in).then_inc(consts_in, 16)
            with sp.Fori(0, B) as b:
                for st in range(ST):
                    u = st % 2
                    sp.wait_ge(turned, (b * ST + max(st - 1, 0)) * PAIRS)
                    for i in range(G8):
                        for kind, buf in ((1, kt), (2, vt)):
                            sp.dma_start(buf[u][i * TG:(i + 1) * TG].rearrange("p (r c) -> p r c", c=WW),
                                         heads_of(b, st, kind)[i]).then_inc(kv_in[u], 16)

        @block.gpsimd
        def _(pool):
            nc.gpsimd.memset(wait_taker[:], 0.0).then_inc(taken, 1)
            with pool.Fori(0, B) as b:
                for c in range(NPC + 1):
                    if c < NPC:
                        pool.wait_ge(stored[c % 2], (b * (NPC // 2) + c // 2) * 16)
                        pool.dma_start(xr[c % 2][:], x_in[bass.ds(b, 1), :, c * PC:(c + 1) * PC]
                                       .rearrange("b (h p) n -> p (b h) n", p=PART)).then_inc(x_loaded[c % 2], 16)
                    if c > 0:
                        pool.wait_ge(taken, b * NPC + c)
                        pool.wait_ge(added, (b * NPC + c) * HALVES)
                        nc.gpsimd.tensor_tensor(wait_taker[:, 0:1], wait_taker[:, 1:2], wait_taker[:, 1:2], ALU.add)\
                            .then_inc(taken, 1)
                        pool.dma_start(x_out[bass.ds(b, 1), :, (c - 1) * PC:c * PC]
                                       .rearrange("b (h p) n -> p (b h) n", p=PART), xr[(c - 1) % 2][:])\
                            .then_inc(stored[(c - 1) % 2], 16)
            for u in range(2):
                pool.wait_ge(stored[u], B * (NPC // 2) * 16)

        @block.tensor
        def _(pe):
            pe.wait_ge(consts_in, 48)
            pe.wait_ge(ones_ready, 2)
            with pe.Fori(0, B) as b:
                def turn(j):
                    st, k = divmod(j, PAIRS)
                    if k == 0:
                        pe.wait_ge(kv_in[st % 2], (b * (ST // 2) + st // 2 + 1) * (2 * G8 * 16))
                    pe.wait_ge(keys_copied, b * ST * PAIRS + max(j - 1, 0))
                    pe.wait_ge(values_copied, b * ST * PAIRS + max(j - 1, 0))
                    for e in range(2):
                        px = slice((2 * k + e) * PART, (2 * k + e + 1) * PART)
                        for v, buf in enumerate((kt, vt)):
                            last = nc.tensor.transpose(work[:, j % 2, v, e * PART:(e + 1) * PART], buf[st % 2][:, px], ident[:])
                    last.then_inc(turned, 1)

                def accumulate(j):
                    st, k = divmod(j, PAIRS)
                    pe.wait_ge(keys_copied, b * ST * PAIRS + j + 1)
                    pe.wait_ge(values_copied, b * ST * PAIRS + j + 1)
                    if k == 0:
                        pe.wait_ge(kv_masked, b * ST + st)
                        pe.wait_ge(ks_masked, b * ST + st)
                    for e in range(2):
                        last = nc.tensor.matmul(pkv[:, 0:PART + 1], lhsT=kvp[j % 2][:, e, 0:PART],
                                                rhs=kvp[j % 2][:, e, PART:2 * PART + 1],
                                                start=k == 0 and e == 0, stop=k == PAIRS - 1 and e == 1)
                    last.then_inc(summed, 1)

                for j in range(ST * PAIRS + 1):
                    if j < ST * PAIRS:
                        turn(j)
                    if j > 0:
                        accumulate(j - 1)

                def ratio(i):
                    c, st = divmod(i, ST)
                    if c == 0:
                        pe.wait_ge(q_positive, b * ST + st + 1)
                        pe.wait_ge(kv_masked, b * ST + st + 1)
                        pe.wait_ge(ks_masked, b * ST + st + 1)
                    pe.wait_ge(attended, b * NPC * ST + max(i - 1, 0))
                    px = slice(c * PC, (c + 1) * PC)
                    nc.tensor.matmul(work[:, i % 2, 1, :], lhsT=ksm[:, st], rhs=qt[:, st, px], start=True, stop=True)\
                        .then_inc(ratio_parts, 1)
                    nc.tensor.matmul(work[:, i % 2, 0, :], lhsT=kvm[:, st], rhs=qt[:, st, px], start=True, stop=True)\
                        .then_inc(ratio_parts, 1)

                def project(i):
                    c, st = divmod(i, ST)
                    pe.wait_ge(attended, b * NPC * ST + i + 1)
                    if st == 0:
                        pe.wait_ge(added, (b * NPC + c) * HALVES)
                    for m in range(HALVES):
                        last = nc.tensor.matmul(pp[:, m, :], lhsT=wp[:, st, m * PART:(m + 1) * PART],
                                                rhs=att[i % 3][:], start=st == 0, stop=st == ST - 1)
                    last.then_inc(projected, 1)

                for i in range(NPC * ST + 2):
                    if i < NPC * ST:
                        ratio(i)
                    if i >= 2:
                        project(i - 2)

        @block.scalar
        def _(act):
            with act.Fori(0, B) as b:
                act.wait_ge(attended, b * (NPC * ST))
                for st in range(ST):
                    for i in range(G8):
                        act.dma_start(qt[i * TG:(i + 1) * TG, st].rearrange("p (r c) -> p r c", c=WW),
                                      heads_of(b, st, 0)[i]).then_inc(q_in[st], 16)
                for j in range(ST * PAIRS):
                    act.wait_ge(turned, b * ST * PAIRS + j + 1)
                    act.wait_ge(summed, b * ST * PAIRS + max(j - 1, 0))
                    nc.scalar.activation(kvp[j % 2][:, :, 0:PART], work[:, j % 2, 0, 0:2 * PART].rearrange("p (e k) -> p e k", e=2), ACT.Relu).then_inc(keys_copied, 1)
                for st in range(ST):
                    act.wait_ge(q_in[st], (b + 1) * (G8 * 16))
                    nc.scalar.activation(qt[:, st], qt[:, st], ACT.Relu).then_inc(q_positive, 1)
                for i in range(NPC * ST):
                    act.wait_ge(ratio_parts, (b * NPC * ST + i) * 2 + 1)
                    act.wait_ge(attended, b * NPC * ST + max(i - 1, 0))
                    nc.scalar.activation(den[i % 2][:], work[:, i % 2, 1, :], ACT.Copy, bias=EPS1).then_inc(den_guarded, 1)

        @block.vector
        def _(dve):
            for u in range(2):
                nc.vector.memset(kvp[u][:, :, 2 * PART:2 * PART + 1], 1.0).then_inc(ones_ready, 1)
            dve.wait_ge(consts_in, 48)
            with dve.Fori(0, B) as b:
                for j in range(ST * PAIRS):
                    dve.wait_ge(turned, b * ST * PAIRS + j + 1)
                    dve.wait_ge(summed, b * ST * PAIRS + max(j - 1, 0))
                    nc.vector.tensor_copy(kvp[j % 2][:, :, PART:2 * PART], work[:, j % 2, 1, 0:2 * PART].rearrange("p (e k) -> p e k", e=2))\
                        .then_inc(values_copied, 1)
                    st, k = divmod(j, PAIRS)
                    if k == PAIRS - 1:
                        dve.wait_ge(summed, b * ST * PAIRS + j + 1)
                        nc.vector.tensor_tensor(kvm[:, st], pkv[:, 0:PART], hm[:], ALU.mult).then_inc(kv_masked, 1)
                        nc.vector.tensor_scalar(ksm[:, st], hm[:], pkv[:, PART:PART + 1], None, ALU.mult).then_inc(ks_masked, 1)

                def add(c):
                    dve.wait_ge(projected, (b * NPC + c + 1) * ST)
                    dve.wait_ge(x_loaded[c % 2], (b * (NPC // 2) + c // 2 + 1) * 16)
                    for m in range(HALVES):
                        nc.vector.tensor_tensor(xr[c % 2][:, m, :], pp[:, m, :], xr[c % 2][:, m, :], ALU.add).then_inc(added, 1)

                for i in range(NPC * ST):
                    dve.wait_ge(den_guarded, b * NPC * ST + i + 1)
                    nc.vector.reciprocal(den[i % 2][:], den[i % 2][:]).then_inc(den_inverted, 1)
                    if i >= 3 and (i - 3) % ST == ST - 1:
                        add((i - 3) // ST)
                    dve.wait_ge(den_inverted, b * NPC * ST + i + 1)
                    dve.wait_ge(ratio_parts, (b * NPC * ST + i) * 2 + 2)
                    dve.wait_ge(projected, b * NPC * ST + max(i - 2, 0))
                    nc.vector.tensor_tensor(att[i % 3][:], work[:, i % 2, 0, :], den[i % 2][:], ALU.mult).then_inc(attended, 1)
                add(NPC - 1)


def head_mask():
    h = np.arange(PART) % TG
    return (h[:, None] == h[None]).astype(np.float32)


def head_channels():
    return np.arange(ST * PART).reshape(ST, TG, G8).transpose(0, 2, 1).reshape(-1)


K2 = 7
R2 = 16
BPX = R2 * WW
HR = R2 + K2 - 1
HPX = HR * PW
NCK = BPX // PART
INNER = 4
GROUPS2 = [(o, i, min(INNER, K2 - i)) for o in range(K2) for i in range(0, K2, INNER)]
NG2 = len(GROUPS2)


def channel_attention(nc, xn, x_in, x_out, w_t, rel, ident_in):
    ctx = ExitStack()
    with ctx:
        sb = lambda n, s, dt=F32: ctx.enter_context(nc.sbuf_tensor(f"e_{n}", s, dt))
        pb = lambda n, s: ctx.enter_context(nc.psum_tensor(f"e_{n}", s, F32))
        sem = lambda n: nc.alloc_semaphore(name=f"e_{n}")
        NSE, NEV = 4, 2
        wt = sb("wt", [PART, 3, HALVES, C])
        rl = sb("rl", [PART, HALVES, K2])
        ident = sb("ident", [PART, PART])
        xb = sb("xb", [PART, HALVES, HPX])
        q = [sb(f"q{u}", [PART, BPX]) for u in range(2)]
        k = [sb(f"k{u}", [PART, HPX]) for u in range(2)]
        v = [sb(f"v{u}", [PART, HPX]) for u in range(2)]
        kr = [sb(f"kr{u}", [PART, HPX]) for u in range(2)]
        m2 = sb("m2", [PART, HPX])
        m4 = sb("m4", [PART, HPX])
        ext = [sb(f"ext{i}", [PART, BPX]) for i in range(2)]
        top = [sb(f"top{u}", [PART, BPX]) for u in range(2)]
        se = [sb(f"se{i}", [PART, INNER, BPX]) for i in range(NSE)]
        ev = [sb(f"ev{i}", [PART, INNER, BPX]) for i in range(NEV)]
        rs = sb("rs", [PART, BPX])
        xr = [sb(f"xr{u}", [PART, BPX]) for u in range(2)]
        pj = pb("pj", [PART, 2, 512])
        pe_sum = pb("pe_sum", [PART, NCK, PART])
        pv_sum = pb("pv_sum", [PART, NCK, PART])
        pback = pb("pback", [PART, 2, 512])
        consts_in = sem("consts_in")
        band_in = sem("band_in")
        rest_in = [sem(f"rest_in{u}") for u in range(2)]
        stored = [sem(f"stored{u}") for u in range(2)]
        projected = sem("projected")
        proj_copied = sem("proj_copied")
        rel_added = sem("rel_added")
        ext_step = sem("ext_step")
        step_done = sem("step_done")
        top_parts = sem("top_parts")
        top_ready = sem("top_ready")
        multiplied = sem("multiplied")
        shifted = sem("shifted")
        exp_done = sem("exp_done")
        weighted = sem("weighted")
        e_summed = sem("e_summed")
        v_summed = sem("v_summed")
        inverted = sem("inverted")
        divided = sem("divided")
        turned_back = sem("turned_back")
        added = sem("added")
        RB = HH // R2
        NJ = HALVES * NG2
        KCH2 = HPX // 4
        PROJ = [(0, i * 512, 512) for i in range(BPX // 512)] + [(w, i * KCH2, KCH2) for w in (1, 2) for i in range(4)]
        NPJ = len(PROJ)
        block = ctx.enter_context(nc.Block())

        def window(t, h, o, i, n):
            dy, dx = (o, i) if h == 0 else (i, o)
            step = 1 if h == 0 else PW
            a = t[:, dy * PW + dx:dy * PW + dx + 1]
            return bass.AP(tensor=a.tensor, offset=a.offset, ap=[a.ap[0], [step, n], [PW, R2], [1, WW]])

        def flat(t, n):
            return t[:, 0:n].rearrange("p i (r c) -> p i r c", c=WW)

        def repeat(t, n):
            return t[:].rearrange("p (i r c) -> p i r c", i=1, c=WW).to_broadcast([PART, n, R2, WW])

        @contextmanager
        def loop(eng):
            with eng.Fori(0, B) as b, eng.Fori(0, RB) as r:
                yield b, r, b * RB + r

        @block.sync
        def _(sp):
            for w in range(3):
                sp.dma_start(wt[:, w], w_t[w].rearrange("(h p) o -> p h o", p=PART)).then_inc(consts_in, 16)
            sp.dma_start(rl[:], rel.rearrange("(h p) k -> p h k", p=PART)).then_inc(consts_in, 16)
            sp.dma_start(ident[:], ident_in).then_inc(consts_in, 16)
            with loop(sp) as (b, r, n):
                sp.wait_ge(projected, n * (HALVES * NPJ))
                sp.dma_start(xb[:], xn[bass.ds(b, 1), :, bass.ds(r * (R2 * PW), HPX)]
                             .rearrange("b (h p) n -> p (b h) n", p=PART)).then_inc(band_in, 16)
                for h in range(HALVES):
                    sp.wait_ge(stored[h], n * 16)
                    sp.dma_start(xr[h][:], x_in[bass.ds(b, 1), h * PART:(h + 1) * PART, bass.ds(r * BPX, BPX)]
                                 .rearrange("b p n -> (b p) n")).then_inc(rest_in[h], 16)
                for h in range(HALVES):
                    sp.wait_ge(added, (n * HALVES + h + 1) * 2)
                    sp.dma_start(x_out[bass.ds(b, 1), h * PART:(h + 1) * PART, bass.ds(r * BPX, BPX)]
                                 .rearrange("b p n -> (b p) n"), xr[h][:]).then_inc(stored[h], 16)
            for h in range(HALVES):
                sp.wait_ge(stored[h], B * RB * 16)

        @block.tensor
        def _(pe):
            pe.wait_ge(consts_in, 80)
            with loop(pe) as (b, r, n):
                def project(h):
                    if h == 0:
                        pe.wait_ge(band_in, n * 16 + 16)
                    for c, (w, first, size) in enumerate(PROJ):
                        pe.wait_ge(proj_copied, (n * HALVES + h) * NPJ + (max(c - 1, 0)))
                        for g in range(HALVES):
                            if w == 0:
                                rows = xb[:, g].rearrange("p (r c) -> p r c", c=PW)
                                first_row = PAD + first // WW
                                rhs = rows[:, first_row:first_row + size // WW, PAD:PAD + WW]
                                out = pj[:, c % 2, 0:size].rearrange("p (r c) -> p r c", c=WW)
                            else:
                                rhs, out = xb[:, g, first:first + size], pj[:, c % 2, 0:size]
                            last = nc.tensor.matmul(out, lhsT=wt[:, w, g, h * PART:(h + 1) * PART], rhs=rhs,
                                                    start=g == 0, stop=g == HALVES - 1)
                        last.then_inc(projected, 1)

                def add_up(J, src, acc, done):
                    h, g = divmod(J, NG2)
                    for e in range(GROUPS2[g][2]):
                        for c in range(NCK):
                            last = nc.tensor.matmul(acc[:, c, :], lhsT=src[:, e, c * PART:(c + 1) * PART], rhs=ident[:],
                                                    is_transpose=True, start=g == 0 and e == 0 and c % 4 == 0,
                                                    stop=g == NG2 - 1 and e == GROUPS2[g][2] - 1, skip_group_check=True)
                    last.then_inc(done, 1)

                def back(h):
                    pe.wait_ge(divided, n * HALVES + h + 1)
                    pe.wait_ge(added, (n * HALVES + h) * 2)
                    for c in range(NCK):
                        last = nc.tensor.transpose(pback[:, c // 4, (c % 4) * PART:(c % 4 + 1) * PART],
                                                   rs[:, c * PART:(c + 1) * PART], ident[:])
                    last.then_inc(turned_back, 1)

                project(0)
                def sum_weighted(J):
                    pe.wait_ge(weighted, n * NJ + J + 1)
                    add_up(J, ev[J % NEV], pv_sum, v_summed)

                for J in range(NJ + 1):
                    if J == NG2:
                        sum_weighted(J - 1)
                    if J < NJ:
                        h, g = divmod(J, NG2)
                        pe.wait_ge(exp_done, n * NJ + J + 1)
                        if g == 0:
                            pe.wait_ge(divided, n * HALVES + h)
                        add_up(J, se[J % NSE], pe_sum, e_summed)
                    if J > 0 and J != NG2:
                        sum_weighted(J - 1)
                    if J == 2:
                        project(1)
                    if J == NG2 + 3:
                        back(0)
                back(1)

        @block.scalar
        def _(act):
            act.wait_ge(consts_in, 80)
            with loop(act) as (b, r, n):
                def copy_projection(h):
                    act.wait_ge(weighted, n * NJ + (0 if h == 0 else 0))
                    for c, (w, first, size) in enumerate(PROJ):
                        act.wait_ge(projected, (n * HALVES + h) * NPJ + c + 1)
                        nc.scalar.activation((q, k, v)[w][h][:, first:first + size], pj[:, c % 2, 0:size], ACT.Copy)\
                            .then_inc(proj_copied, 1)

                def add_rel(h, o):
                    N = (n * HALVES + h) * K2 + o
                    act.wait_ge(multiplied, n * NJ + h * NG2 + 2 * max(o - 1, 0))
                    act.wait_ge(proj_copied, (n * HALVES + h + 1) * NPJ)
                    nc.scalar.activation(kr[o % 2][:], k[h][:], ACT.Identity, bias=rl[:, h, o:o + 1]).then_inc(rel_added, 1)

                copy_projection(0)
                for J in range(NJ):
                    h, g = divmod(J, NG2)
                    o, i, taps = GROUPS2[g]
                    if J == 0 or J == NG2 - 1:
                        for o in range(2):
                            add_rel(0 if J == 0 else 1, o)
                        o = GROUPS2[g][0]
                    act.wait_ge(shifted, n * NJ + J + 1)
                    nc.scalar.activation(se[J % NSE][:, 0:taps], se[J % NSE][:, 0:taps], ACT.Exp).then_inc(exp_done, 1)
                    if i > 0 and o + 2 < K2:
                        add_rel(h, o + 2)
                    if J == 3:
                        copy_projection(1)

        @block.gpsimd
        def _(pool):
            with loop(pool) as (b, r, n):
                def top_products(h):
                    for i in range(2):
                        pool.wait_ge(top_parts, (n * HALVES + h) * 2 + i + 1)
                        nc.gpsimd.tensor_tensor(ext[i][:], ext[i][:], q[h][:], ALU.mult).then_inc(step_done, 1)

                top_products(0)
                for J in range(NJ):
                    h, g = divmod(J, NG2)
                    if J == NG2 - 1:
                        top_products(1)
                    o, i, taps = GROUPS2[g]
                    pool.wait_ge(exp_done, n * NJ + J + 1)
                    pool.wait_ge(v_summed, n * NJ + max(J - 1, 0))
                    nc.gpsimd.tensor_tensor(flat(ev[J % NEV], taps), flat(se[J % NSE], taps),
                                            window(v[h], h, o, i, taps), ALU.mult).then_inc(weighted, 1)

        @block.vector
        def _(dve):
            dve.wait_ge(consts_in, 80)
            EXT = 3 + K2 - 1
            STEPS = HALVES * 2 * EXT
            with loop(dve) as (b, r, n):
                chain = [0]

                def extremes(h):
                    dve.wait_ge(proj_copied, (n * HALVES + h + 1) * NPJ)
                    step = 1 if h == 0 else PW
                    for i, op in enumerate((ALU.max, ALU.min)):
                        src = k[h]
                        size = HPX
                        for dst, by in ((m2, 1), (m4, 2), (m2, 3)):
                            size -= by * step
                            nc.vector.tensor_tensor(dst[:, 0:size], src[:, 0:size], src[:, by * step:by * step + size], op)\
                                .then_inc(ext_step, 1)
                            chain[0] += 1
                            dve.wait_ge(ext_step, n * STEPS + chain[0])
                            src = dst
                        for o in range(K2):
                            at = o * PW if h == 0 else o
                            a = m2[:, at:at + 1]
                            win = bass.AP(tensor=a.tensor, offset=a.offset, ap=[a.ap[0], [PW, R2], [1, WW]])
                            to = ext[i][:].rearrange("p (r c) -> p r c", c=WW)
                            if o == 0:
                                dve.wait_ge(top_ready, n * HALVES + h)
                                nc.vector.tensor_scalar(to, win, rl[:, h, 0:1], None, ALU.add).then_inc(ext_step, 1)
                            else:
                                ins = nc.vector.scalar_tensor_tensor(to, win, rl[:, h, o:o + 1], to, ALU.add, op)
                                if o == K2 - 1:
                                    ins.then_inc(top_parts, 1)
                                    break
                                ins.then_inc(ext_step, 1)
                            chain[0] += 1
                            dve.wait_ge(ext_step, n * STEPS + chain[0])
                        if i == 0:
                            dve.wait_ge(top_parts, (n * HALVES + h) * 2 + 1)

                def largest(h):
                    dve.wait_ge(step_done, (n * HALVES + h + 1) * 2)
                    nc.vector.tensor_tensor(top[h][:], ext[0][:], ext[1][:], ALU.max).then_inc(top_ready, 1)

                def multiply(J):
                    h, g = divmod(J, NG2)
                    o, i, taps = GROUPS2[g]
                    dve.wait_ge(rel_added, (n * HALVES + h) * K2 + o + 1)
                    dve.wait_ge(e_summed, n * NJ + max(J - 3, 0))
                    dve.wait_ge(weighted, n * NJ + max(J - 3, 0))
                    a = kr[o % 2][:, 0:1]
                    nc.vector.tensor_tensor(flat(se[J % NSE], taps), window(kr[o % 2], h, o, i, taps),
                                            repeat(q[h], taps), ALU.mult).then_inc(multiplied, 1)

                def shift(J):
                    h, g = divmod(J, NG2)
                    o, i, taps = GROUPS2[g]
                    dve.wait_ge(multiplied, n * NJ + J + 1)
                    if g == 0:
                        dve.wait_ge(top_ready, n * HALVES + h + 1)
                    nc.vector.tensor_tensor(flat(se[J % NSE], taps), flat(se[J % NSE], taps), repeat(top[h], taps),
                                            ALU.subtract).then_inc(shifted, 1)

                def divide(h):
                    dve.wait_ge(e_summed, n * NJ + (h + 1) * NG2)
                    dve.wait_ge(turned_back, n * HALVES + h)
                    nc.vector.reciprocal(rs[:], pe_sum[:].rearrange("p c k -> p (c k)")).then_inc(inverted, 1)
                    dve.wait_ge(v_summed, n * NJ + (h + 1) * NG2)
                    dve.wait_ge(inverted, n * HALVES + h + 1)
                    nc.vector.tensor_tensor(rs[:], rs[:], pv_sum[:].rearrange("p c k -> p (c k)"), ALU.mult).then_inc(divided, 1)

                def add(h):
                    dve.wait_ge(turned_back, n * HALVES + h + 1)
                    dve.wait_ge(rest_in[h], n * 16 + 16)
                    for c in range(2):
                        s = slice(c * 512, (c + 1) * 512)
                        nc.vector.tensor_tensor(xr[h][:, s], pback[:, c, :], xr[h][:, s], ALU.add).then_inc(added, 1)

                extremes(0)
                largest(0)
                for J in range(NJ + 1):
                    if J < NJ:
                        if J % NG2 == 0:
                            if J:
                                largest(1)
                        multiply(J)
                    if J > 0:
                        shift(J - 1)
                    if J == NG2 - 3:
                        extremes(1)
                    if J == NG2 + 1:
                        divide(0)
                    if J == NG2 + 5:
                        add(0)
                divide(1)
                add(1)
                assert chain[0] == STEPS, chain


K3 = 4
HID = 65
TEMP = 0.5
KW3 = 3
TAPS = KW3 * KW3
R3 = 8
BPX3 = R3 * WW
HR3 = R3 + KW3 - 1


def dynamic_conv(nc, xn, pooled, x_in, x_out, w1_t, w2_t, b2, w_sets, ident_in):
    ctx = ExitStack()
    with ctx:
        sb = lambda n, s, dt=F32: ctx.enter_context(nc.sbuf_tensor(f"f_{n}", s, dt))
        pb = lambda n, s: ctx.enter_context(nc.psum_tensor(f"f_{n}", s, F32))
        sem = lambda n: nc.alloc_semaphore(name=f"f_{n}")
        KH = K3 * HALVES
        w1 = sb("w1", [PART, HALVES, HID])
        w2 = sb("w2", [HID, KH, PART])
        b2t = sb("b2t", [PART, KH])
        pl = sb("pl", [PART, HALVES, B])
        hid = sb("hid", [HID, B])
        lg = sb("lg", [PART, K3, HALVES * B])
        mx = sb("mx", [PART, HALVES * B])
        sm = sb("sm", [PART, HALVES * B])
        ident = sb("ident", [PART, PART])
        ws = sb("ws", [PART, K3, HALVES, TAPS * C])
        mw = [sb(f"mw{u}", [PART, HALVES, TAPS * C]) for u in range(2)]
        wc = [sb(f"wc{u}", [PART, HALVES, TAPS, C]) for u in range(2)]
        xb = [sb(f"xb{u}", [PART, HALVES, HR3 * PW]) for u in range(2)]
        xr = [sb(f"xr{u}", [PART, HALVES, BPX3]) for u in range(2)]
        pm = pb("pm", [PART, 2, 512])
        pw = pb("pw", [PART, 2, 512])
        pc = pb("pc", [PART, 2, HALVES, 512])
        consts_in = sem("consts_in")
        sets_in = sem("sets_in")
        hidden = sem("hidden")
        hidden_ready = sem("hidden_ready")
        logits = sem("logits")
        soft = sem("soft")
        mixed_part = sem("mixed_part")
        mixed = sem("mixed")
        turned = sem("turned")
        turned_copied = sem("turned_copied")
        band_in = [sem(f"band_in{u}") for u in range(2)]
        rest_in = [sem(f"rest_in{u}") for u in range(2)]
        convolved = [sem(f"convolved{u}") for u in range(2)]
        added = [sem(f"added{u}") for u in range(2)]
        stored = [sem(f"stored{u}") for u in range(2)]
        TURNS = HH // R3 // 2
        NTURN = TAPS * HALVES * HALVES // 4
        block = ctx.enter_context(nc.Block())

        @block.sync
        def _(sp):
            slow = dict(allow_slow_non_contiguous=True)
            sp.dma_start(w1[:], w1_t.rearrange("(h p) o -> p h o", p=PART)).then_inc(consts_in, 16)
            sp.dma_start(w2[:].rearrange("p k o -> p (k o)"), w2_t).then_inc(consts_in, 16)
            sp.dma_start(b2t[:], b2.rearrange("(m p) -> p m", p=PART), **slow).then_inc(consts_in, 16)
            for b in range(B):
                sp.dma_start(pl[:, :, b], pooled[b].rearrange("(h p) -> p h", p=PART), **slow).then_inc(consts_in, 16)
            sp.dma_start(ident[:], ident_in).then_inc(consts_in, 16)
            for k in range(K3):
                sp.dma_start(ws[:, k], w_sets[k].rearrange("(h p) n -> p h n", p=PART)).then_inc(sets_in, 16)
            for b in range(B):
                with sp.Fori(0, TURNS) as r:
                    n = r + b * TURNS
                    for u in range(2):
                        sp.wait_ge(convolved[u], n * HALVES)
                        first = (PAD - KW3 // 2 + u * R3) * PW
                        sp.dma_start(xb[u][:], xn[b, :, bass.ds(r * (2 * R3 * PW) + first, HR3 * PW)]
                                     .rearrange("(h p) n -> p h n", p=PART)).then_inc(band_in[u], 16)
                        sp.wait_ge(stored[u], n * 16)
                        sp.dma_start(xr[u][:], x_in[b, :, bass.ds(r * (2 * BPX3) + u * BPX3, BPX3)]
                                     .rearrange("(h p) n -> p h n", p=PART)).then_inc(rest_in[u], 16)

        @block.gpsimd
        def _(pool):
            for b in range(B):
                with pool.Fori(0, TURNS) as r:
                    n = r + b * TURNS
                    for u in range(2):
                        pool.wait_ge(added[u], (n + 1) * HALVES)
                        pool.dma_start(x_out[b, :, bass.ds(r * (2 * BPX3) + u * BPX3, BPX3)]
                                       .rearrange("(h p) n -> p h n", p=PART), xr[u][:]).then_inc(stored[u], 16)
            for u in range(2):
                pool.wait_ge(stored[u], B * TURNS * 16)

        @block.tensor
        def _(pe):
            pe.wait_ge(consts_in, (4 + B) * 16)
            for h in range(HALVES):
                last = nc.tensor.matmul(pm[0:HID, 0, 0:B], lhsT=w1[:, h], rhs=pl[:, h], start=h == 0, stop=h == 1)
            last.then_inc(hidden, 1)
            pe.wait_ge(hidden_ready, 1)
            for m in range(KH):
                last = nc.tensor.matmul(pm[:, 1, m * B:(m + 1) * B], lhsT=w2[:, m], rhs=hid[:], start=True, stop=True)
            last.then_inc(logits, 1)
            for b in range(B):
                pe.wait_ge(mixed, (b + 1) * HALVES)
                for j in range(NTURN):
                    pe.wait_ge(turned_copied, b * NTURN + max(j - 1, 0))
                    for i in range(4):
                        t, g = divmod(j * 2 + i // 2, HALVES)
                        o = i % 2
                        last = nc.tensor.transpose(pw[:, j % 2, i * PART:(i + 1) * PART],
                                                   mw[b % 2][:, o, t * C + g * PART:t * C + (g + 1) * PART], ident[:])
                    last.then_inc(turned, 1)
                pe.wait_ge(turned_copied, (b + 1) * NTURN)
                with pe.Fori(0, TURNS) as r:
                    n = r + b * TURNS
                    for u in range(2):
                        pe.wait_ge(band_in[u], n * 16 + 16)
                        pe.wait_ge(added[u], n * HALVES)
                        rows = xb[u][:].rearrange("p h (r c) -> p h r c", c=PW)
                        for m in range(HALVES):
                            for t in range(TAPS):
                                dy, dx = divmod(t, KW3)
                                for g in range(HALVES):
                                    c0 = PAD - KW3 // 2 + dx
                                    last = nc.tensor.matmul(pc[:, u, m].rearrange("p (r c) -> p r c", c=WW),
                                                            lhsT=wc[b % 2][:, g, t, m * PART:(m + 1) * PART],
                                                            rhs=rows[:, g, dy:dy + R3, c0:c0 + WW],
                                                            start=t == 0 and g == 0, stop=t == TAPS - 1 and g == 1)
                            last.then_inc(convolved[u], 1)

        @block.scalar
        def _(act):
            act.wait_ge(hidden, 1)
            nc.scalar.activation(hid[:], pm[0:HID, 0, 0:B], ACT.Relu).then_inc(hidden_ready, 1)
            act.wait_ge(soft, KH + 2)
            nc.scalar.activation(lg[:].rearrange("p k n -> p (k n)"), lg[:].rearrange("p k n -> p (k n)"), ACT.Exp,
                                 scale=1.0 / TEMP).then_inc(soft, 1)
            for b in range(B):
                for j in range(NTURN):
                    act.wait_ge(turned, b * NTURN + j + 1)
                    if b >= 2:
                        for u in range(2):
                            act.wait_ge(convolved[u], (b - 1) * TURNS * HALVES)
                    src = pw[:, j % 2].rearrange("p (g o) -> p g o", g=2)
                    nc.scalar.activation(wc[b % 2][:, :, j, :], src, ACT.Copy).then_inc(turned_copied, 1)

        @block.vector
        def _(dve):
            dve.wait_ge(consts_in, (4 + B) * 16)
            dve.wait_ge(logits, 1)
            flat = lg[:].rearrange("p k (h b) -> p (k h) b", b=B)
            for m in range(KH):
                nc.vector.tensor_scalar(flat[:, m], pm[:, 1, m * B:(m + 1) * B], b2t[:, m:m + 1], None, ALU.add)\
                    .then_inc(soft, 1)
            dve.wait_ge(soft, KH)
            by_k = lg[:].rearrange("p k n -> p n k")
            nc.vector.tensor_reduce(mx[:], by_k, AX.X, ALU.max).then_inc(soft, 1)
            dve.wait_ge(soft, KH + 1)
            rep = lambda t: t[:].rearrange("p (o n) -> p o n", o=1).to_broadcast([PART, K3, HALVES * B])
            nc.vector.tensor_tensor(lg[:], lg[:], rep(mx), ALU.subtract).then_inc(soft, 1)
            dve.wait_ge(soft, KH + 3)
            nc.vector.tensor_reduce(sm[:], by_k, AX.X, ALU.add).then_inc(soft, 1)
            dve.wait_ge(soft, KH + 4)
            nc.vector.reciprocal(sm[:], sm[:]).then_inc(soft, 1)
            dve.wait_ge(soft, KH + 5)
            nc.vector.tensor_tensor(lg[:], lg[:], rep(sm), ALU.mult).then_inc(soft, 1)
            dve.wait_ge(soft, KH + 6)
            dve.wait_ge(sets_in, K3 * 16)

            def mix(b):
                if b >= 2:
                    dve.wait_ge(turned, (b - 1) * NTURN)
                for k in range(K3):
                    for o in range(HALVES):
                        s = lg[:, k, o * B + b:o * B + b + 1]
                        to = mw[b % 2][:, o]
                        if k == 0:
                            ins = nc.vector.tensor_scalar(to, ws[:, k, o], s, None, ALU.mult)
                        else:
                            dve.wait_ge(mixed_part, (b * (K3 - 1) + k - 1) * HALVES + o + 1)
                            ins = nc.vector.scalar_tensor_tensor(to, ws[:, k, o], s, to, ALU.mult, ALU.add)
                        ins.then_inc(mixed if k == K3 - 1 else mixed_part, 1)

            mix(0)
            mix(1)
            for b in range(B):
                with dve.Fori(0, TURNS) as r:
                    n = r + b * TURNS
                    for u in range(2):
                        dve.wait_ge(rest_in[u], n * 16 + 16)
                        for m in range(HALVES):
                            dve.wait_ge(convolved[u], n * HALVES + m + 1)
                            nc.vector.tensor_tensor(xr[u][:, m], pc[:, u, m], xr[u][:, m], ALU.add).then_inc(added[u], 1)
                if b + 2 < B:
                    mix(b + 2)


def four_layers(nc, x, out, w):
    def scratch(name, shape):
        return nc.dram_tensor(name, shape, F32, kind="Internal").ap()

    xn = [scratch(f"xn{i}", [B, C, PPX]) for i in range(4)]
    xs = [x] + [scratch(f"x{i}", [B, C, NPX]) for i in (1, 2, 3)] + [out]
    qkv = scratch("qkv", [B, GROUPS, GPX])
    agg = scratch("agg", [B, GROUPS, GPX])
    pooled = scratch("pooled", [B, C])

    norm_sems = norm_semaphores(nc)
    group_norm(nc, norm_sems, 0, xs[0], xn[0], w["group_mean"])
    window_attention(nc, xn[0], xs[0], xs[1], w["L0_w_qkv_t"], w["L0_b_qkv"], w["attention_masks"], w["identity"])
    group_norm(nc, norm_sems, 1, xs[1], xn[1], w["group_mean"])
    qkv_project(nc, xn[1], qkv, w["L1_w_qkv_t"])
    grouped_conv(nc, qkv, agg, w["L1_w_dw"], w["L1_w_pw"], w["row_masks"])
    linear_attention(nc, [qkv, agg], xs[1], xs[2], w["L1_w_proj_t"], w["head_mask"], w["identity"])
    group_norm(nc, norm_sems, 2, xs[2], xn[2], w["group_mean"])
    channel_attention(nc, xn[2], xs[2], xs[3], w["L2_w_t"], w["L2_rel"], w["identity"])
    group_norm(nc, norm_sems, 3, xs[3], xn[3], w["group_mean"], pooled=pooled)
    dynamic_conv(nc, xn[3], pooled, xs[3], xs[4], w["L3_w1_t"], w["L3_w2_t"], w["L3_b2"], w["L3_w_sets"], w["identity"])


def laid_out(i):
    a = {k: np.asarray(v) for k, v in i.items()}
    return {
        "L0_w_qkv_t": a["L0_conv_w_qkv"].T,
        "L0_b_qkv": a["L0_conv_b_qkv"],
        "L1_w_qkv_t": a["L1_conv_w_qkv"].reshape(C3, C)[permuted_channels()].T,
        "L1_w_dw": a["L1_conv_w_dw"].reshape(GROUPS, G8, K1 * K1).transpose(1, 0, 2).reshape(G8, -1),
        "L1_w_pw": a["L1_conv_w_pw"].reshape(GROUPS, G8, G8).transpose(2, 0, 1).reshape(G8, -1),
        "L1_w_proj_t": a["L1_conv_w_proj"].reshape(C, ST * PART).T[head_channels()],
        "L2_w_t": np.stack([a[f"L2_conv_w_{c}"].T for c in "qkv"]),
        "L2_rel": np.concatenate([a["L2_conv_rel_h"].reshape(C // 2, K2), a["L2_conv_rel_w"].reshape(C // 2, K2)]),
        "L3_w1_t": a["L3_conv_w1"].T,
        "L3_w2_t": a["L3_conv_w2"].T,
        "L3_b2": a["L3_conv_b2"],
        "L3_w_sets": a["L3_conv_weight"].reshape(K3, C, C, TAPS).transpose(0, 1, 3, 2).reshape(K3, C, TAPS * C),
        "group_mean": group_mean(),
        "attention_masks": attention_masks(),
        "row_masks": row_masks(),
        "head_mask": head_mask(),
        "identity": np.eye(PART, dtype=np.float32),
    }


def kernel(**inputs):
    import concourse.bacc as _bacc
    from concourse.bass_utils import run_bass_kernel_spmd as _run

    x = np.asarray(inputs["x"])
    arrays = {"x": np.ascontiguousarray(x.reshape(B, C, NPX))}
    arrays.update((k, np.ascontiguousarray(v)) for k, v in laid_out(inputs).items())
    nc = _bacc.Bacc("TRN2", target_bir_lowering=False, num_devices=1)
    aps = {k: nc.dram_tensor(f"in_{k}", v.shape, mybir.dt.from_np(v.dtype), kind="ExternalInput").ap()
           for k, v in arrays.items()}
    out = nc.dram_tensor("out_x", (B, C, NPX), F32, kind="ExternalOutput").ap()
    four_layers(nc, aps["x"], out, aps)
    r = _run(nc, [{f"in_{k}": v for k, v in arrays.items()}], core_ids=[0])
    return r.results[0]["out_x"].reshape(x.shape)
```

```python
import concourse.bass as bass
from concourse import mybir
from concourse.alu_op_type import AluOpType as ALU
from contextlib import ExitStack, contextmanager
import numpy as np

ACT = mybir.ActivationFunctionType
AX = mybir.AxisListType
F32 = mybir.dt.float32
F32R = mybir.dt.float32r

B, C, HH, WW = 4, 256, 64, 64
NPX = HH * WW
PART = 128
HALVES = C // PART
PAD = 3
PW = WW + 2 * PAD
PPX = (HH + 2 * PAD) * PW
EPS = 1e-5


NORM_PAIRS = ("x_loaded", "stats_ready", "group_ready", "var_ready", "std_ready", "coef_ready", "norm_done",
              "xn_stored", "pooled_stored")


def norm_semaphores(nc):
    sems = {n: [nc.alloc_semaphore(name=f"n_{n}{h}") for h in range(HALVES)] for n in NORM_PAIRS}
    return sems | {n: nc.alloc_semaphore(name=f"n_{n}") for n in ("gm_loaded", "border_zero", "chain")}


def group_norm(nc, sems, call, x_in, xn_out, mean_matrix, pooled=None):
    tag = f"n{call}"
    before = call * B
    (x_loaded, stats_ready, group_ready, var_ready, std_ready, coef_ready, norm_done, xn_stored,
     pooled_stored) = (sems[n] for n in NORM_PAIRS)
    gm_loaded, border_zero, chain = sems["gm_loaded"], sems["border_zero"], sems["chain"]
    ctx = ExitStack()
    with ctx:
        sb = lambda n, s, dt=F32: ctx.enter_context(nc.sbuf_tensor(f"{tag}_{n}", s, dt))
        xt = [sb(f"xt{h}", [PART, NPX]) for h in range(HALVES)]
        xnp = [sb(f"xnp{h}", [PART, PPX]) for h in range(HALVES)]
        stats = [sb(f"stats{h}", [PART, NPX // 512, 6]) for h in range(HALVES)]
        ms = [sb(f"ms{h}", [PART, 2]) for h in range(HALVES)]
        gs = [sb(f"gs{h}", [PART, 2]) for h in range(HALVES)]
        var = [sb(f"var{h}", [PART, 1]) for h in range(HALVES)]
        std = [sb(f"std{h}", [PART, 1]) for h in range(HALVES)]
        coef = [sb(f"coef{h}", [PART, 2]) for h in range(HALVES)]
        pool_t = [sb(f"pool{h}", [PART, 1]) for h in range(HALVES)]
        wait_taker = sb("wait_taker", [PART, 1])
        gm = sb("gm", [PART, PART])
        psum = ctx.enter_context(nc.psum_tensor(f"{tag}_psum", [PART, HALVES, 512], F32))
        block = ctx.enter_context(nc.Block())

        @block.sync
        def _(sp):
            sp.dma_start(gm[:], mean_matrix).then_inc(gm_loaded, 16)
            with sp.Fori(0, B) as b:
                for h in range(HALVES):
                    sp.wait_ge(norm_done[h], before + b)
                    sp.dma_start(xt[h][:], x_in[bass.ds(b, 1), h * PART:(h + 1) * PART, :]
                                 .rearrange("b p n -> (b p) n")).then_inc(x_loaded[h], 16)

        @block.gpsimd
        def _(pool):
            pool.memset(xnp[0][:], 0.0).then_inc(border_zero, 1)
            pool.memset(xnp[1][:], 0.0).then_inc(border_zero, 1)
            with pool.Fori(0, B) as b:
                for h in range(HALVES):
                    pool.wait_ge(norm_done[h], before + b + 1)
                    pool.dma_start(xn_out[bass.ds(b, 1), h * PART:(h + 1) * PART, :]
                                   .rearrange("b p n -> (b p) n"), xnp[h][:]).then_inc(xn_stored[h], 16)
                    if pooled is not None:
                        pool.wait_ge(coef_ready[h], before + b + 1)
                        pool.dma_start(pooled[bass.ds(b, 1), h * PART:(h + 1) * PART]
                                       .rearrange("b p -> p b"), pool_t[h][:]).then_inc(pooled_stored[h], 16)
            for h in range(HALVES):
                pool.wait_ge(xn_stored[h], 16 * (before + B))
                if pooled is not None:
                    pool.wait_ge(pooled_stored[h], 16 * B)

        @block.vector
        def _(dve):
            STEPS0 = 1 + 4 * HALVES
            STEPS = STEPS0 + (HALVES if pooled is not None else 0)
            with dve.Fori(0, B) as b:
                n = [0]

                def link(ins):
                    n[0] += 1
                    ins.then_inc(chain, 1)
                    dve.wait_ge(chain, before * STEPS0 + b * STEPS + n[0])

                for h in range(HALVES):
                    dve.wait_ge(x_loaded[h], (before + b + 1) * 16)
                    for k in range(NPX // 512):
                        ins = nc.vector.bn_stats(stats[h][:, k, :], xt[h][:, k * 512:(k + 1) * 512])
                    link(ins)
                nc.vector.memset(wait_taker[:], 0.0)
                for h in range(HALVES):
                    ins = nc.vector.bn_aggr(ms[h][:], stats[h][:])
                link(ins)
                for h in range(HALVES):
                    nc.vector.scalar_tensor_tensor(ms[h][:, 1:2], ms[h][:, 0:1], ms[h][:, 0:1], ms[h][:, 1:2],
                                                   ALU.mult, ALU.add).then_inc(stats_ready[h], 1)
                for h in range(HALVES):
                    dve.wait_ge(group_ready[h], before + b + 1)
                    link(nc.vector.tensor_copy(gs[h][:], psum[:, h, 0:2]))
                    link(nc.vector.scalar_tensor_tensor(var[h][:], gs[h][:, 0:1], gs[h][:, 0:1], gs[h][:, 1:2],
                                                        ALU.mult, ALU.subtract))
                    nc.vector.tensor_scalar(var[h][:], var[h][:], -1.0, EPS, ALU.mult, ALU.add)\
                        .then_inc(var_ready[h], 1)
                for h in range(HALVES):
                    dve.wait_ge(std_ready[h], before + b + 1)
                    link(nc.vector.reciprocal(coef[h][:, 0:1], std[h][:]))
                    if pooled is not None:
                        dve.wait_ge(pooled_stored[h], b * 16)
                        link(nc.vector.tensor_scalar(pool_t[h][:], ms[h][:, 0:1], gs[h][:, 0:1],
                                                     coef[h][:, 0:1], ALU.subtract, ALU.mult))
                    nc.vector.tensor_scalar(coef[h][:, 1:2], gs[h][:, 0:1], coef[h][:, 0:1], -1.0,
                                            ALU.mult, ALU.mult).then_inc(coef_ready[h], 1)

        @block.tensor
        def _(pe):
            pe.wait_ge(gm_loaded, (call + 1) * 16)
            with pe.Fori(0, B) as b:
                for h in range(HALVES):
                    pe.wait_ge(stats_ready[h], before + b + 1)
                    nc.tensor.matmul(psum[:, h, 0:2], lhsT=gm[:], rhs=ms[h][:], start=True, stop=True)\
                        .then_inc(group_ready[h], 1)

        @block.scalar
        def _(act):
            act.wait_ge(border_zero, (call + 1) * 2)
            with act.Fori(0, B) as b:
                for h in range(HALVES):
                    act.wait_ge(var_ready[h], before + b + 1)
                    nc.scalar.activation(std[h][:], var[h][:], ACT.Sqrt).then_inc(std_ready[h], 1)
                for h in range(HALVES):
                    act.wait_ge(coef_ready[h], before + b + 1)
                    act.wait_ge(xn_stored[h], (before + b) * 16)
                    inner = xnp[h][:].rearrange("p (r c) -> p r c", c=PW)[:, PAD:PAD + HH, PAD:PAD + WW]
                    nc.scalar.activation(inner, xt[h][:].rearrange("p (r c) -> p r c", c=WW), ACT.Identity,
                                         bias=coef[h][:, 1:2], scale=coef[h][:, 0:1]).then_inc(norm_done[h], 1)


def group_mean():
    g = np.arange(PART) // (C // 32)
    return (g[:, None] == g[None, :]).astype(np.float32) / np.float32(C // 32)


HEADS0, HD0, K0 = 8, 32, 5
TR, TC = 8, 16
TQ = TR * TC
KR, KC = TR + K0 - 1, TC + K0 - 1
NK = KR * KC
KCH = NK // 2
TILES = WW // TC
BROWS = TR + K0 - 1
BAND0 = TR * WW


def attention_masks():
    qr, qc = np.divmod(np.arange(TQ), TC)
    kr, kc = np.divmod(np.arange(NK), KC)
    near = (np.abs(kr[None] - qr[:, None] - K0 // 2) <= K0 // 2) & (np.abs(kc[None] - qc[:, None] - K0 // 2) <= K0 // 2)
    out = np.zeros((HH // TR, TQ, TILES, NK), np.float32)
    for r in range(HH // TR):
        for c in range(TILES):
            y, x = r * TR + kr - K0 // 2, c * TC + kc - K0 // 2
            inside = (y >= 0) & (y < HH) & (x >= 0) & (x < WW)
            out[r, :, c] = np.where(near & inside[None], 0.0, -1e30)
    return out


def window_attention(nc, xn, x_in, x_out, w_qkv_t, b_qkv, masks, ident_in):
    ctx = ExitStack()
    with ctx:
        sb = lambda n, s, dt=F32: ctx.enter_context(nc.sbuf_tensor(f"a_{n}", s, dt))
        pb = lambda n, s: ctx.enter_context(nc.psum_tensor(f"a_{n}", s, F32))
        sem = lambda n: nc.alloc_semaphore(name=f"a_{n}")
        wt = sb("wt", [PART, HALVES, 3 * C])
        bias = sb("bias", [PART, 3 * HALVES])
        wait_taker = sb("wait_taker", [PART, 2])
        ident = sb("ident", [PART, PART])
        xb = [sb(f"xb{u}", [PART, HALVES, BROWS * PW]) for u in range(2)]
        xr = [sb(f"xr{u}", [PART, HALVES, BAND0]) for u in range(2)]
        mk = [sb(f"mk{u}", [TQ, TILES, NK]) for u in range(2)]
        xk = [sb(f"xk{u}", [PART, HALVES, NK]) for u in range(2)]
        qk = [sb(f"qk{u}", [PART, HALVES, TQ + NK]) for u in range(2)]
        vt = [sb(f"vt{u}", [KCH, 2, C]) for u in range(2)]
        ms = [sb(f"ms{i}", [TQ, 2, NK]) for i in range(3)]
        pr = [sb(f"pr{i}", [TQ, 2, NK]) for i in range(3)]
        nmax = [sb(f"nmax{i}", [TQ, 2]) for i in range(3)]
        den = [sb(f"den{u}", [TQ, HEADS0]) for u in range(2)]
        rden = sb("rden", [TQ, HEADS0])
        pt = [sb(f"pt{i}", [KCH, 4, TQ]) for i in range(2)]
        on = [sb(f"on{u}", [TQ, C]) for u in range(2)]
        pqk = pb("pqk", [PART, 2, 512])
        pv = pb("pv", [PART, 512])
        ps = pb("ps", [PART, 2, 512])
        ppt = pb("ppt", [PART, 512])
        po = pb("po", [PART, 512])
        pot = pb("pot", [PART, 512])
        consts_in = sem("consts_in")
        band_in = [sem(f"band_in{u}") for u in range(2)]
        rest_in = [sem(f"rest_in{u}") for u in range(2)]
        out_stored = [sem(f"out_stored{u}") for u in range(2)]
        taker_ready = sem("taker_ready")
        area_ready = sem("area_ready")
        projected = sem("projected")
        qk_copied = sem("qk_copied")
        v_copied = sem("v_copied")
        scored = sem("scored")
        masked = [sem(f"masked{u}") for u in range(2)]
        max_ready = sem("max_ready")
        exp_done = sem("exp_done")
        turned = sem("turned")
        turned_copied = sem("turned_copied")
        weighted = sem("weighted")
        recip_ready = sem("recip_ready")
        normalised = sem("normalised")
        turned_back = sem("turned_back")
        added = sem("added")

        NT = 2 * TILES
        NP = HEADS0 // 2
        BP = TILES * NP
        TURNS = HH // TR // 2
        LAG = 2
        block = ctx.enter_context(nc.Block())

        @contextmanager
        def turn(eng):
            with eng.Fori(0, B) as b, eng.Fori(0, TURNS) as r:
                yield b, r, b * TURNS + r

        @block.sync
        def _(sp):
            sp.dma_start(wt[:], w_qkv_t.rearrange("(h p) o -> p h o", p=PART)).then_inc(consts_in, 16)
            sp.dma_start(bias[:], b_qkv.rearrange("(m p) -> p m", p=PART), allow_slow_non_contiguous=True).then_inc(consts_in, 16)
            sp.dma_start(ident[:], ident_in).then_inc(consts_in, 16)
            with turn(sp) as (b, rr, n):
                for u in range(2):
                    sp.wait_ge(area_ready, n * NT)
                    first = (PAD - K0 // 2 + u * TR) * PW
                    sp.dma_start(xb[u][:], xn[bass.ds(b, 1), :, bass.ds(rr * (2 * TR * PW) + first, BROWS * PW)]
                                 .rearrange("b (h p) n -> p (b h) n", p=PART)).then_inc(band_in[u], 16)
                    sp.wait_ge(masked[u], n * BP)
                    sp.dma_start(mk[u][:], masks[bass.ds(rr * 2 + u, 1)]
                                 .rearrange("r q c k -> (r q) c k")).then_inc(rest_in[u], 16)
                    sp.wait_ge(out_stored[u], n * 16)
                    sp.dma_start(xr[u][:], x_in[bass.ds(b, 1), :, bass.ds(rr * (2 * BAND0) + u * BAND0, BAND0)]
                                 .rearrange("b (h p) n -> p (b h) n", p=PART)).then_inc(rest_in[u], 16)

        @block.gpsimd
        def _(pool):
            nc.gpsimd.memset(wait_taker[:], 0.0).then_inc(taker_ready, 1)
            pool.wait_ge(taker_ready, 1)
            with turn(pool) as (b, rr, n):
                for t in range(NT):
                    u, c = divmod(t, TILES)
                    if c == 0:
                        pool.wait_ge(band_in[u], n * 16 + 16)
                    pool.wait_ge(projected, n * NT + max(t - 1, 0))
                    pool.wait_ge(area_ready, n * NT + t)
                    nc.gpsimd.tensor_tensor(wait_taker[:, 0:1], wait_taker[:, 1:2], wait_taker[:, 1:2], ALU.add)
                    k0 = PAD - K0 // 2 + c * TC
                    for h in range(HALVES):
                        last = nc.gpsimd.tensor_copy(xk[t % 2][:, h, :].rearrange("p (r c) -> p r c", c=KC),
                                                     xb[u][:, h, :].rearrange("p (r c) -> p r c", c=PW)[:, :, k0:k0 + KC])
                    last.then_inc(area_ready, 1)
                for u in range(2):
                    pool.wait_ge(added, n * NT + (u + 1) * TILES)
                    pool.dma_start(x_out[bass.ds(b, 1), :, bass.ds(rr * (2 * BAND0) + u * BAND0, BAND0)]
                                   .rearrange("b (h p) n -> p (b h) n", p=PART), xr[u][:]).then_inc(out_stored[u], 16)
            for u in range(2):
                pool.wait_ge(out_stored[u], 16 * B * TURNS)

        @block.tensor
        def _(pe):
            pe.wait_ge(consts_in, 48)
            with turn(pe) as (b, rr, n):
                def project(t):
                    u, c = divmod(t, TILES)
                    pe.wait_ge(area_ready, n * NT + t + 1)
                    pe.wait_ge(qk_copied, n * NT + t)
                    pe.wait_ge(v_copied, n * NT + t)
                    area = xk[t % 2]
                    grid = area[:].rearrange("p h (r c) -> p h r c", c=KC)
                    own = grid[:, :, K0 // 2:K0 // 2 + TR, K0 // 2:K0 // 2 + TC]
                    for m in range(HALVES):
                        for h in range(HALVES):
                            nc.tensor.matmul(pqk[:, m, 0:TQ].rearrange("p (r c) -> p r c", c=TC),
                                             lhsT=wt[:, h, m * PART:(m + 1) * PART], rhs=own[:, h],
                                             start=h == 0, stop=h == HALVES - 1)
                        for h in range(HALVES):
                            nc.tensor.matmul(pqk[:, m, TQ:TQ + NK], lhsT=wt[:, h, C + m * PART:C + (m + 1) * PART],
                                             rhs=area[:, h, :], start=h == 0, stop=h == HALVES - 1)
                    for j in range(2):
                        for h in range(HALVES):
                            last = nc.tensor.matmul(pv[0:KCH, j * C:(j + 1) * C],
                                                    lhsT=area[:, h, j * KCH:(j + 1) * KCH],
                                                    rhs=wt[:, h, 2 * C:3 * C], start=h == 0, stop=h == HALVES - 1)
                    last.then_inc(projected, 1)

                def scores(P):
                    t, p = divmod(P, NP)
                    if p == 0:
                        pe.wait_ge(qk_copied, n * NT + t + 1)
                    if P >= 2:
                        pe.wait_ge(masked[(P - 2) // BP], n * BP + (P - 2) % BP + 1)
                    else:
                        pe.wait_ge(masked[1], n * BP)
                    for e in range(2):
                        s = slice(p * HD0, (p + 1) * HD0)
                        last = nc.tensor.matmul(ps[0:TQ, P % 2, e * NK:(e + 1) * NK], lhsT=qk[t % 2][s, e, 0:TQ],
                                                rhs=qk[t % 2][s, e, TQ:TQ + NK], start=True, stop=True)
                    last.then_inc(scored, 1)

                def turned_exps(P):
                    pe.wait_ge(exp_done, n * NT * NP + P + 1)
                    pe.wait_ge(turned_copied, n * NT * NP + P)
                    for e in range(2):
                        for j in range(2):
                            k = 2 * e + j
                            last = nc.tensor.transpose(ppt[0:KCH, k * TQ:(k + 1) * TQ],
                                                       pr[P % 3][:, e, j * KCH:(j + 1) * KCH], ident[:])
                    last.then_inc(turned, 1)

                def weigh(P):
                    t, p = divmod(P, NP)
                    pe.wait_ge(turned_copied, n * NT * NP + P + 1)
                    if p == 0:
                        pe.wait_ge(v_copied, n * NT + t + 1)
                        pe.wait_ge(normalised, n * NT + t)
                    for e in range(2):
                        s = slice((e * NP + p) * HD0, (e * NP + p + 1) * HD0)
                        for j in range(2):
                            last = nc.tensor.matmul(po[0:TQ, s], lhsT=pt[P % 2][:, 2 * e + j, :],
                                                    rhs=vt[t % 2][:, j, s], start=j == 0, stop=j == 1)
                    last.then_inc(weighted, 1)

                def back(t):
                    pe.wait_ge(normalised, n * NT + t + 1)
                    pe.wait_ge(added, n * NT + t)
                    for m in range(HALVES):
                        last = nc.tensor.transpose(pot[:, m * TQ:(m + 1) * TQ],
                                                   on[t % 2][:, m * PART:(m + 1) * PART], ident[:])
                    last.then_inc(turned_back, 1)

                project(0)
                for P in range(NT * NP + LAG + 3):
                    if P < NT * NP:
                        scores(P)
                        if P % NP == 1 and P // NP + 1 < NT:
                            project(P // NP + 1)
                    if 0 <= P - LAG < NT * NP:
                        turned_exps(P - LAG)
                    if 0 <= P - LAG - 1 < NT * NP:
                        weigh(P - LAG - 1)
                    if P - LAG - 2 >= 0 and (P - LAG - 2) % NP == NP - 1:
                        back((P - LAG - 2) // NP)

        @block.scalar
        def _(act):
            act.wait_ge(consts_in, 48)
            with turn(act) as (b, rr, n):
                def copy_qkv(t):
                    act.wait_ge(projected, n * NT + t + 1)
                    act.wait_ge(weighted, (n * NT + max(t - 1, 0)) * NP)
                    for m in range(HALVES):
                        nc.scalar.activation(qk[t % 2][:, m, 0:TQ], pqk[:, m, 0:TQ], ACT.Identity,
                                             bias=bias[:, m:m + 1])
                        last = nc.scalar.activation(qk[t % 2][:, m, TQ:TQ + NK], pqk[:, m, TQ:TQ + NK], ACT.Identity,
                                                    bias=bias[:, HALVES + m:HALVES + m + 1])
                    last.then_inc(qk_copied, 1)
                    nc.scalar.activation(vt[t % 2][:].rearrange("p j c -> p (j c)"), pv[0:KCH, :], ACT.Copy)\
                        .then_inc(v_copied, 1)

                copy_qkv(0)
                for P in range(NT * NP):
                    t, p = divmod(P, NP)
                    if p == 2 and t + 1 < NT:
                        copy_qkv(t + 1)
                    act.wait_ge(max_ready, n * NT * NP + P + 1)
                    act.wait_ge(turned, n * NT * NP + max(P - 2, 0))
                    if p == 0:
                        act.wait_ge(recip_ready, n * NT + max(t - 1, 0))
                    for e in range(2):
                        last = nc.scalar.activation(pr[P % 3][:, e, :], ms[P % 3][:, e, :], ACT.Exp,
                                                    bias=nmax[P % 3][:, e:e + 1],
                                                    accum_out=den[t % 2][:, e * NP + p:e * NP + p + 1])
                    last.then_inc(exp_done, 1)

        @block.vector
        def _(dve):
            dve.wait_ge(consts_in, 48)
            with turn(dve) as (b, rr, n):
                def mask(P):
                    t, p = divmod(P, NP)
                    u, c = divmod(t, TILES)
                    if c == 0 and p == 0:
                        dve.wait_ge(rest_in[u], n * 32 + 32)
                    dve.wait_ge(scored, n * NT * NP + P + 1)
                    dve.wait_ge(exp_done, n * NT * NP + max(P - 2, 0))
                    ins = nc.vector.tensor_tensor(ms[P % 3][:], ps[0:TQ, P % 2, 0:2 * NK].rearrange("p (e k) -> p e k", e=2),
                                                  mk[u][:, c:c + 1, :].to_broadcast([TQ, 2, NK]), ALU.add)
                    ins.then_inc(masked[u], 1)

                def maximum(P):
                    dve.wait_ge(masked[P // BP], n * BP + P % BP + 1)
                    nc.vector.tensor_reduce(nmax[P % 3][:], ms[P % 3][:], AX.X, ALU.max, negate=True).then_inc(max_ready, 1)

                def copy_turned(P):
                    dve.wait_ge(turned, n * NT * NP + P + 1)
                    dve.wait_ge(weighted, n * NT * NP + max(P - 1, 0))
                    nc.vector.tensor_copy(pt[P % 2][:].rearrange("p k q -> p (k q)"), ppt[0:KCH, :]).then_inc(turned_copied, 1)

                def normalise(t):
                    dve.wait_ge(exp_done, (n * NT + t + 1) * NP)
                    dve.wait_ge(normalised, n * NT + t)
                    nc.vector.reciprocal(rden[:], den[t % 2][:]).then_inc(recip_ready, 1)
                    dve.wait_ge(weighted, (n * NT + t + 1) * NP)
                    dve.wait_ge(recip_ready, n * NT + t + 1)
                    dve.wait_ge(turned_back, n * NT + max(t - 1, 0))
                    nc.vector.tensor_tensor(on[t % 2][:].rearrange("p (g d) -> p g d", d=HD0),
                                            po[0:TQ, 0:C].rearrange("p (g d) -> p g d", d=HD0),
                                            rden[:].rearrange("p (g o) -> p g o", o=1).to_broadcast([TQ, HEADS0, HD0]),
                                            ALU.mult).then_inc(normalised, 1)

                def add(t):
                    u, c = divmod(t, TILES)
                    dve.wait_ge(turned_back, n * NT + t + 1)
                    for m in range(HALVES):
                        res = xr[u][:, m, :].rearrange("p (r c) -> p r c", c=WW)[:, :, c * TC:(c + 1) * TC]
                        last = nc.vector.scalar_tensor_tensor(
                            res, pot[:, m * TQ:(m + 1) * TQ].rearrange("p (r c) -> p r c", c=TC),
                            bias[:, 2 * HALVES + m:2 * HALVES + m + 1], res, ALU.add, ALU.add)
                    last.then_inc(added, 1)

                for P in range(NT * NP + LAG + 3):
                    if P < NT * NP:
                        mask(P)
                    if 0 <= P - LAG < NT * NP:
                        copy_turned(P - LAG)
                    if P < NT * NP:
                        maximum(P)
                    if P - LAG - 1 >= 0 and (P - LAG - 1) % NP == NP - 1:
                        normalise((P - LAG - 1) // NP)
                    if P - LAG - 2 >= 0 and (P - LAG - 2) % NP == NP - 1:
                        add((P - LAG - 2) // NP)


G8 = 8
C3 = 3 * C
GROUPS = C3 // G8
GPX = HH * G8 * WW
TG = PART // G8
CHUNK = 512
CROWS = CHUNK // WW


def qkv_project(nc, xn, qkv, w_t):
    ctx = ExitStack()
    with ctx:
        sb = lambda n, s, dt=F32: ctx.enter_context(nc.sbuf_tensor(f"b_{n}", s, dt))
        sem = lambda n: nc.alloc_semaphore(name=f"b_{n}")
        MT = C3 // PART
        NC = NPX // CHUNK
        wt = sb("wt", [PART, HALVES, C3])
        xi = [sb(f"xi{u}", [PART, HALVES, PPX]) for u in range(2)]
        ot = [sb(f"ot{u}", [PART, NPX]) for u in range(2)]
        pq = ctx.enter_context(nc.psum_tensor("b_pq", [PART, 8, 512], F32))
        w_in = sem("w_in")
        image_in = [sem(f"image_in{u}") for u in range(2)]
        product = sem("product")
        copied = [sem("copied_act"), sem("copied_dve")]
        stored = [sem(f"stored{u}") for u in range(2)]
        block = ctx.enter_context(nc.Block())
        TURNS = B // 2
        T = 2 * MT

        @block.gpsimd
        def _(pool):
            with pool.Fori(0, TURNS) as n:
                for u in range(2):
                    pool.wait_ge(product, n * (T * NC))
                    pool.dma_start(xi[u][:], xn[bass.ds(n * 2 + u, 1)].rearrange("b (h p) n -> p (b h) n", p=PART))\
                        .then_inc(image_in[u], 16)

        @block.sync
        def _(sp):
            sp.dma_start(wt[:], w_t.rearrange("(h p) o -> p h o", p=PART)).then_inc(w_in, 16)
            with sp.Fori(0, TURNS) as n:
                for t in range(T):
                    u, m = divmod(t, MT)
                    for k in range(2):
                        sp.wait_ge(copied[k], (n * T + t + 1) * (NC // 2))
                    dst = qkv[bass.ds(n * 2 + u, 1), m * TG:(m + 1) * TG, :].rearrange("b g (r i c) -> i (b g) r c", i=G8, c=WW)
                    src = ot[t % 2][:].rearrange("p (r c) -> p r c", c=WW)
                    for i in range(G8):
                        sp.dma_start(dst[i], src[i * TG:(i + 1) * TG]).then_inc(stored[t % 2], 16)
            for k in range(2):
                sp.wait_ge(stored[k], TURNS * T // 2 * G8 * 16)

        @block.tensor
        def _(pe):
            pe.wait_ge(w_in, 16)
            with pe.Fori(0, TURNS) as n:
                for t in range(T):
                    u, m = divmod(t, MT)
                    if m == 0:
                        pe.wait_ge(image_in[u], n * 16 + 16)
                    rows = xi[u][:].rearrange("p h (r c) -> p h r c", c=PW)
                    for k in range(NC):
                        pe.wait_ge(copied[k % 2], (n * T + max(t - 1, 0)) * (NC // 2) + (k // 2 + 1 if t else 0))
                        for h in range(HALVES):
                            last = nc.tensor.matmul(pq[:, k, :].rearrange("p (r c) -> p r c", c=WW),
                                                    lhsT=wt[:, h, m * PART:(m + 1) * PART],
                                                    rhs=rows[:, h, PAD + k * CROWS:PAD + (k + 1) * CROWS, PAD:PAD + WW],
                                                    start=h == 0, stop=h == HALVES - 1)
                        last.then_inc(product, 1)

        def copy_chunks(eng, copy, which):
            with eng.Fori(0, TURNS) as n:
                for t in range(T):
                    eng.wait_ge(stored[t % 2], (n * (T // 2) + t // 2) * (G8 * 16))
                    for k in range(which, NC, 2):
                        eng.wait_ge(product, (n * T + t) * NC + k + 1)
                        copy(ot[t % 2][:, k * CHUNK:(k + 1) * CHUNK], pq[:, k, :]).then_inc(copied[which], 1)

        @block.scalar
        def _(act):
            copy_chunks(act, lambda o, i: nc.scalar.activation(o, i, ACT.Copy), 0)

        @block.vector
        def _(dve):
            copy_chunks(dve, nc.vector.tensor_copy, 1)


def permuted_channels():
    return np.arange(C3).reshape(C3 // PART, TG, G8).transpose(0, 2, 1).reshape(-1)


K1 = 5
BLK = 16
STEP = BLK - K1 + 1
NBLK = (HH - BLK) // STEP + 1
TW = WW + K1 - 1


def grouped_conv(nc, qkv, agg, w_dw, w_pw, row_masks):
    ctx = ExitStack()
    with ctx:
        sb = lambda n, s, dt=F32: ctx.enter_context(nc.sbuf_tensor(f"c_{n}", s, dt))
        sem = lambda n: nc.alloc_semaphore(name=f"c_{n}")
        dw = sb("dw", [PART, GROUPS, K1, K1])
        pw = sb("pw", [PART, GROUPS, G8])
        band = sb("band", [PART, GROUPS, K1, BLK])
        rm = sb("rm", [PART, BLK])
        NB_IN = 2
        xt = [sb(f"xt{u}", [PART, B, NBLK, TW]) for u in range(NB_IN)]
        wm = [sb(f"wm{u}", [PART, K1, BLK, G8]) for u in range(2)]
        ot = [sb(f"ot{u}", [PART, B, NBLK, WW]) for u in range(2)]
        pa = ctx.enter_context(nc.psum_tensor("c_pa", [PART, 2, B, 512], F32))
        consts_in = sem("consts_in")
        border_zero = sem("border_zero")
        band_step = sem("band_step")
        group_in = [sem(f"group_in{u}") for u in range(2)]
        weights_ready = sem("weights_ready")
        product = [sem(f"product{u}") for u in range(2)]
        copied = [[sem(f"copied_{k}{u}") for u in range(2)] for k in ("act", "dve")]
        stored = [sem(f"stored{u}") for u in range(2)]
        STORES = B + 2
        TURNS = GROUPS // 2
        block = ctx.enter_context(nc.Block())

        @block.gpsimd
        def _(pool):
            for y in range(BLK):
                pool.dma_start(dw[y * G8:(y + 1) * G8].rearrange("p g a b -> p (g a b)"), w_dw).then_inc(consts_in, 16)
                pool.dma_start(pw[y * G8:(y + 1) * G8].rearrange("p g o -> p (g o)"), w_pw).then_inc(consts_in, 16)
            pool.dma_start(rm[:], row_masks).then_inc(consts_in, 16)
            with pool.Fori(0, TURNS) as n:
                for u in range(2):
                    g = n * 2 + u
                    for k in range(2):
                        pool.wait_ge(copied[k][u], (n + 1) * (B // 2))
                    rows = agg[:, bass.ds(g, 1), :].rearrange("b g (r c) -> (g r) b c", c=WW)
                    for b in range(B):
                        dst = agg[b:b + 1, bass.ds(g, 1), 2 * G8 * WW:(2 + NBLK * STEP) * G8 * WW]\
                            .rearrange("b g (k r c) -> (b g r) k c", k=NBLK, c=WW)
                        pool.dma_start(dst, ot[u][2 * G8:(2 + STEP) * G8, b]).then_inc(stored[u], 16)
                    pool.dma_start(rows[0:2 * G8], ot[u][0:2 * G8, :, 0, :]).then_inc(stored[u], 16)
                    pool.dma_start(rows[(HH - 2) * G8:HH * G8], ot[u][(BLK - 2) * G8:BLK * G8, :, NBLK - 1, :])\
                        .then_inc(stored[u], 16)
            for u in range(2):
                pool.wait_ge(stored[u], TURNS * STORES * 16)

        @block.sync
        def _(sp):
            sp.wait_ge(border_zero, 2)
            with sp.Fori(0, TURNS) as n:
                for u in range(2):
                    g = n * 2 + u
                    sp.wait_ge(product[u], n * B)
                    for b in range(B):
                        one = qkv[b:b + 1, bass.ds(g, 1), :]
                        src = bass.AP(tensor=one.tensor, offset=one.offset,
                                      ap=[[WW, PART], [STEP * G8 * WW, NBLK], [1, WW]])
                        sp.dma_start(xt[u][:, b, :, K1 // 2:K1 // 2 + WW], src).then_inc(group_in[u], 16)

        @block.tensor
        def _(pe):
            with pe.Fori(0, TURNS) as n:
                for u in range(2):
                    g = n * 2 + u
                    pe.wait_ge(group_in[u], (n + 1) * (B * 16))
                    pe.wait_ge(weights_ready, g + 1)
                    for b in range(B):
                        pe.wait_ge(copied[b % 2][u], n * (B // 2))
                        for dx in range(K1):
                            last = nc.tensor.matmul(pa[:, u, b, 0:NBLK * WW].rearrange("p (k c) -> p k c", c=WW),
                                                    lhsT=wm[u][:, dx].rearrange("p y o -> p (y o)"),
                                                    rhs=xt[u][:, b, :, dx:dx + WW], start=dx == 0, stop=dx == K1 - 1)
                        last.then_inc(product[u], 1)

        def copy_out(eng, copy, which):
            with eng.Fori(0, TURNS) as n:
                for u in range(2):
                    g = n * 2 + u
                    if which == 1:
                        make_weights(eng, n, u)
                    eng.wait_ge(stored[u], n * (STORES * 16))
                    for b in range(which, B, 2):
                        eng.wait_ge(product[u], n * B + b + 1)
                        copy(ot[u][:, b].rearrange("p k c -> p (k c)"), pa[:, u, b, 0:NBLK * WW]).then_inc(copied[which][u], 1)

        def make_weights(dve, n, u):
            g = n * 2 + u
            dve.wait_ge(product[u], n * B)
            nc.vector.tensor_tensor(
                wm[u][:].rearrange("p d y o -> p (d y) o"),
                band[:, bass.ds(g, 1)].rearrange("p g d (y o) -> p (g d y) o", o=1).to_broadcast([PART, K1 * BLK, G8]),
                pw[:, bass.ds(g, 1), :].to_broadcast([PART, K1 * BLK, G8]), ALU.mult).then_inc(weights_ready, 1)

        @block.scalar
        def _(act):
            copy_out(act, lambda o, i: nc.scalar.activation(o, i, ACT.Copy), 0)

        @block.vector
        def _(dve):
            for u in range(2):
                nc.vector.memset(xt[u][:], 0.0).then_inc(border_zero, 1)
            dve.wait_ge(consts_in, (2 * BLK + 1) * 16)
            nc.vector.memset(band[:], 0.0).then_inc(band_step, 1)
            dve.wait_ge(band_step, 1)
            done = 1
            for dy in range(K1):
                first = done
                for y in range(BLK):
                    j = y + dy - K1 // 2
                    if 0 <= j < BLK:
                        to = band[:, :, :, y]
                        nc.vector.scalar_tensor_tensor(to, dw[:, :, dy, :], rm[:, j:j + 1], to, ALU.mult, ALU.add)\
                            .then_inc(band_step, 1)
                        done += 1
                dve.wait_ge(band_step, done)
            copy_out(dve, nc.vector.tensor_copy, 1)


def row_masks():
    return (np.arange(PART)[:, None] // G8 == np.arange(BLK)[None]).astype(np.float32)


HEADS1 = C // G8
SCALES = 2
ST = SCALES * HEADS1 // TG
EPS1 = 1e-15


def linear_attention(nc, scales, x_in, x_out, w_proj_t, head_mask, ident_in):
    ctx = ExitStack()
    with ctx:
        sb = lambda n, s, dt=F32: ctx.enter_context(nc.sbuf_tensor(f"d_{n}", s, dt))
        pb = lambda n, s: ctx.enter_context(nc.psum_tensor(f"d_{n}", s, F32))
        sem = lambda n: nc.alloc_semaphore(name=f"d_{n}")
        TPS = ST // SCALES
        NCH = NPX // PART
        PC = 512
        NPC = NPX // PC
        kt = [sb(f"kt{u}", [PART, NPX]) for u in range(2)]
        vt = [sb(f"vt{u}", [PART, NPX]) for u in range(2)]
        qt = sb("qt", [PART, ST, NPX])
        kvp = [sb(f"kvp{u}", [PART, 2, 2 * PART + 1]) for u in range(2)]
        kvm = sb("kvm", [PART, ST, PART])
        ksm = sb("ksm", [PART, ST, PART])
        wp = sb("wp", [PART, ST, C])
        hm = sb("hm", [PART, PART])
        ident = sb("ident", [PART, PART])
        den = [sb(f"den{u}", [PART, PC]) for u in range(2)]
        att = [sb(f"att{i}", [PART, PC]) for i in range(3)]
        xr = [sb(f"xr{u}", [PART, HALVES, PC]) for u in range(2)]
        work = pb("work", [PART, 2, 2, 512])
        pkv = pb("pkv", [PART, 512])
        pp = pb("pp", [PART, 2, 512])
        wait_taker = sb("wait_taker", [PART, 2])
        taken = sem("taken")
        consts_in = sem("consts_in")
        ones_ready = sem("ones_ready")
        kv_in = [sem(f"kv_in{u}") for u in range(2)]
        q_in = [sem(f"q_in{st}") for st in range(ST)]
        q_positive = sem("q_positive")
        turned = sem("turned")
        keys_copied = sem("keys_copied")
        values_copied = sem("values_copied")
        summed = sem("summed")
        kv_masked = sem("kv_masked")
        ks_masked = sem("ks_masked")
        ratio_parts = sem("ratio_parts")
        den_guarded = sem("den_guarded")
        den_inverted = sem("den_inverted")
        attended = sem("attended")
        projected = sem("projected")
        added = sem("added")
        x_loaded = [sem(f"x_loaded{u}") for u in range(2)]
        stored = [sem(f"stored{u}") for u in range(2)]
        block = ctx.enter_context(nc.Block())
        PAIRS = NCH // 2

        def heads_of(b, st, kind):
            s, t = divmod(st, TPS)
            first = 3 * TG * t
            return scales[s][bass.ds(b, 1), first:first + 3 * TG, :]\
                .rearrange("b (h k) (r i c) -> k i (b h) r c", k=3, i=G8, c=WW)[kind]

        @block.sync
        def _(sp):
            sp.dma_start(wp[:], w_proj_t.rearrange("(s p) o -> p s o", p=PART)).then_inc(consts_in, 16)
            sp.dma_start(hm[:], head_mask).then_inc(consts_in, 16)
            sp.dma_start(ident[:], ident_in).then_inc(consts_in, 16)
            with sp.Fori(0, B) as b:
                for st in range(ST):
                    u = st % 2
                    sp.wait_ge(turned, (b * ST + max(st - 1, 0)) * PAIRS)
                    for i in range(G8):
                        for kind, buf in ((1, kt), (2, vt)):
                            sp.dma_start(buf[u][i * TG:(i + 1) * TG].rearrange("p (r c) -> p r c", c=WW),
                                         heads_of(b, st, kind)[i]).then_inc(kv_in[u], 16)

        @block.gpsimd
        def _(pool):
            nc.gpsimd.memset(wait_taker[:], 0.0).then_inc(taken, 1)
            with pool.Fori(0, B) as b:
                for c in range(NPC + 1):
                    if c < NPC:
                        pool.wait_ge(stored[c % 2], (b * (NPC // 2) + c // 2) * 16)
                        pool.dma_start(xr[c % 2][:], x_in[bass.ds(b, 1), :, c * PC:(c + 1) * PC]
                                       .rearrange("b (h p) n -> p (b h) n", p=PART)).then_inc(x_loaded[c % 2], 16)
                    if c > 0:
                        pool.wait_ge(taken, b * NPC + c)
                        pool.wait_ge(added, (b * NPC + c) * HALVES)
                        nc.gpsimd.tensor_tensor(wait_taker[:, 0:1], wait_taker[:, 1:2], wait_taker[:, 1:2], ALU.add)\
                            .then_inc(taken, 1)
                        pool.dma_start(x_out[bass.ds(b, 1), :, (c - 1) * PC:c * PC]
                                       .rearrange("b (h p) n -> p (b h) n", p=PART), xr[(c - 1) % 2][:])\
                            .then_inc(stored[(c - 1) % 2], 16)
            for u in range(2):
                pool.wait_ge(stored[u], B * (NPC // 2) * 16)

        @block.tensor
        def _(pe):
            pe.wait_ge(consts_in, 48)
            pe.wait_ge(ones_ready, 2)
            with pe.Fori(0, B) as b:
                def turn(j):
                    st, k = divmod(j, PAIRS)
                    if k == 0:
                        pe.wait_ge(kv_in[st % 2], (b * (ST // 2) + st // 2 + 1) * (2 * G8 * 16))
                    pe.wait_ge(keys_copied, b * ST * PAIRS + max(j - 1, 0))
                    pe.wait_ge(values_copied, b * ST * PAIRS + max(j - 1, 0))
                    for e in range(2):
                        px = slice((2 * k + e) * PART, (2 * k + e + 1) * PART)
                        for v, buf in enumerate((kt, vt)):
                            last = nc.tensor.transpose(work[:, j % 2, v, e * PART:(e + 1) * PART], buf[st % 2][:, px], ident[:])
                    last.then_inc(turned, 1)

                def accumulate(j):
                    st, k = divmod(j, PAIRS)
                    pe.wait_ge(keys_copied, b * ST * PAIRS + j + 1)
                    pe.wait_ge(values_copied, b * ST * PAIRS + j + 1)
                    if k == 0:
                        pe.wait_ge(kv_masked, b * ST + st)
                        pe.wait_ge(ks_masked, b * ST + st)
                    for e in range(2):
                        last = nc.tensor.matmul(pkv[:, 0:PART + 1], lhsT=kvp[j % 2][:, e, 0:PART],
                                                rhs=kvp[j % 2][:, e, PART:2 * PART + 1],
                                                start=k == 0 and e == 0, stop=k == PAIRS - 1 and e == 1)
                    last.then_inc(summed, 1)

                for j in range(ST * PAIRS + 1):
                    if j < ST * PAIRS:
                        turn(j)
                    if j > 0:
                        accumulate(j - 1)

                def ratio(i):
                    c, st = divmod(i, ST)
                    if c == 0:
                        pe.wait_ge(q_positive, b * ST + st + 1)
                        pe.wait_ge(kv_masked, b * ST + st + 1)
                        pe.wait_ge(ks_masked, b * ST + st + 1)
                    pe.wait_ge(attended, b * NPC * ST + max(i - 1, 0))
                    px = slice(c * PC, (c + 1) * PC)
                    nc.tensor.matmul(work[:, i % 2, 1, :], lhsT=ksm[:, st], rhs=qt[:, st, px], start=True, stop=True)\
                        .then_inc(ratio_parts, 1)
                    nc.tensor.matmul(work[:, i % 2, 0, :], lhsT=kvm[:, st], rhs=qt[:, st, px], start=True, stop=True)\
                        .then_inc(ratio_parts, 1)

                def project(i):
                    c, st = divmod(i, ST)
                    pe.wait_ge(attended, b * NPC * ST + i + 1)
                    if st == 0:
                        pe.wait_ge(added, (b * NPC + c) * HALVES)
                    for m in range(HALVES):
                        last = nc.tensor.matmul(pp[:, m, :], lhsT=wp[:, st, m * PART:(m + 1) * PART],
                                                rhs=att[i % 3][:], start=st == 0, stop=st == ST - 1)
                    last.then_inc(projected, 1)

                for i in range(NPC * ST + 2):
                    if i < NPC * ST:
                        ratio(i)
                    if i >= 2:
                        project(i - 2)

        @block.scalar
        def _(act):
            with act.Fori(0, B) as b:
                act.wait_ge(attended, b * (NPC * ST))
                for st in range(ST):
                    for i in range(G8):
                        act.dma_start(qt[i * TG:(i + 1) * TG, st].rearrange("p (r c) -> p r c", c=WW),
                                      heads_of(b, st, 0)[i]).then_inc(q_in[st], 16)
                for j in range(ST * PAIRS):
                    act.wait_ge(turned, b * ST * PAIRS + j + 1)
                    act.wait_ge(summed, b * ST * PAIRS + max(j - 1, 0))
                    nc.scalar.activation(kvp[j % 2][:, :, 0:PART], work[:, j % 2, 0, 0:2 * PART].rearrange("p (e k) -> p e k", e=2), ACT.Relu).then_inc(keys_copied, 1)
                for st in range(ST):
                    act.wait_ge(q_in[st], (b + 1) * (G8 * 16))
                    nc.scalar.activation(qt[:, st], qt[:, st], ACT.Relu).then_inc(q_positive, 1)
                for i in range(NPC * ST):
                    act.wait_ge(ratio_parts, (b * NPC * ST + i) * 2 + 1)
                    act.wait_ge(attended, b * NPC * ST + max(i - 1, 0))
                    nc.scalar.activation(den[i % 2][:], work[:, i % 2, 1, :], ACT.Copy, bias=EPS1).then_inc(den_guarded, 1)

        @block.vector
        def _(dve):
            for u in range(2):
                nc.vector.memset(kvp[u][:, :, 2 * PART:2 * PART + 1], 1.0).then_inc(ones_ready, 1)
            dve.wait_ge(consts_in, 48)
            with dve.Fori(0, B) as b:
                for j in range(ST * PAIRS):
                    dve.wait_ge(turned, b * ST * PAIRS + j + 1)
                    dve.wait_ge(summed, b * ST * PAIRS + max(j - 1, 0))
                    nc.vector.tensor_copy(kvp[j % 2][:, :, PART:2 * PART], work[:, j % 2, 1, 0:2 * PART].rearrange("p (e k) -> p e k", e=2))\
                        .then_inc(values_copied, 1)
                    st, k = divmod(j, PAIRS)
                    if k == PAIRS - 1:
                        dve.wait_ge(summed, b * ST * PAIRS + j + 1)
                        nc.vector.tensor_tensor(kvm[:, st], pkv[:, 0:PART], hm[:], ALU.mult).then_inc(kv_masked, 1)
                        nc.vector.tensor_scalar(ksm[:, st], hm[:], pkv[:, PART:PART + 1], None, ALU.mult).then_inc(ks_masked, 1)

                def add(c):
                    dve.wait_ge(projected, (b * NPC + c + 1) * ST)
                    dve.wait_ge(x_loaded[c % 2], (b * (NPC // 2) + c // 2 + 1) * 16)
                    for m in range(HALVES):
                        nc.vector.tensor_tensor(xr[c % 2][:, m, :], pp[:, m, :], xr[c % 2][:, m, :], ALU.add).then_inc(added, 1)

                for i in range(NPC * ST):
                    dve.wait_ge(den_guarded, b * NPC * ST + i + 1)
                    nc.vector.reciprocal(den[i % 2][:], den[i % 2][:]).then_inc(den_inverted, 1)
                    if i >= 3 and (i - 3) % ST == ST - 1:
                        add((i - 3) // ST)
                    dve.wait_ge(den_inverted, b * NPC * ST + i + 1)
                    dve.wait_ge(ratio_parts, (b * NPC * ST + i) * 2 + 2)
                    dve.wait_ge(projected, b * NPC * ST + max(i - 2, 0))
                    nc.vector.tensor_tensor(att[i % 3][:], work[:, i % 2, 0, :], den[i % 2][:], ALU.mult).then_inc(attended, 1)
                add(NPC - 1)


def head_mask():
    h = np.arange(PART) % TG
    return (h[:, None] == h[None]).astype(np.float32)


def head_channels():
    return np.arange(ST * PART).reshape(ST, TG, G8).transpose(0, 2, 1).reshape(-1)


K2 = 7
R2 = 16
BPX = R2 * WW
HR = R2 + K2 - 1
HPX = HR * PW
NCK = BPX // PART
SPLIT = ((0, 3), (3, 2), (5, 2))
PER_O = len(SPLIT)
INNER = max(n for _, n in SPLIT)
GROUPS2 = [(o, i, n) for o in range(K2) for i, n in SPLIT]
NG2 = len(GROUPS2)
ON_POOL = (4, 8, 13, 17)


def channel_attention(nc, xn, x_in, x_out, w_t, rel, ident_in):
    ctx = ExitStack()
    with ctx:
        sb = lambda n, s, dt=F32: ctx.enter_context(nc.sbuf_tensor(f"e_{n}", s, dt))
        pb = lambda n, s: ctx.enter_context(nc.psum_tensor(f"e_{n}", s, F32))
        sem = lambda n: nc.alloc_semaphore(name=f"e_{n}")
        NSE, NEV = 6, 2
        POOL_AHEAD = 3
        wt = sb("wt", [PART, 3, HALVES, C])
        rl = sb("rl", [PART, HALVES, K2])
        ident = sb("ident", [PART, PART])
        xb = sb("xb", [PART, HALVES, HPX])
        q = [sb(f"q{u}", [PART, BPX]) for u in range(2)]
        k = [sb(f"k{u}", [PART, HPX]) for u in range(2)]
        v = [sb(f"v{u}", [PART, HPX]) for u in range(2)]
        kr = [sb(f"kr{u}", [PART, HPX]) for u in range(2)]
        m2 = sb("m2", [PART, HPX])
        m4 = sb("m4", [PART, HPX])
        ext = [sb(f"ext{i}", [PART, BPX]) for i in range(2)]
        top = [sb(f"top{u}", [PART, BPX]) for u in range(2)]
        se = [sb(f"se{i}", [PART, INNER, BPX]) for i in range(NSE)]
        ev = [sb(f"ev{i}", [PART, INNER, BPX]) for i in range(NEV)]
        rs = sb("rs", [PART, BPX])
        ws = sb("ws", [PART, BPX])
        xr = [sb(f"xr{u}", [PART, BPX]) for u in range(2)]
        pj = pb("pj", [PART, 2, 512])
        pe_sum = pb("pe_sum", [PART, NCK, PART])
        pv_sum = pb("pv_sum", [PART, NCK, PART])
        pback = pb("pback", [PART, 2, 512])
        consts_in = sem("consts_in")
        band_in = sem("band_in")
        rest_in = [sem(f"rest_in{u}") for u in range(2)]
        stored = [sem(f"stored{u}") for u in range(2)]
        projected = sem("projected")
        proj_copied = sem("proj_copied")
        rel_added = sem("rel_added")
        ext_step = sem("ext_step")
        top_products = sem("top_products")
        top_parts = sem("top_parts")
        top_ready = sem("top_ready")
        multiplied = sem("multiplied")
        pool_multiplied = sem("pool_multiplied")
        shifted = sem("shifted")
        exp_done = sem("exp_done")
        weighted = sem("weighted")
        e_summed = sem("e_summed")
        v_summed = sem("v_summed")
        e_taken = sem("e_taken")
        v_taken = sem("v_taken")
        inverted = sem("inverted")
        divided = sem("divided")
        turned_back = sem("turned_back")
        added = sem("added")
        RB = HH // R2
        NT = B * RB
        KCH2 = HPX // 4
        PROJ = [(1, i * KCH2, KCH2) for i in range(4)] + [(0, i * 512, 512) for i in range(BPX // 512)] \
            + [(2, i * KCH2, KCH2) for i in range(4)]
        NPJ = len(PROJ)
        NKEYS = 4
        PROJ_AT = [(0, 1), (2, 3)] + [(c,) for c in range(NKEYS, NPJ)]
        EXT = 3 + K2
        TOP_EARLY = 1
        ADD_AT = 13
        V_LAG = 2
        INV_PARTS = 4
        BACK_AT = 8
        EXT_FROM, EXT_TO = 6, 18
        EXT_GROUP = [EXT_FROM + s * (EXT_TO - EXT_FROM) // (2 * EXT) for s in range(2 * EXT)]
        block = ctx.enter_context(nc.Block())

        def count(n, h, per, more):
            return n * (HALVES * per) + (h * per + more)

        def window(t, h, o, i, n):
            dy, dx = (o, i) if h == 0 else (i, o)
            step = 1 if h == 0 else PW
            a = t[:, dy * PW + dx:dy * PW + dx + 1]
            return bass.AP(tensor=a.tensor, offset=a.offset, ap=[a.ap[0], [step, n], [PW, R2], [1, WW]])

        def flat(t, n):
            return t[:, 0:n].rearrange("p i (r c) -> p i r c", c=WW)

        def repeat(t, n):
            return t[:].rearrange("p (i r c) -> p i r c", i=1, c=WW).to_broadcast([PART, n, R2, WW])

        def scores(h, g):
            return se[(h * NG2 + g) % NSE]

        def keys_plus_rel(h, o):
            return kr[(h * K2 + o) % 2]

        def score_products(engine, h, g):
            o, i, taps = GROUPS2[g]
            return engine.tensor_tensor(flat(scores(h, g), taps), window(keys_plus_rel(h, o), h % 2, o, i, taps),
                                        repeat(q[h % 2], taps), ALU.mult)

        def all_half_bands(eng, half_band):
            half_band(0, 0, first=True)
            with eng.Fori(0, NT - 1) as n:
                half_band(n, 1)
                half_band(n, 2)
            half_band(NT - 1, 1, final=True)

        @block.sync
        def _(sp):
            for w in range(3):
                sp.dma_start(wt[:, w], w_t[w].rearrange("(h p) o -> p h o", p=PART)).then_inc(consts_in, 16)
            sp.dma_start(rl[:], rel.rearrange("(h p) k -> p h k", p=PART)).then_inc(consts_in, 16)
            sp.dma_start(ident[:], ident_in).then_inc(consts_in, 16)

            def band(t, n, h):
                return t[bass.ds(n // RB, 1), h * PART:(h + 1) * PART, bass.ds((n % RB) * BPX, BPX)]\
                    .rearrange("b p n -> (b p) n")

            def load_band(n):
                sp.dma_start(xb[:], xn[bass.ds(n // RB, 1), :, bass.ds((n % RB) * (R2 * PW), HPX)]
                             .rearrange("b (h p) n -> p (b h) n", p=PART)).then_inc(band_in, 16)

            def load_rest(n, h):
                sp.dma_start(xr[h][:], band(x_in, n, h)).then_inc(rest_in[h], 16)

            def store(n, h):
                sp.wait_ge(added, count(n, h, 2, 2))
                sp.dma_start(band(x_out, n, h), xr[h][:]).then_inc(stored[h], 16)

            def turn(n, final=False):
                sp.wait_ge(stored[0], n * 16)
                load_rest(n, 0)
                store(n - 1, 1)
                sp.wait_ge(stored[1], n * 16)
                load_rest(n, 1)
                if not final:
                    sp.wait_ge(projected, count(n, 2, NPJ, 0))
                    load_band(n + 1)
                store(n, 0)

            load_band(0)
            load_rest(0, 0)
            load_rest(0, 1)
            sp.wait_ge(projected, 2 * NPJ)
            load_band(1)
            store(0, 0)
            with sp.Fori(1, NT - 1) as n:
                turn(n)
            turn(NT - 1, final=True)
            store(NT - 1, 1)
            for h in range(HALVES):
                sp.wait_ge(stored[h], NT * 16)

        @block.tensor
        def _(pe):
            pe.wait_ge(consts_in, 80)

            def project(n, h, chunks):
                for c in chunks:
                    w, first, size = PROJ[c]
                    if h % 2 == 0 and c == 0:
                        pe.wait_ge(band_in, (n + h // 2 + 1) * 16)
                    if h or c >= 2:
                        pe.wait_ge(proj_copied, count(n, h, NPJ, c - 1))
                    for g in range(HALVES):
                        if w == 0:
                            rows = xb[:, g].rearrange("p (r c) -> p r c", c=PW)
                            first_row = PAD + first // WW
                            rhs = rows[:, first_row:first_row + size // WW, PAD:PAD + WW]
                            out = pj[:, c % 2, 0:size].rearrange("p (r c) -> p r c", c=WW)
                        else:
                            rhs, out = xb[:, g, first:first + size], pj[:, c % 2, 0:size]
                        last = nc.tensor.matmul(out, lhsT=wt[:, w, g, (h % 2) * PART:(h % 2 + 1) * PART], rhs=rhs,
                                                start=g == 0, stop=g == HALVES - 1)
                    last.then_inc(projected, 1)

            def add_up(g, src, acc):
                for e in range(GROUPS2[g][2]):
                    for c in range(NCK):
                        last = nc.tensor.matmul(acc[:, c, :], lhsT=src[:, e, c * PART:(c + 1) * PART], rhs=ident[:],
                                                is_transpose=True, start=g == 0 and e == 0 and c % 4 == 0,
                                                stop=g == NG2 - 1 and e == GROUPS2[g][2] - 1, skip_group_check=True)
                return last

            def sum_exponentials(n, h, g):
                pe.wait_ge(exp_done, count(n, h, NG2, g + 1))
                add_up(g, scores(h, g), pe_sum).then_inc(e_summed, 1)

            def sum_weighted(n, h, g):
                pe.wait_ge(weighted, count(n, h, NG2, g + 1))
                add_up(g, ev[(h * NG2 + g) % NEV], pv_sum).then_inc(v_summed, 1)

            def back(n, h):
                pe.wait_ge(divided, count(n, h, 1, 1))
                if h:
                    pe.wait_ge(added, count(n, h, 2, 0))
                for c in range(NCK):
                    last = nc.tensor.transpose(pback[:, c // 4, (c % 4) * PART:(c % 4 + 1) * PART],
                                               rs[:, c * PART:(c + 1) * PART], ident[:])
                last.then_inc(turned_back, 1)

            def half_band(n, h, first=False, final=False):
                for g in range(NG2):
                    if g < len(PROJ_AT) and not final:
                        project(n, h + 1, PROJ_AT[g])
                    if g == 0 and not first:
                        pe.wait_ge(e_taken, count(n, h, 1, 0))
                    sum_exponentials(n, h, g)
                    if g == V_LAG and not first:
                        pe.wait_ge(v_taken, count(n, h, 1, 0))
                    if g >= V_LAG:
                        sum_weighted(n, h, g - V_LAG)
                    elif not first:
                        sum_weighted(n, h - 1, NG2 + g - V_LAG)
                    if g == BACK_AT and not first:
                        back(n, h - 1)

            project(0, 0, range(NPJ))
            all_half_bands(pe, half_band)
            for g in range(NG2 - V_LAG, NG2):
                sum_weighted(NT - 1, 1, g)
            back(NT - 1, 1)

        @block.scalar
        def _(act):
            act.wait_ge(consts_in, 80)

            def copy_projection(n, h, chunks):
                for c in chunks:
                    w, first, size = PROJ[c]
                    if h and c == 0:
                        act.wait_ge(shifted, count(n, h - 1, NG2, 0))
                    if h and w == 2 and first == 0:
                        act.wait_ge(weighted, count(n, h - 1, NG2, 0))
                    act.wait_ge(projected, count(n, h, NPJ, c + 1))
                    nc.scalar.activation((q, k, v)[w][h % 2][:, first:first + size], pj[:, c % 2, 0:size], ACT.Copy)\
                        .then_inc(proj_copied, 1)

            def add_rel(n, h, o):
                if h or o >= 2:
                    act.wait_ge(shifted, count(n, h, NG2, PER_O * (o - 1)))
                act.wait_ge(proj_copied, count(n, h, NPJ, NKEYS))
                nc.scalar.activation(keys_plus_rel(h, o)[:], k[h % 2][:], ACT.Identity, bias=rl[:, h % 2, o:o + 1])\
                    .then_inc(rel_added, 1)

            def take_e_sums(n, h):
                act.wait_ge(e_summed, count(n, h, NG2, NG2))
                if h:
                    act.wait_ge(turned_back, count(n, h, 1, 0))
                nc.scalar.activation(rs[:], pe_sum[:].rearrange("p c k -> p (c k)"), ACT.Copy).then_inc(e_taken, 1)

            def take_v_sums(n, h):
                act.wait_ge(v_summed, count(n, h, NG2, NG2))
                if h:
                    act.wait_ge(divided, count(n, h, 1, 0))
                nc.scalar.activation(ws[:], pv_sum[:].rearrange("p c k -> p (c k)"), ACT.Copy).then_inc(v_taken, 1)

            def half_band(n, h, first=False, final=False):
                for g in range(NG2):
                    taps = GROUPS2[g][2]
                    act.wait_ge(shifted, count(n, h, NG2, g + 1))
                    nc.scalar.activation(scores(h, g)[:, 0:taps], scores(h, g)[:, 0:taps], ACT.Exp).then_inc(exp_done, 1)
                    if g == 0 and not first:
                        take_e_sums(n, h - 1)
                    if g == V_LAG and not first:
                        take_v_sums(n, h - 1)
                    if g % PER_O == PER_O - 1:
                        next_h, o = divmod(g // PER_O + 2, K2)
                        if next_h == 0 or not final:
                            add_rel(n, h + next_h, o)
                    if 1 <= g <= len(PROJ_AT) and not final:
                        copy_projection(n, h + 1, PROJ_AT[g - 1])

            copy_projection(0, 0, range(NPJ))
            add_rel(0, 0, 0)
            add_rel(0, 0, 1)
            all_half_bands(act, half_band)
            take_e_sums(NT - 1, 1)
            take_v_sums(NT - 1, 1)

        @block.gpsimd
        def _(pool):
            def top_product(n, h, i):
                pool.wait_ge(top_parts, count(n, h, 2, i + 1))
                pool.wait_ge(proj_copied, count(n, h, NPJ, NKEYS + BPX // 512))
                nc.gpsimd.tensor_tensor(ext[i][:], ext[i][:], q[h % 2][:], ALU.mult).then_inc(top_products, 1)

            def weigh(n, h, g):
                o, i, taps = GROUPS2[g]
                pool.wait_ge(exp_done, count(n, h, NG2, g + 1))
                if h or g >= 2:
                    pool.wait_ge(v_summed, count(n, h, NG2, g - 1))
                nc.gpsimd.tensor_tensor(flat(ev[(h * NG2 + g) % NEV], taps), flat(scores(h, g), taps),
                                        window(v[h % 2], h % 2, o, i, taps), ALU.mult).then_inc(weighted, 1)

            def multiply(n, h, g):
                pool.wait_ge(rel_added, count(n, h, K2, GROUPS2[g][0] + 1))
                if h or g >= NSE:
                    pool.wait_ge(e_summed, count(n, h, NG2, g - NSE + 1))
                    pool.wait_ge(weighted, count(n, h, NG2, g - NSE + 1))
                score_products(nc.gpsimd, h, g).then_inc(pool_multiplied, 1)

            def half_band(n, h, first=False, final=False):
                for g in range(NG2):
                    if g + POOL_AHEAD in ON_POOL:
                        multiply(n, h, g + POOL_AHEAD)
                    weigh(n, h, g)
                    if not final:
                        if g == EXT_GROUP[EXT - 1] - TOP_EARLY:
                            top_product(n, h + 1, 0)
                        if g == EXT_GROUP[2 * EXT - 1] - TOP_EARLY:
                            top_product(n, h + 1, 1)

            top_product(0, 0, 0)
            top_product(0, 0, 1)
            all_half_bands(pool, half_band)

        @block.vector
        def _(dve):
            dve.wait_ge(consts_in, 80)

            def extreme_step(n, h, step):
                i, t = divmod(step, EXT)
                op = (ALU.max, ALU.min)[i]
                if step == 0:
                    dve.wait_ge(proj_copied, count(n, h, NPJ, NKEYS))
                if t == 0 and (h or i):
                    dve.wait_ge(top_parts, count(n, h, 2, i))
                if t > 0:
                    dve.wait_ge(ext_step, count(n, h, 2 * (EXT - 1), i * (EXT - 1) + t))
                if t < 3:
                    away = 1 if h % 2 == 0 else PW
                    size = HPX - (1, 3, 6)[t] * away
                    by = (1, 2, 3)[t] * away
                    src, dst = ((k[h % 2], m2), (m2, m4), (m4, m2))[t]
                    nc.vector.tensor_tensor(dst[:, 0:size], src[:, 0:size], src[:, by:by + size], op).then_inc(ext_step, 1)
                    return
                o = t - 3
                first = o * PW if h % 2 == 0 else o
                win = m2[:, first:first + 1]
                win = bass.AP(tensor=win.tensor, offset=win.offset, ap=[win.ap[0], [PW, R2], [1, WW]])
                to = ext[i][:].rearrange("p (r c) -> p r c", c=WW)
                r = rl[:, h % 2, o:o + 1]
                if o == 0:
                    if h:
                        dve.wait_ge(top_ready, count(n, h, 1, 0))
                    nc.vector.tensor_scalar(to, win, r, None, ALU.add).then_inc(ext_step, 1)
                else:
                    nc.vector.scalar_tensor_tensor(to, win, r, to, ALU.add, op)\
                        .then_inc(top_parts if o == K2 - 1 else ext_step, 1)

            def largest(n, h):
                dve.wait_ge(top_products, count(n, h, 2, 2))
                nc.vector.tensor_tensor(top[h % 2][:], ext[0][:], ext[1][:], ALU.max).then_inc(top_ready, 1)

            def multiply(n, h, g):
                dve.wait_ge(rel_added, count(n, h, K2, GROUPS2[g][0] + 1))
                if h or g >= NSE:
                    dve.wait_ge(e_summed, count(n, h, NG2, g - NSE + 1))
                    dve.wait_ge(weighted, count(n, h, NG2, g - NSE + 1))
                score_products(nc.vector, h, g).then_inc(multiplied, 1)

            def shift(n, h, g):
                taps = GROUPS2[g][2]
                on_pool = sum(p <= g for p in ON_POOL)
                if g in ON_POOL:
                    dve.wait_ge(pool_multiplied, count(n, h, len(ON_POOL), on_pool))
                else:
                    dve.wait_ge(multiplied, count(n, h, NG2 - len(ON_POOL), g + 1 - on_pool))
                if g == 0:
                    dve.wait_ge(top_ready, count(n, h, 1, 1))
                nc.vector.tensor_tensor(flat(scores(h, g), taps), flat(scores(h, g), taps), repeat(top[h % 2], taps),
                                        ALU.subtract).then_inc(shifted, 1)

            def invert(n, h, part):
                dve.wait_ge(e_taken, count(n, h, 1, 1))
                s = slice(part * (BPX // INV_PARTS), (part + 1) * (BPX // INV_PARTS))
                nc.vector.reciprocal(rs[:, s], rs[:, s]).then_inc(inverted, 1)

            def divide(n, h):
                dve.wait_ge(v_taken, count(n, h, 1, 1))
                dve.wait_ge(inverted, count(n, h, INV_PARTS, INV_PARTS))
                nc.vector.tensor_tensor(rs[:], rs[:], ws[:], ALU.mult).then_inc(divided, 1)

            def add(n, h):
                dve.wait_ge(turned_back, count(n, h, 1, 1))
                dve.wait_ge(rest_in[h % 2], (n + h // 2 + 1) * 16)
                for c in range(2):
                    s = slice(c * 512, (c + 1) * 512)
                    nc.vector.tensor_tensor(xr[h % 2][:, s], pback[:, c, :], xr[h % 2][:, s], ALU.add).then_inc(added, 1)

            def half_band(n, h, first=False, final=False):
                for g in range(NG2):
                    if g + 1 < NG2:
                        if g + 1 not in ON_POOL:
                            multiply(n, h, g + 1)
                    elif not final:
                        multiply(n, h + 1, 0)
                    if g == 0:
                        largest(n, h)
                    shift(n, h, g)
                    if not first:
                        if 2 <= g < 2 + INV_PARTS:
                            invert(n, h - 1, g - 2)
                        if g == 2 + INV_PARTS:
                            divide(n, h - 1)
                        if g == ADD_AT:
                            add(n, h - 1)
                    if not final:
                        for step in range(2 * EXT):
                            if EXT_GROUP[step] == g:
                                extreme_step(n, h + 1, step)

            for step in range(2 * EXT):
                extreme_step(0, 0, step)
            multiply(0, 0, 0)
            all_half_bands(dve, half_band)
            for part in range(INV_PARTS):
                invert(NT - 1, 1, part)
            divide(NT - 1, 1)
            add(NT - 1, 1)


K3 = 4
HID = 65
TEMP = 0.5
KW3 = 3
TAPS = KW3 * KW3
R3 = 8
BPX3 = R3 * WW
HR3 = R3 + KW3 - 1


def dynamic_conv(nc, xn, pooled, x_in, x_out, w1_t, w2_t, b2, w_sets, ident_in):
    ctx = ExitStack()
    with ctx:
        sb = lambda n, s, dt=F32: ctx.enter_context(nc.sbuf_tensor(f"f_{n}", s, dt))
        pb = lambda n, s: ctx.enter_context(nc.psum_tensor(f"f_{n}", s, F32))
        sem = lambda n: nc.alloc_semaphore(name=f"f_{n}")
        KH = K3 * HALVES
        w1 = sb("w1", [PART, HALVES, HID])
        w2 = sb("w2", [HID, KH, PART])
        b2t = sb("b2t", [PART, KH])
        pl = sb("pl", [PART, HALVES, B])
        hid = sb("hid", [HID, B])
        lg = sb("lg", [PART, K3, HALVES * B])
        mx = sb("mx", [PART, HALVES * B])
        sm = sb("sm", [PART, HALVES * B])
        ident = sb("ident", [PART, PART])
        ws = sb("ws", [PART, K3, HALVES, TAPS * C])
        mw = [sb(f"mw{u}", [PART, HALVES, TAPS * C]) for u in range(2)]
        wc = [sb(f"wc{u}", [PART, HALVES, TAPS, C]) for u in range(2)]
        xb = [sb(f"xb{u}", [PART, HALVES, HR3 * PW]) for u in range(2)]
        xr = [sb(f"xr{u}", [PART, HALVES, BPX3]) for u in range(2)]
        pm = pb("pm", [PART, 2, 512])
        pw = pb("pw", [PART, 2, 512])
        pc = pb("pc", [PART, 2, HALVES, 512])
        consts_in = sem("consts_in")
        sets_in = sem("sets_in")
        hidden = sem("hidden")
        hidden_ready = sem("hidden_ready")
        logits = sem("logits")
        soft = sem("soft")
        mixed_part = sem("mixed_part")
        mixed = sem("mixed")
        turned = sem("turned")
        turned_copied = sem("turned_copied")
        band_in = [sem(f"band_in{u}") for u in range(2)]
        rest_in = [sem(f"rest_in{u}") for u in range(2)]
        convolved = [sem(f"convolved{u}") for u in range(2)]
        added = [sem(f"added{u}") for u in range(2)]
        stored = [sem(f"stored{u}") for u in range(2)]
        TURNS = HH // R3 // 2
        NTURN = TAPS * HALVES * HALVES // 4
        block = ctx.enter_context(nc.Block())

        @block.sync
        def _(sp):
            slow = dict(allow_slow_non_contiguous=True)
            sp.dma_start(w1[:], w1_t.rearrange("(h p) o -> p h o", p=PART)).then_inc(consts_in, 16)
            sp.dma_start(w2[:].rearrange("p k o -> p (k o)"), w2_t).then_inc(consts_in, 16)
            sp.dma_start(b2t[:], b2.rearrange("(m p) -> p m", p=PART), **slow).then_inc(consts_in, 16)
            for b in range(B):
                sp.dma_start(pl[:, :, b], pooled[b].rearrange("(h p) -> p h", p=PART), **slow).then_inc(consts_in, 16)
            sp.dma_start(ident[:], ident_in).then_inc(consts_in, 16)
            for k in range(K3):
                sp.dma_start(ws[:, k], w_sets[k].rearrange("(h p) n -> p h n", p=PART)).then_inc(sets_in, 16)
            for b in range(B):
                with sp.Fori(0, TURNS) as r:
                    n = r + b * TURNS
                    for u in range(2):
                        sp.wait_ge(convolved[u], n * HALVES)
                        first = (PAD - KW3 // 2 + u * R3) * PW
                        sp.dma_start(xb[u][:], xn[b, :, bass.ds(r * (2 * R3 * PW) + first, HR3 * PW)]
                                     .rearrange("(h p) n -> p h n", p=PART)).then_inc(band_in[u], 16)
                        sp.wait_ge(stored[u], n * 16)
                        sp.dma_start(xr[u][:], x_in[b, :, bass.ds(r * (2 * BPX3) + u * BPX3, BPX3)]
                                     .rearrange("(h p) n -> p h n", p=PART)).then_inc(rest_in[u], 16)

        @block.gpsimd
        def _(pool):
            for b in range(B):
                with pool.Fori(0, TURNS) as r:
                    n = r + b * TURNS
                    for u in range(2):
                        pool.wait_ge(added[u], (n + 1) * HALVES)
                        pool.dma_start(x_out[b, :, bass.ds(r * (2 * BPX3) + u * BPX3, BPX3)]
                                       .rearrange("(h p) n -> p h n", p=PART), xr[u][:]).then_inc(stored[u], 16)
            for u in range(2):
                pool.wait_ge(stored[u], B * TURNS * 16)

        @block.tensor
        def _(pe):
            pe.wait_ge(consts_in, (4 + B) * 16)
            for h in range(HALVES):
                last = nc.tensor.matmul(pm[0:HID, 0, 0:B], lhsT=w1[:, h], rhs=pl[:, h], start=h == 0, stop=h == 1)
            last.then_inc(hidden, 1)
            pe.wait_ge(hidden_ready, 1)
            for m in range(KH):
                last = nc.tensor.matmul(pm[:, 1, m * B:(m + 1) * B], lhsT=w2[:, m], rhs=hid[:], start=True, stop=True)
            last.then_inc(logits, 1)
            for b in range(B):
                pe.wait_ge(mixed, (b + 1) * HALVES)
                for j in range(NTURN):
                    pe.wait_ge(turned_copied, b * NTURN + max(j - 1, 0))
                    for i in range(4):
                        t, g = divmod(j * 2 + i // 2, HALVES)
                        o = i % 2
                        last = nc.tensor.transpose(pw[:, j % 2, i * PART:(i + 1) * PART],
                                                   mw[b % 2][:, o, t * C + g * PART:t * C + (g + 1) * PART], ident[:])
                    last.then_inc(turned, 1)
                pe.wait_ge(turned_copied, (b + 1) * NTURN)
                with pe.Fori(0, TURNS) as r:
                    n = r + b * TURNS
                    for u in range(2):
                        pe.wait_ge(band_in[u], n * 16 + 16)
                        pe.wait_ge(added[u], n * HALVES)
                        rows = xb[u][:].rearrange("p h (r c) -> p h r c", c=PW)
                        for m in range(HALVES):
                            for t in range(TAPS):
                                dy, dx = divmod(t, KW3)
                                for g in range(HALVES):
                                    c0 = PAD - KW3 // 2 + dx
                                    last = nc.tensor.matmul(pc[:, u, m].rearrange("p (r c) -> p r c", c=WW),
                                                            lhsT=wc[b % 2][:, g, t, m * PART:(m + 1) * PART],
                                                            rhs=rows[:, g, dy:dy + R3, c0:c0 + WW],
                                                            start=t == 0 and g == 0, stop=t == TAPS - 1 and g == 1)
                            last.then_inc(convolved[u], 1)

        @block.scalar
        def _(act):
            act.wait_ge(hidden, 1)
            nc.scalar.activation(hid[:], pm[0:HID, 0, 0:B], ACT.Relu).then_inc(hidden_ready, 1)
            act.wait_ge(soft, KH + 2)
            nc.scalar.activation(lg[:].rearrange("p k n -> p (k n)"), lg[:].rearrange("p k n -> p (k n)"), ACT.Exp,
                                 scale=1.0 / TEMP).then_inc(soft, 1)
            for b in range(B):
                for j in range(NTURN):
                    act.wait_ge(turned, b * NTURN + j + 1)
                    if b >= 2:
                        for u in range(2):
                            act.wait_ge(convolved[u], (b - 1) * TURNS * HALVES)
                    src = pw[:, j % 2].rearrange("p (g o) -> p g o", g=2)
                    nc.scalar.activation(wc[b % 2][:, :, j, :], src, ACT.Copy).then_inc(turned_copied, 1)

        @block.vector
        def _(dve):
            dve.wait_ge(consts_in, (4 + B) * 16)
            dve.wait_ge(logits, 1)
            flat = lg[:].rearrange("p k (h b) -> p (k h) b", b=B)
            for m in range(KH):
                nc.vector.tensor_scalar(flat[:, m], pm[:, 1, m * B:(m + 1) * B], b2t[:, m:m + 1], None, ALU.add)\
                    .then_inc(soft, 1)
            dve.wait_ge(soft, KH)
            by_k = lg[:].rearrange("p k n -> p n k")
            nc.vector.tensor_reduce(mx[:], by_k, AX.X, ALU.max).then_inc(soft, 1)
            dve.wait_ge(soft, KH + 1)
            rep = lambda t: t[:].rearrange("p (o n) -> p o n", o=1).to_broadcast([PART, K3, HALVES * B])
            nc.vector.tensor_tensor(lg[:], lg[:], rep(mx), ALU.subtract).then_inc(soft, 1)
            dve.wait_ge(soft, KH + 3)
            nc.vector.tensor_reduce(sm[:], by_k, AX.X, ALU.add).then_inc(soft, 1)
            dve.wait_ge(soft, KH + 4)
            nc.vector.reciprocal(sm[:], sm[:]).then_inc(soft, 1)
            dve.wait_ge(soft, KH + 5)
            nc.vector.tensor_tensor(lg[:], lg[:], rep(sm), ALU.mult).then_inc(soft, 1)
            dve.wait_ge(soft, KH + 6)
            dve.wait_ge(sets_in, K3 * 16)

            def mix(b):
                if b >= 2:
                    dve.wait_ge(turned, (b - 1) * NTURN)
                for k in range(K3):
                    for o in range(HALVES):
                        s = lg[:, k, o * B + b:o * B + b + 1]
                        to = mw[b % 2][:, o]
                        if k == 0:
                            ins = nc.vector.tensor_scalar(to, ws[:, k, o], s, None, ALU.mult)
                        else:
                            dve.wait_ge(mixed_part, (b * (K3 - 1) + k - 1) * HALVES + o + 1)
                            ins = nc.vector.scalar_tensor_tensor(to, ws[:, k, o], s, to, ALU.mult, ALU.add)
                        ins.then_inc(mixed if k == K3 - 1 else mixed_part, 1)

            mix(0)
            mix(1)
            for b in range(B):
                with dve.Fori(0, TURNS) as r:
                    n = r + b * TURNS
                    for u in range(2):
                        dve.wait_ge(rest_in[u], n * 16 + 16)
                        for m in range(HALVES):
                            dve.wait_ge(convolved[u], n * HALVES + m + 1)
                            nc.vector.tensor_tensor(xr[u][:, m], pc[:, u, m], xr[u][:, m], ALU.add).then_inc(added[u], 1)
                if b + 2 < B:
                    mix(b + 2)


def four_layers(nc, x, out, w):
    def scratch(name, shape):
        return nc.dram_tensor(name, shape, F32, kind="Internal").ap()

    xn = [scratch(f"xn{i}", [B, C, PPX]) for i in range(4)]
    xs = [x] + [scratch(f"x{i}", [B, C, NPX]) for i in (1, 2, 3)] + [out]
    qkv = scratch("qkv", [B, GROUPS, GPX])
    agg = scratch("agg", [B, GROUPS, GPX])
    pooled = scratch("pooled", [B, C])

    norm_sems = norm_semaphores(nc)
    group_norm(nc, norm_sems, 0, xs[0], xn[0], w["group_mean"])
    window_attention(nc, xn[0], xs[0], xs[1], w["L0_w_qkv_t"], w["L0_b_qkv"], w["attention_masks"], w["identity"])
    group_norm(nc, norm_sems, 1, xs[1], xn[1], w["group_mean"])
    qkv_project(nc, xn[1], qkv, w["L1_w_qkv_t"])
    grouped_conv(nc, qkv, agg, w["L1_w_dw"], w["L1_w_pw"], w["row_masks"])
    linear_attention(nc, [qkv, agg], xs[1], xs[2], w["L1_w_proj_t"], w["head_mask"], w["identity"])
    group_norm(nc, norm_sems, 2, xs[2], xn[2], w["group_mean"])
    channel_attention(nc, xn[2], xs[2], xs[3], w["L2_w_t"], w["L2_rel"], w["identity"])
    group_norm(nc, norm_sems, 3, xs[3], xn[3], w["group_mean"], pooled=pooled)
    dynamic_conv(nc, xn[3], pooled, xs[3], xs[4], w["L3_w1_t"], w["L3_w2_t"], w["L3_b2"], w["L3_w_sets"], w["identity"])


def laid_out(i):
    a = {k: np.asarray(v) for k, v in i.items()}
    return {
        "L0_w_qkv_t": a["L0_conv_w_qkv"].T,
        "L0_b_qkv": a["L0_conv_b_qkv"],
        "L1_w_qkv_t": a["L1_conv_w_qkv"].reshape(C3, C)[permuted_channels()].T,
        "L1_w_dw": a["L1_conv_w_dw"].reshape(GROUPS, G8, K1 * K1).transpose(1, 0, 2).reshape(G8, -1),
        "L1_w_pw": a["L1_conv_w_pw"].reshape(GROUPS, G8, G8).transpose(2, 0, 1).reshape(G8, -1),
        "L1_w_proj_t": a["L1_conv_w_proj"].reshape(C, ST * PART).T[head_channels()],
        "L2_w_t": np.stack([a[f"L2_conv_w_{c}"].T for c in "qkv"]),
        "L2_rel": np.concatenate([a["L2_conv_rel_h"].reshape(C // 2, K2), a["L2_conv_rel_w"].reshape(C // 2, K2)]),
        "L3_w1_t": a["L3_conv_w1"].T,
        "L3_w2_t": a["L3_conv_w2"].T,
        "L3_b2": a["L3_conv_b2"],
        "L3_w_sets": a["L3_conv_weight"].reshape(K3, C, C, TAPS).transpose(0, 1, 3, 2).reshape(K3, C, TAPS * C),
        "group_mean": group_mean(),
        "attention_masks": attention_masks(),
        "row_masks": row_masks(),
        "head_mask": head_mask(),
        "identity": np.eye(PART, dtype=np.float32),
    }


def kernel(**inputs):
    import concourse.bacc as _bacc
    from concourse.bass_utils import run_bass_kernel_spmd as _run

    x = np.asarray(inputs["x"])
    arrays = {"x": np.ascontiguousarray(x.reshape(B, C, NPX))}
    arrays.update((k, np.ascontiguousarray(v)) for k, v in laid_out(inputs).items())
    nc = _bacc.Bacc("TRN2", target_bir_lowering=False, num_devices=1)
    aps = {k: nc.dram_tensor(f"in_{k}", v.shape, mybir.dt.from_np(v.dtype), kind="ExternalInput").ap()
           for k, v in arrays.items()}
    out = nc.dram_tensor("out_x", (B, C, NPX), F32, kind="ExternalOutput").ap()
    four_layers(nc, aps["x"], out, aps)
    r = _run(nc, [{f"in_{k}": v for k, v in arrays.items()}], core_ids=[0])
    return r.results[0]["out_x"].reshape(x.shape)
```

```python
import concourse.bass as bass
from concourse import mybir
from concourse.alu_op_type import AluOpType as ALU
from contextlib import ExitStack, contextmanager
import numpy as np

ACT = mybir.ActivationFunctionType
AX = mybir.AxisListType
F32 = mybir.dt.float32
F32R = mybir.dt.float32r

B, C, HH, WW = 4, 256, 64, 64
NPX = HH * WW
PART = 128
HALVES = C // PART
PAD = 3
PW = WW + 2 * PAD
PPX = (HH + 2 * PAD) * PW
EPS = 1e-5


NORM_PAIRS = ("x_loaded", "stats_ready", "group_ready", "var_ready", "std_ready", "coef_ready", "norm_done",
              "xn_stored", "pooled_stored")


def norm_semaphores(nc):
    sems = {n: [nc.alloc_semaphore(name=f"n_{n}{h}") for h in range(HALVES)] for n in NORM_PAIRS}
    return sems | {n: nc.alloc_semaphore(name=f"n_{n}") for n in ("gm_loaded", "border_zero", "chain")}


def group_norm(nc, sems, call, x_in, xn_out, mean_matrix, pooled=None):
    tag = f"n{call}"
    before = call * B
    (x_loaded, stats_ready, group_ready, var_ready, std_ready, coef_ready, norm_done, xn_stored,
     pooled_stored) = (sems[n] for n in NORM_PAIRS)
    gm_loaded, border_zero, chain = sems["gm_loaded"], sems["border_zero"], sems["chain"]
    ctx = ExitStack()
    with ctx:
        sb = lambda n, s, dt=F32: ctx.enter_context(nc.sbuf_tensor(f"{tag}_{n}", s, dt))
        xt = [sb(f"xt{h}", [PART, NPX]) for h in range(HALVES)]
        xnp = [sb(f"xnp{h}", [PART, PPX]) for h in range(HALVES)]
        stats = [sb(f"stats{h}", [PART, NPX // 512, 6]) for h in range(HALVES)]
        ms = [sb(f"ms{h}", [PART, 2]) for h in range(HALVES)]
        gs = [sb(f"gs{h}", [PART, 2]) for h in range(HALVES)]
        var = [sb(f"var{h}", [PART, 1]) for h in range(HALVES)]
        std = [sb(f"std{h}", [PART, 1]) for h in range(HALVES)]
        coef = [sb(f"coef{h}", [PART, 2]) for h in range(HALVES)]
        pool_t = [sb(f"pool{h}", [PART, 1]) for h in range(HALVES)]
        wait_taker = sb("wait_taker", [PART, HALVES])
        gm = sb("gm", [PART, PART])
        psum = ctx.enter_context(nc.psum_tensor(f"{tag}_psum", [PART, HALVES, 512], F32))
        block = ctx.enter_context(nc.Block())

        @block.sync
        def _(sp):
            sp.dma_start(gm[:], mean_matrix).then_inc(gm_loaded, 16)
            with sp.Fori(0, B) as b:
                for h in range(HALVES):
                    sp.wait_ge(norm_done[h], before + b)
                    sp.dma_start(xt[h][:], x_in[bass.ds(b, 1), h * PART:(h + 1) * PART, :]
                                 .rearrange("b p n -> (b p) n")).then_inc(x_loaded[h], 16)

        @block.gpsimd
        def _(pool):
            pool.memset(xnp[0][:], 0.0).then_inc(border_zero, 1)
            pool.memset(xnp[1][:], 0.0).then_inc(border_zero, 1)
            with pool.Fori(0, B) as b:
                for h in range(HALVES):
                    pool.wait_ge(norm_done[h], before + b + 1)
                    pool.dma_start(xn_out[bass.ds(b, 1), h * PART:(h + 1) * PART, :]
                                   .rearrange("b p n -> (b p) n"), xnp[h][:]).then_inc(xn_stored[h], 16)
                    if pooled is not None:
                        pool.wait_ge(coef_ready[h], before + b + 1)
                        pool.dma_start(pooled[bass.ds(b, 1), h * PART:(h + 1) * PART]
                                       .rearrange("b p -> p b"), pool_t[h][:]).then_inc(pooled_stored[h], 16)
            for h in range(HALVES):
                pool.wait_ge(xn_stored[h], 16 * (before + B))
                if pooled is not None:
                    pool.wait_ge(pooled_stored[h], 16 * B)

        @block.vector
        def _(dve):
            STEPS0 = 5 * HALVES
            STEPS = STEPS0 + (HALVES if pooled is not None else 0)
            with dve.Fori(0, B) as b:
                n = [0]

                def link(ins):
                    n[0] += 1
                    ins.then_inc(chain, 1)
                    dve.wait_ge(chain, before * STEPS0 + b * STEPS + n[0])

                for h in range(HALVES):
                    dve.wait_ge(x_loaded[h], (before + b + 1) * 16)
                    for k in range(NPX // 512):
                        ins = nc.vector.bn_stats(stats[h][:, k, :], xt[h][:, k * 512:(k + 1) * 512])
                    link(ins)
                    nc.vector.memset(wait_taker[:, h:h + 1], 0.0)
                    link(nc.vector.bn_aggr(ms[h][:], stats[h][:]))
                    nc.vector.scalar_tensor_tensor(ms[h][:, 1:2], ms[h][:, 0:1], ms[h][:, 0:1], ms[h][:, 1:2],
                                                   ALU.mult, ALU.add).then_inc(stats_ready[h], 1)
                    dve.wait_ge(group_ready[h], before + b + 1)
                    link(nc.vector.tensor_copy(gs[h][:], psum[:, h, 0:2]))
                    link(nc.vector.scalar_tensor_tensor(var[h][:], gs[h][:, 0:1], gs[h][:, 0:1], gs[h][:, 1:2],
                                                        ALU.mult, ALU.subtract))
                    nc.vector.tensor_scalar(var[h][:], var[h][:], -1.0, EPS, ALU.mult, ALU.add)\
                        .then_inc(var_ready[h], 1)
                    dve.wait_ge(std_ready[h], before + b + 1)
                    link(nc.vector.reciprocal(coef[h][:, 0:1], std[h][:]))
                    if pooled is not None:
                        dve.wait_ge(pooled_stored[h], b * 16)
                        link(nc.vector.tensor_scalar(pool_t[h][:], ms[h][:, 0:1], gs[h][:, 0:1],
                                                     coef[h][:, 0:1], ALU.subtract, ALU.mult))
                    nc.vector.tensor_scalar(coef[h][:, 1:2], gs[h][:, 0:1], coef[h][:, 0:1], -1.0,
                                            ALU.mult, ALU.mult).then_inc(coef_ready[h], 1)

        @block.tensor
        def _(pe):
            pe.wait_ge(gm_loaded, (call + 1) * 16)
            with pe.Fori(0, B) as b:
                for h in range(HALVES):
                    pe.wait_ge(stats_ready[h], before + b + 1)
                    nc.tensor.matmul(psum[:, h, 0:2], lhsT=gm[:], rhs=ms[h][:], start=True, stop=True)\
                        .then_inc(group_ready[h], 1)

        @block.scalar
        def _(act):
            act.wait_ge(border_zero, (call + 1) * 2)
            with act.Fori(0, B) as b:
                for h in range(HALVES):
                    act.wait_ge(var_ready[h], before + b + 1)
                    nc.scalar.activation(std[h][:], var[h][:], ACT.Sqrt).then_inc(std_ready[h], 1)
                    act.wait_ge(coef_ready[h], before + b + 1)
                    act.wait_ge(xn_stored[h], (before + b) * 16)
                    inner = xnp[h][:].rearrange("p (r c) -> p r c", c=PW)[:, PAD:PAD + HH, PAD:PAD + WW]
                    nc.scalar.activation(inner, xt[h][:].rearrange("p (r c) -> p r c", c=WW), ACT.Identity,
                                         bias=coef[h][:, 1:2], scale=coef[h][:, 0:1]).then_inc(norm_done[h], 1)


def group_mean():
    g = np.arange(PART) // (C // 32)
    return (g[:, None] == g[None, :]).astype(np.float32) / np.float32(C // 32)


HEADS0, HD0, K0 = 8, 32, 5
TR, TC = 8, 16
TQ = TR * TC
KR, KC = TR + K0 - 1, TC + K0 - 1
NK = KR * KC
KCH = NK // 2
TILES = WW // TC
BROWS = TR + K0 - 1
BAND0 = TR * WW


def attention_masks():
    qr, qc = np.divmod(np.arange(TQ), TC)
    kr, kc = np.divmod(np.arange(NK), KC)
    near = (np.abs(kr[None] - qr[:, None] - K0 // 2) <= K0 // 2) & (np.abs(kc[None] - qc[:, None] - K0 // 2) <= K0 // 2)
    out = np.zeros((HH // TR, TQ, TILES, NK), np.float32)
    for r in range(HH // TR):
        for c in range(TILES):
            y, x = r * TR + kr - K0 // 2, c * TC + kc - K0 // 2
            inside = (y >= 0) & (y < HH) & (x >= 0) & (x < WW)
            out[r, :, c] = np.where(near & inside[None], 0.0, -1e30)
    return out


def window_attention(nc, xn, x_in, x_out, w_qkv_t, b_qkv, masks, ident_in):
    ctx = ExitStack()
    with ctx:
        sb = lambda n, s, dt=F32: ctx.enter_context(nc.sbuf_tensor(f"a_{n}", s, dt))
        pb = lambda n, s: ctx.enter_context(nc.psum_tensor(f"a_{n}", s, F32))
        sem = lambda n: nc.alloc_semaphore(name=f"a_{n}")
        BUF = 4
        wt = sb("wt", [PART, HALVES, 3 * C])
        bias = sb("bias", [PART, 3 * HALVES])
        wait_taker = sb("wait_taker", [PART, 2])
        ident = sb("ident", [PART, PART])
        xb = [sb(f"xb{u}", [PART, HALVES, BROWS * PW]) for u in range(2)]
        xr = [sb(f"xr{u}", [PART, HALVES, BAND0]) for u in range(2)]
        mk = [sb(f"mk{u}", [TQ, TILES, NK]) for u in range(2)]
        xk = [sb(f"xk{u}", [PART, HALVES, NK]) for u in range(2)]
        qk = [sb(f"qk{u}", [PART, HALVES, TQ + NK]) for u in range(2)]
        vt = [sb(f"vt{u}", [KCH, 2, C]) for u in range(2)]
        ms = [sb(f"ms{i}", [TQ, 2, NK]) for i in range(BUF)]
        pr = [sb(f"pr{i}", [TQ, 2, NK]) for i in range(BUF)]
        nmax = [sb(f"nmax{i}", [TQ, 2]) for i in range(BUF)]
        den = [sb(f"den{u}", [TQ, HEADS0]) for u in range(2)]
        rden = sb("rden", [TQ, HEADS0])
        pt = [sb(f"pt{i}", [KCH, 4, TQ]) for i in range(2)]
        on = [sb(f"on{u}", [TQ, C]) for u in range(2)]
        pqk = pb("pqk", [PART, 2, 512])
        pv = pb("pv", [PART, 512])
        ps = pb("ps", [PART, 2, 512])
        ppt = pb("ppt", [PART, 512])
        po = pb("po", [PART, 512])
        pot = pb("pot", [PART, 512])
        consts_in = sem("consts_in")
        band_in = [sem(f"band_in{u}") for u in range(2)]
        masks_in = [sem(f"masks_in{u}") for u in range(2)]
        rest_in = [sem(f"rest_in{u}") for u in range(2)]
        out_stored = [sem(f"out_stored{u}") for u in range(2)]
        taker_ready = sem("taker_ready")
        area_ready = sem("area_ready")
        qk_projected = sem("qk_projected")
        projected = sem("projected")
        qk_copied = sem("qk_copied")
        v_copied = sem("v_copied")
        scored = sem("scored")
        masked = [sem(f"masked{u}") for u in range(2)]
        max_ready = sem("max_ready")
        exp_done = sem("exp_done")
        turned = sem("turned")
        turned_copied = sem("turned_copied")
        weighted = sem("weighted")
        recip_ready = sem("recip_ready")
        normalised = sem("normalised")
        turned_back = sem("turned_back")
        added = sem("added")

        NT = 2 * TILES
        NP = HEADS0 // 2
        BP = TILES * NP
        PT = NT * NP
        TURNS = HH // TR // 2
        ALL = B * TURNS
        LAG = 2
        block = ctx.enter_context(nc.Block())


        def all_turns(eng, step):
            def turn(n, **end):
                for P in range(PT):
                    step(n, P, **end)
            turn(0, first=True)
            with eng.Fori(1, ALL - 1) as n:
                turn(n)
            turn(ALL - 1, final=True)

        def masked_up_to(eng, n, P):
            band, r = divmod(P, BP)
            eng.wait_ge(masked[band % 2], (n + band // 2) * BP + r + 1)

        @block.sync
        def _(sp):
            sp.dma_start(wt[:], w_qkv_t.rearrange("(h p) o -> p h o", p=PART)).then_inc(consts_in, 16)
            sp.dma_start(bias[:], b_qkv.rearrange("(m p) -> p m", p=PART), allow_slow_non_contiguous=True).then_inc(consts_in, 16)
            sp.dma_start(ident[:], ident_in).then_inc(consts_in, 16)

            def band(t, n, u):
                return t[bass.ds(n // TURNS, 1), :, bass.ds((n % TURNS) * (2 * BAND0) + u * BAND0, BAND0)]\
                    .rearrange("b (h p) n -> p (b h) n", p=PART)

            def load_band(n, u):
                first = (PAD - K0 // 2 + u * TR) * PW
                sp.dma_start(xb[u][:], xn[bass.ds(n // TURNS, 1), :, bass.ds((n % TURNS) * (2 * TR * PW) + first, BROWS * PW)]
                             .rearrange("b (h p) n -> p (b h) n", p=PART)).then_inc(band_in[u], 16)

            def load_masks(n, u):
                sp.dma_start(mk[u][:], masks[bass.ds((n % TURNS) * 2 + u, 1)]
                             .rearrange("r q c k -> (r q) c k")).then_inc(masks_in[u], 16)

            def load_rest(n, u):
                sp.dma_start(xr[u][:], band(x_in, n, u)).then_inc(rest_in[u], 16)

            def store(n, u):
                sp.wait_ge(added, n * NT + (u + 1) * TILES)
                sp.dma_start(band(x_out, n, u), xr[u][:]).then_inc(out_stored[u], 16)

            for u in range(2):
                load_band(0, u)
                load_masks(0, u)
                load_rest(0, u)
            with sp.Fori(1, ALL) as n:
                for u in range(2):
                    sp.wait_ge(area_ready, n * NT)
                    load_band(n, u)
                    sp.wait_ge(masked[u], n * BP)
                    load_masks(n, u)
                for u in range(2):
                    store(n - 1, u)
                    sp.wait_ge(out_stored[u], n * 16)
                    load_rest(n, u)
            for u in range(2):
                store(ALL - 1, u)
            for u in range(2):
                sp.wait_ge(out_stored[u], 16 * ALL)

        @block.gpsimd
        def _(pool):
            nc.gpsimd.memset(wait_taker[:], 0.0).then_inc(taker_ready, 1)
            pool.wait_ge(taker_ready, 1)
            with pool.Fori(0, ALL) as n:
                for t in range(NT):
                    u, c = divmod(t, TILES)
                    if c == 0:
                        pool.wait_ge(band_in[u], n * 16 + 16)
                    pool.wait_ge(projected, n * NT + max(t - 1, 0))
                    pool.wait_ge(area_ready, n * NT + t)
                    nc.gpsimd.tensor_tensor(wait_taker[:, 0:1], wait_taker[:, 1:2], wait_taker[:, 1:2], ALU.add)
                    k0 = PAD - K0 // 2 + c * TC
                    for h in range(HALVES):
                        last = nc.gpsimd.tensor_copy(xk[t % 2][:, h, :].rearrange("p (r c) -> p r c", c=KC),
                                                     xb[u][:, h, :].rearrange("p (r c) -> p r c", c=PW)[:, :, k0:k0 + KC])
                    last.then_inc(area_ready, 1)

        @block.tensor
        def _(pe):
            pe.wait_ge(consts_in, 48)

            def project(n, t, part):
                if part == 0:
                    pe.wait_ge(area_ready, n * NT + t + 1)
                first_tile = t == 0 and isinstance(n, int)
                area = xk[t % 2]
                grid = area[:].rearrange("p h (r c) -> p h r c", c=KC)
                own = grid[:, :, K0 // 2:K0 // 2 + TR, K0 // 2:K0 // 2 + TC]
                m = part % 2
                if part < 2:
                    if not first_tile:
                        pe.wait_ge(qk_copied, (n * NT + t) * 2 - 1 + m)
                    for h in range(HALVES):
                        nc.tensor.matmul(pqk[:, m, 0:TQ].rearrange("p (r c) -> p r c", c=TC),
                                         lhsT=wt[:, h, m * PART:(m + 1) * PART], rhs=own[:, h],
                                         start=h == 0, stop=h == HALVES - 1)
                    for h in range(HALVES):
                        last = nc.tensor.matmul(pqk[:, m, TQ:TQ + NK], lhsT=wt[:, h, C + m * PART:C + (m + 1) * PART],
                                                rhs=area[:, h, :], start=h == 0, stop=h == HALVES - 1)
                    last.then_inc(qk_projected, 1)
                else:
                    if m == 0 and not first_tile:
                        pe.wait_ge(v_copied, n * NT + t)
                    for h in range(HALVES):
                        last = nc.tensor.matmul(pv[0:KCH, m * C:(m + 1) * C],
                                                lhsT=area[:, h, m * KCH:(m + 1) * KCH],
                                                rhs=wt[:, h, 2 * C:3 * C], start=h == 0, stop=h == HALVES - 1)
                    if m == 1:
                        last.then_inc(projected, 1)

            def scores(n, P, first=False):
                t, p = divmod(P, NP)
                if p == 0:
                    pe.wait_ge(qk_copied, (n * NT + t + 1) * 2)
                if P >= 2 or not first:
                    masked_up_to(pe, n, P - 2)
                for e in range(2):
                    s = slice(p * HD0, (p + 1) * HD0)
                    last = nc.tensor.matmul(ps[0:TQ, P % 2, e * NK:(e + 1) * NK], lhsT=qk[t % 2][s, e, 0:TQ],
                                            rhs=qk[t % 2][s, e, TQ:TQ + NK], start=True, stop=True)
                last.then_inc(scored, 1)

            def turned_exps(n, P, first=False):
                pe.wait_ge(exp_done, n * PT + P + 1)
                if P >= 1 or not first:
                    pe.wait_ge(turned_copied, n * PT + P)
                for e in range(2):
                    for j in range(2):
                        k = 2 * e + j
                        last = nc.tensor.transpose(ppt[0:KCH, k * TQ:(k + 1) * TQ],
                                                   pr[P % BUF][:, e, j * KCH:(j + 1) * KCH], ident[:])
                last.then_inc(turned, 1)

            def weigh(n, P, first=False):
                t, p = divmod(P, NP)
                pe.wait_ge(turned_copied, n * PT + P + 1)
                if p == 0:
                    pe.wait_ge(v_copied, n * NT + t + 1)
                    if t or not first:
                        pe.wait_ge(normalised, n * NT + t)
                for e in range(2):
                    s = slice((e * NP + p) * HD0, (e * NP + p + 1) * HD0)
                    for j in range(2):
                        last = nc.tensor.matmul(po[0:TQ, s], lhsT=pt[P % 2][:, 2 * e + j, :],
                                                rhs=vt[t % 2][:, j, s], start=j == 0, stop=j == 1)
                last.then_inc(weighted, 1)

            def back(n, t, first=False):
                pe.wait_ge(normalised, n * NT + t + 1)
                if t or not first:
                    pe.wait_ge(added, n * NT + t)
                for m in range(HALVES):
                    last = nc.tensor.transpose(pot[:, m * TQ:(m + 1) * TQ],
                                               on[t % 2][:, m * PART:(m + 1) * PART], ident[:])
                last.then_inc(turned_back, 1)

            def lagging(n, P, first=False):
                if P >= LAG or not first:
                    if P - LAG < PT:
                        turned_exps(n, P - LAG, first)
                if P >= LAG + 1 or not first:
                    weigh(n, P - LAG - 1, first)
                    if (P - LAG - 2) % NP == NP - 1 and (P >= LAG + 2 + NP - 1 or not first):
                        back(n, (P - LAG - 2) // NP, first)

            def step(n, P, first=False, final=False):
                scores(n, P, first)
                if not (final and P // NP + 1 == NT):
                    project(n, P // NP + 1, P % NP)
                lagging(n, P, first)

            for part in range(4):
                project(0, 0, part)
            all_turns(pe, step)
            for P in range(PT, PT + LAG + 1):
                lagging(ALL - 1, P)
            back(ALL - 1, NT - 1)

        @block.scalar
        def _(act):
            act.wait_ge(consts_in, 48)

            def copy_qk(n, t, m, first=False):
                act.wait_ge(qk_projected, (n * NT + t) * 2 + m + 1)
                if t >= 2 or not first:
                    act.wait_ge(weighted, (n * NT + t - 1) * NP)
                nc.scalar.activation(qk[t % 2][:, m, 0:TQ], pqk[:, m, 0:TQ], ACT.Identity, bias=bias[:, m:m + 1])
                nc.scalar.activation(qk[t % 2][:, m, TQ:TQ + NK], pqk[:, m, TQ:TQ + NK], ACT.Identity,
                                     bias=bias[:, HALVES + m:HALVES + m + 1]).then_inc(qk_copied, 1)

            def copy_v(n, t):
                act.wait_ge(projected, n * NT + t + 1)
                nc.scalar.activation(vt[t % 2][:].rearrange("p j c -> p (j c)"), pv[0:KCH, :], ACT.Copy)\
                    .then_inc(v_copied, 1)

            def step(n, P, first=False, final=False):
                t, p = divmod(P, NP)
                if 1 <= p <= 2 and not (final and t + 1 == NT):
                    copy_qk(n, t + 1, p - 1, first)
                if p == 0 and (t or not first):
                    copy_v(n, t)
                act.wait_ge(max_ready, n * PT + P + 1)
                if P >= BUF or not first:
                    act.wait_ge(turned, n * PT + P - BUF + 1)
                if p == 0 and (t >= 2 or not first):
                    act.wait_ge(recip_ready, n * NT + t - 1)
                for e in range(2):
                    last = nc.scalar.activation(pr[P % BUF][:, e, :], ms[P % BUF][:, e, :], ACT.Exp,
                                                bias=nmax[P % BUF][:, e:e + 1],
                                                accum_out=den[t % 2][:, e * NP + p:e * NP + p + 1])
                last.then_inc(exp_done, 1)

            for m in range(HALVES):
                copy_qk(0, 0, m, first=True)
            copy_v(0, 0)
            all_turns(act, step)

        @block.vector
        def _(dve):
            dve.wait_ge(consts_in, 48)

            def mask(n, P, first):
                t, p = divmod(P, NP)
                u, c = divmod(t, TILES)
                if c == 0 and p == 0:
                    dve.wait_ge(masks_in[u], n * 16 + 16)
                dve.wait_ge(scored, n * PT + P + 1)
                if P >= BUF or not first:
                    dve.wait_ge(exp_done, n * PT + P - BUF + 1)
                nc.vector.tensor_tensor(ms[P % BUF][:], ps[0:TQ, P % 2, 0:2 * NK].rearrange("p (e k) -> p e k", e=2),
                                        mk[u][:, c:c + 1, :].to_broadcast([TQ, 2, NK]), ALU.add).then_inc(masked[u], 1)

            def maximum(n, P):
                masked_up_to(dve, n, P)
                nc.vector.tensor_reduce(nmax[P % BUF][:], ms[P % BUF][:], AX.X, ALU.max, negate=True).then_inc(max_ready, 1)

            def copy_turned(n, P, first):
                dve.wait_ge(turned, n * PT + P + 1)
                if P >= 2 or not first:
                    dve.wait_ge(weighted, n * PT + P - 1)
                nc.vector.tensor_copy(pt[P % 2][:].rearrange("p k q -> p (k q)"), ppt[0:KCH, :]).then_inc(turned_copied, 1)

            def normalise(n, t, first):
                dve.wait_ge(exp_done, (n * NT + t + 1) * NP)
                if t or not first:
                    dve.wait_ge(normalised, n * NT + t)
                nc.vector.reciprocal(rden[:], den[t % 2][:]).then_inc(recip_ready, 1)
                dve.wait_ge(weighted, (n * NT + t + 1) * NP)
                dve.wait_ge(recip_ready, n * NT + t + 1)
                if t >= 2 or not first:
                    dve.wait_ge(turned_back, n * NT + t - 1)
                nc.vector.tensor_tensor(on[t % 2][:].rearrange("p (g d) -> p g d", d=HD0),
                                        po[0:TQ, 0:C].rearrange("p (g d) -> p g d", d=HD0),
                                        rden[:].rearrange("p (g o) -> p g o", o=1).to_broadcast([TQ, HEADS0, HD0]),
                                        ALU.mult).then_inc(normalised, 1)

            def add(n, t):
                band, c = divmod(t, TILES)
                u = band % 2
                dve.wait_ge(turned_back, n * NT + t + 1)
                dve.wait_ge(rest_in[u], (n + band // 2 + 1) * 16)
                for m in range(HALVES):
                    res = xr[u][:, m, :].rearrange("p (r c) -> p r c", c=WW)[:, :, c * TC:(c + 1) * TC]
                    last = nc.vector.scalar_tensor_tensor(
                        res, pot[:, m * TQ:(m + 1) * TQ].rearrange("p (r c) -> p r c", c=TC),
                        bias[:, 2 * HALVES + m:2 * HALVES + m + 1], res, ALU.add, ALU.add)
                last.then_inc(added, 1)

            def finish(n, P, first=False):
                if (P - LAG - 1) % NP == NP - 1 and (P >= LAG + NP or not first):
                    normalise(n, (P - LAG - 1) // NP, first)
                if (P - LAG - 2) % NP == NP - 1 and (P >= LAG + NP + 1 or not first):
                    add(n, (P - LAG - 2) // NP)

            def step(n, P, first=False, final=False):
                mask(n, P, first)
                if P >= LAG or not first:
                    copy_turned(n, P - LAG, first)
                maximum(n, P)
                finish(n, P, first)

            all_turns(dve, step)
            for P in range(PT, PT + LAG + 2):
                if P < PT + LAG:
                    copy_turned(ALL - 1, P - LAG, False)
                finish(ALL - 1, P)


G8 = 8
C3 = 3 * C
GROUPS = C3 // G8
GPX = HH * G8 * WW
TG = PART // G8
CHUNK = 512
CROWS = CHUNK // WW


def qkv_project(nc, xn, qkv, w_t):
    ctx = ExitStack()
    with ctx:
        sb = lambda n, s, dt=F32: ctx.enter_context(nc.sbuf_tensor(f"b_{n}", s, dt))
        sem = lambda n: nc.alloc_semaphore(name=f"b_{n}")
        MT = C3 // PART
        NC = NPX // CHUNK
        wt = sb("wt", [PART, HALVES, C3])
        w_high = sb("w_high", [PART, HALVES, C3], F32R)
        w_low = sb("w_low", [PART, HALVES, C3], F32R)
        xc = [sb(f"xc{v}", [PART, HALVES, CROWS * PW]) for v in range(2)]
        x_high = [sb(f"x_high{u}", [PART, HALVES, NPX], F32R) for u in range(2)]
        x_low = [sb(f"x_low{u}", [PART, HALVES, NPX], F32R) for u in range(2)]
        ot = [sb(f"ot{u}", [PART, NPX]) for u in range(2)]
        pq = ctx.enter_context(nc.psum_tensor("b_pq", [PART, 8, 512], F32))
        w_in = sem("w_in")
        w_high_ready = sem("w_high_ready")
        w_low_ready = sem("w_low_ready")
        chunk_in = [sem(f"chunk_in{v}") for v in range(2)]
        x_high_ready = sem("x_high_ready")
        x_low_ready = sem("x_low_ready")
        product = sem("product")
        copied = [sem("copied_act"), sem("copied_dve")]
        stored = [sem(f"stored{u}") for u in range(2)]
        block = ctx.enter_context(nc.Block())
        TURNS = B // 2
        T = 2 * MT
        SPLIT_AT = [(0, 1), (2, 3), (4, 5), (6, 7), (), ()]

        def all_images(eng, tile):
            with eng.Fori(0, TURNS - 1) as n:
                for t in range(T):
                    tile(n, t // MT, t % MT, True)
            for t in range(T):
                tile(TURNS - 1, t // MT, t % MT, t < MT)

        @block.sync
        def _(sp):
            sp.dma_start(wt[:], w_t.rearrange("(h p) o -> p h o", p=PART)).then_inc(w_in, 16)

            def load(n, u, c):
                if not (isinstance(n, int) and u == 0 and c < 2):
                    sp.wait_ge(x_low_ready, (n * 2 + u) * NC + c - 1)
                first = (PAD + c * CROWS) * PW
                sp.dma_start(xc[c % 2][:], xn[bass.ds(n * 2 + u, 1), :, first:first + CROWS * PW]
                             .rearrange("b (h p) n -> p (b h) n", p=PART)).then_inc(chunk_in[c % 2], 16)

            def tile(n, u, m, more):
                t = u * MT + m
                if more:
                    for c in SPLIT_AT[m]:
                        load(n, u + 1, c)
                for k in range(2):
                    sp.wait_ge(copied[k], (n * T + t + 1) * (NC // 2))
                dst = qkv[bass.ds(n * 2 + u, 1), m * TG:(m + 1) * TG, :].rearrange("b g (r i c) -> i (b g) r c", i=G8, c=WW)
                src = ot[t % 2][:].rearrange("p (r c) -> p r c", c=WW)
                for i in range(G8):
                    sp.dma_start(dst[i], src[i * TG:(i + 1) * TG]).then_inc(stored[t % 2], 16)

            for c in range(NC):
                load(0, 0, c)
            all_images(sp, tile)
            for k in range(2):
                sp.wait_ge(stored[k], TURNS * T // 2 * G8 * 16)

        @block.tensor
        def _(pe):
            pe.wait_ge(w_low_ready, 1)

            def tile(n, u, m, more):
                t = u * MT + m
                for k in range(NC):
                    if m == 0:
                        pe.wait_ge(x_low_ready, (n * 2 + u) * NC + k + 1)
                    pe.wait_ge(copied[k % 2], (n * T + max(t - 1, 0)) * (NC // 2) + (k // 2 + 1 if t else 0))
                    px = slice(k * CHUNK, (k + 1) * CHUNK)
                    for h in range(HALVES):
                        for i, (w, x) in enumerate(((w_high, x_high), (w_high, x_low), (w_low, x_high))):
                            last = nc.tensor.matmul(pq[:, k, :], lhsT=w[:, h, m * PART:(m + 1) * PART], rhs=x[u][:, h, px],
                                                    start=h == 0 and i == 0, stop=h == HALVES - 1 and i == 2)
                    last.then_inc(product, 1)

            all_images(pe, tile)

        def copy_chunks(eng, copy, which, n, t):
            eng.wait_ge(stored[t % 2], (n * (T // 2) + t // 2) * (G8 * 16))
            for k in range(which, NC, 2):
                eng.wait_ge(product, (n * T + t) * NC + k + 1)
                copy(ot[t % 2][:, k * CHUNK:(k + 1) * CHUNK], pq[:, k, :]).then_inc(copied[which], 1)

        def inner(c):
            return xc[c % 2][:].rearrange("p h (r c) -> p h r c", c=PW)[:, :, :, PAD:PAD + WW]

        def part(x, u, c):
            return x[u % 2][:, :, c * CHUNK:(c + 1) * CHUNK].rearrange("p h (r c) -> p h r c", c=WW)

        @block.scalar
        def _(act):
            act.wait_ge(w_in, 16)
            nc.scalar.activation(w_high[:], wt[:], ACT.Copy).then_inc(w_high_ready, 1)

            def split(n, u, c):
                act.wait_ge(chunk_in[c % 2], ((n * 2 + u) * (NC // 2) + c // 2 + 1) * 16)
                if c == 0 and u:
                    act.wait_ge(product, (n * 2 + u - 1) * (MT * NC))
                nc.scalar.activation(part(x_high, u, c), inner(c), ACT.Copy).then_inc(x_high_ready, 1)

            def tile(n, u, m, more):
                copy_chunks(act, lambda o, i: nc.scalar.activation(o, i, ACT.Copy), 0, n, u * MT + m)
                if more:
                    for c in SPLIT_AT[m]:
                        split(n, u + 1, c)

            for c in range(NC):
                split(0, 0, c)
            all_images(act, tile)

        @block.vector
        def _(dve):
            flat = lambda t: t[:].rearrange("p h o -> p (h o)")
            dve.wait_ge(w_high_ready, 1)
            nc.vector.tensor_tensor(flat(w_low), flat(wt), flat(w_high).bitcast(F32), ALU.subtract).then_inc(w_low_ready, 1)

            def split(n, u, c):
                dve.wait_ge(x_high_ready, (n * 2 + u) * NC + c + 1)
                nc.vector.tensor_tensor(part(x_low, u, c), inner(c), part(x_high, u, c).bitcast(F32), ALU.subtract)\
                    .then_inc(x_low_ready, 1)

            def tile(n, u, m, more):
                copy_chunks(dve, nc.vector.tensor_copy, 1, n, u * MT + m)
                if more:
                    for c in SPLIT_AT[m]:
                        split(n, u + 1, c)

            for c in range(NC):
                split(0, 0, c)
            all_images(dve, tile)


def permuted_channels():
    return np.arange(C3).reshape(C3 // PART, TG, G8).transpose(0, 2, 1).reshape(-1)


K1 = 5
BLK = 16
STEP = BLK - K1 + 1
NBLK = (HH - BLK) // STEP + 1
TW = WW + K1 - 1


def grouped_conv(nc, qkv, agg, w_dw, w_pw, row_masks):
    ctx = ExitStack()
    with ctx:
        sb = lambda n, s, dt=F32: ctx.enter_context(nc.sbuf_tensor(f"c_{n}", s, dt))
        sem = lambda n: nc.alloc_semaphore(name=f"c_{n}")
        dw = sb("dw", [PART, GROUPS, K1, K1])
        pw = sb("pw", [PART, GROUPS, G8])
        band = sb("band", [PART, GROUPS, K1, BLK])
        rm = sb("rm", [PART, BLK])
        NB_IN = 2
        xt = [sb(f"xt{u}", [PART, B, NBLK, TW]) for u in range(NB_IN)]
        x_high = [sb(f"x_high{u}", [PART, B, NBLK, TW], F32R) for u in range(2)]
        x_low = [sb(f"x_low{u}", [PART, B, NBLK, TW], F32R) for u in range(2)]
        wm = [sb(f"wm{u}", [PART, K1, BLK, G8]) for u in range(2)]
        w_high = [sb(f"w_high{u}", [PART, K1, BLK, G8], F32R) for u in range(2)]
        w_low = [sb(f"w_low{u}", [PART, K1, BLK, G8], F32R) for u in range(2)]
        ot = [sb(f"ot{u}", [PART, B, NBLK, WW]) for u in range(2)]
        pa = ctx.enter_context(nc.psum_tensor("c_pa", [PART, 2, B, 512], F32))
        consts_in = sem("consts_in")
        border_zero = sem("border_zero")
        band_step = sem("band_step")
        group_in = [sem(f"group_in{u}") for u in range(2)]
        weights_made = sem("weights_made")
        w_high_ready = sem("w_high_ready")
        w_low_ready = sem("w_low_ready")
        x_high_ready = sem("x_high_ready")
        x_low_ready = sem("x_low_ready")
        product = [sem(f"product{u}") for u in range(2)]
        copied = [[sem(f"copied_{k}{u}") for u in range(2)] for k in ("act", "dve")]
        stored = [sem(f"stored{u}") for u in range(2)]
        STORES = B + 2
        TURNS = GROUPS // 2
        block = ctx.enter_context(nc.Block())

        @block.gpsimd
        def _(pool):
            with pool.Fori(0, TURNS) as n:
                for u in range(2):
                    g = n * 2 + u
                    for k in range(2):
                        pool.wait_ge(copied[k][u], (n + 1) * (B // 2))
                    rows = agg[:, bass.ds(g, 1), :].rearrange("b g (r c) -> (g r) b c", c=WW)
                    for b in range(B):
                        dst = agg[b:b + 1, bass.ds(g, 1), 2 * G8 * WW:(2 + NBLK * STEP) * G8 * WW]\
                            .rearrange("b g (k r c) -> (b g r) k c", k=NBLK, c=WW)
                        pool.dma_start(dst, ot[u][2 * G8:(2 + STEP) * G8, b]).then_inc(stored[u], 16)
                    pool.dma_start(rows[0:2 * G8], ot[u][0:2 * G8, :, 0, :]).then_inc(stored[u], 16)
                    pool.dma_start(rows[(HH - 2) * G8:HH * G8], ot[u][(BLK - 2) * G8:BLK * G8, :, NBLK - 1, :])\
                        .then_inc(stored[u], 16)
            for u in range(2):
                pool.wait_ge(stored[u], TURNS * STORES * 16)

        @block.sync
        def _(sp):
            for to, w in ((dw[:].rearrange("p g a b -> p (g a b)"), w_dw), (pw[:].rearrange("p g o -> p (g o)"), w_pw)):
                sp.dma_start(to, bass.AP(tensor=w.tensor, offset=w.offset, ap=[[0, BLK], w.ap[0], w.ap[1]]))\
                    .then_inc(consts_in, 16)
            sp.dma_start(rm[:], row_masks).then_inc(consts_in, 16)
            sp.wait_ge(border_zero, 2)
            with sp.Fori(0, TURNS) as n:
                for u in range(2):
                    g = n * 2 + u
                    sp.wait_ge(x_low_ready, n * 2)
                    for b in range(B):
                        one = qkv[b:b + 1, bass.ds(g, 1), :]
                        src = bass.AP(tensor=one.tensor, offset=one.offset,
                                      ap=[[WW, PART], [STEP * G8 * WW, NBLK], [1, WW]])
                        sp.dma_start(xt[u][:, b, :, K1 // 2:K1 // 2 + WW], src).then_inc(group_in[u], 16)

        @block.tensor
        def _(pe):
            with pe.Fori(0, TURNS) as n:
                for u in range(2):
                    g = n * 2 + u
                    pe.wait_ge(x_low_ready, g + 1)
                    pe.wait_ge(w_low_ready, g + 1)
                    for b in range(B):
                        pe.wait_ge(copied[b % 2][u], n * (B // 2))
                        for dx in range(K1):
                            for i, (w, x) in enumerate(((w_high, x_high), (w_high, x_low), (w_low, x_high))):
                                last = nc.tensor.matmul(pa[:, u, b, 0:NBLK * WW].rearrange("p (k c) -> p k c", c=WW),
                                                        lhsT=w[u][:, dx].rearrange("p y o -> p (y o)"),
                                                        rhs=x[u][:, b, :, dx:dx + WW],
                                                        start=dx == 0 and i == 0, stop=dx == K1 - 1 and i == 2)
                        last.then_inc(product[u], 1)

        def all_groups(eng, prepare, copy_out):
            prepare(0, 0)
            with eng.Fori(0, TURNS - 1) as n:
                prepare(n, 1)
                copy_out(n, 0)
                prepare(n + 1, 0)
                copy_out(n, 1)
            prepare(TURNS - 1, 1)
            copy_out(TURNS - 1, 0)
            copy_out(TURNS - 1, 1)

        def copy_products(eng, copy, which, n, u):
            eng.wait_ge(stored[u], n * (STORES * 16))
            for b in range(which, B, 2):
                eng.wait_ge(product[u], n * B + b + 1)
                copy(ot[u][:, b].rearrange("p k c -> p (k c)"), pa[:, u, b, 0:NBLK * WW]).then_inc(copied[which][u], 1)

        @block.scalar
        def _(act):
            def prepare(n, u):
                g = n * 2 + u
                act.wait_ge(group_in[u], (n + 1) * (B * 16))
                act.wait_ge(product[u], n * B)
                nc.scalar.activation(x_high[u][:], xt[u][:], ACT.Copy).then_inc(x_high_ready, 1)
                act.wait_ge(weights_made, g + 1)
                nc.scalar.activation(w_high[u][:], wm[u][:], ACT.Copy).then_inc(w_high_ready, 1)

            all_groups(act, prepare,
                       lambda n, u: copy_products(act, lambda o, i: nc.scalar.activation(o, i, ACT.Copy), 0, n, u))

        @block.vector
        def _(dve):
            for u in range(2):
                nc.vector.memset(xt[u][:], 0.0).then_inc(border_zero, 1)
            dve.wait_ge(consts_in, 48)
            nc.vector.memset(band[:], 0.0).then_inc(band_step, 1)
            dve.wait_ge(band_step, 1)
            done = 1
            for dy in range(K1):
                for y in range(BLK):
                    j = y + dy - K1 // 2
                    if 0 <= j < BLK:
                        to = band[:, :, :, y]
                        nc.vector.scalar_tensor_tensor(to, dw[:, :, dy, :], rm[:, j:j + 1], to, ALU.mult, ALU.add)\
                            .then_inc(band_step, 1)
                        done += 1
                dve.wait_ge(band_step, done)

            def prepare(n, u):
                g = n * 2 + u
                dve.wait_ge(w_low_ready, n * 2)
                nc.vector.tensor_tensor(
                    wm[u][:].rearrange("p d y o -> p (d y) o"),
                    band[:, bass.ds(g, 1)].rearrange("p g d (y o) -> p (g d y) o", o=1).to_broadcast([PART, K1 * BLK, G8]),
                    pw[:, bass.ds(g, 1), :].to_broadcast([PART, K1 * BLK, G8]), ALU.mult).then_inc(weights_made, 1)
                dve.wait_ge(product[u], n * B)
                flat = lambda t: t[:].rearrange("p b k c -> p (b k c)")
                dve.wait_ge(x_high_ready, g + 1)
                nc.vector.tensor_tensor(flat(x_low[u]), flat(xt[u]), flat(x_high[u]).bitcast(F32), ALU.subtract)\
                    .then_inc(x_low_ready, 1)
                flat = lambda t: t[:].rearrange("p d y o -> p (d y o)")
                dve.wait_ge(w_high_ready, g + 1)
                nc.vector.tensor_tensor(flat(w_low[u]), flat(wm[u]), flat(w_high[u]).bitcast(F32), ALU.subtract)\
                    .then_inc(w_low_ready, 1)

            all_groups(dve, prepare, lambda n, u: copy_products(dve, nc.vector.tensor_copy, 1, n, u))


def row_masks():
    return (np.arange(PART)[:, None] // G8 == np.arange(BLK)[None]).astype(np.float32)


HEADS1 = C // G8
SCALES = 2
ST = SCALES * HEADS1 // TG
EPS1 = 1e-15


def linear_attention(nc, scales, x_in, x_out, w_proj_t, head_mask, ident_in):
    ctx = ExitStack()
    with ctx:
        sb = lambda n, s, dt=F32: ctx.enter_context(nc.sbuf_tensor(f"d_{n}", s, dt))
        sem = lambda n: nc.alloc_semaphore(name=f"d_{n}")
        TPS = ST // SCALES
        NCH = NPX // PART
        PC = 512
        NPC = NPX // PC
        SUB = PC // PART
        NI = NPC * ST
        DEEP = 3
        kt = [sb(f"kt{u}", [PART, NPX]) for u in range(2)]
        vt = [sb(f"vt{u}", [PART, NPX]) for u in range(2)]
        qt = sb("qt", [PART, ST, NPX])
        kvp = [sb(f"kvp{u}", [PART, 2, 2 * PART + 1]) for u in range(DEEP)]
        kvm = sb("kvm", [PART, ST, PART])
        ksm = sb("ksm", [PART, ST, TG])
        wp = sb("wp", [PART, ST, C])
        hm = sb("hm", [PART, PART])
        ident = sb("ident", [PART, PART])
        den = [sb(f"den{u}", [PART, SUB, TG]) for u in range(2)]
        attp = [sb(f"attp{u}", [PART, SUB, PART]) for u in range(2)]
        att = [sb(f"att{u}", [PART, PC]) for u in range(2)]
        xr = [sb(f"xr{u}", [PART, HALVES, PC]) for u in range(2)]
        banks = ctx.enter_context(nc.psum_tensor("d_banks", [PART, 8, 512], F32))
        turned_bank = lambda j, v: banks[:, 2 * (j % DEEP) + v, :]
        pkv = banks[:, 2 * DEEP, :]
        numer_bank = lambda i: banks[:, i % 2, :]
        denom_bank = lambda i: banks[:, 2 + i % 2, :]
        att_bank = lambda i: banks[:, 4 + i % 2, :]
        pp = banks[:, 6:8, :]
        wait_taker = sb("wait_taker", [PART, 2])
        taken = sem("taken")
        consts_in = sem("consts_in")
        ones_ready = sem("ones_ready")
        kv_in = [sem(f"kv_in{u}") for u in range(2)]
        q_in = [sem(f"q_in{v}") for v in range(2)]
        q_positive = sem("q_positive")
        turned = sem("turned")
        keys_copied = sem("keys_copied")
        values_copied = sem("values_copied")
        summed = sem("summed")
        sums_masked = sem("sums_masked")
        ratio_parts = [sem(f"ratio_parts{v}") for v in range(2)]
        den_steps = sem("den_steps")
        attended = sem("attended")
        turned_back = sem("turned_back")
        att_copied = sem("att_copied")
        projected = sem("projected")
        added = sem("added")
        x_loaded = [sem(f"x_loaded{u}") for u in range(2)]
        stored = [sem(f"stored{u}") for u in range(2)]
        block = ctx.enter_context(nc.Block())
        PAIRS = NCH // 2
        NPR = ST * PAIRS

        def heads_of(b, st, kind):
            s, t = divmod(st, TPS)
            first = 3 * TG * t
            return scales[s][bass.ds(b, 1), first:first + 3 * TG, :]\
                .rearrange("b (h k) (r i c) -> k i (b h) r c", k=3, i=G8, c=WW)[kind]

        def load_queries(eng, b, v):
            half = slice(v * (HH // 2), (v + 1) * (HH // 2))
            eng.wait_ge(ratio_parts[v], b * (NI // 2))
            for t in range(ST):
                for i in reversed(range(G8)):
                    eng.dma_start(qt[i * TG:(i + 1) * TG, t].rearrange("p (r c) -> p r c", c=WW)[:, half],
                                  heads_of(b, t, 0)[i][:, half]).then_inc(q_in[v], 16)

        @block.sync
        def _(sp):
            sp.dma_start(wp[:], w_proj_t.rearrange("(s p) o -> p s o", p=PART)).then_inc(consts_in, 16)
            sp.dma_start(hm[:], head_mask).then_inc(consts_in, 16)
            sp.dma_start(ident[:], ident_in).then_inc(consts_in, 16)
            with sp.Fori(0, B) as b:
                for st in range(ST):
                    u = st % 2
                    sp.wait_ge(turned, (b * ST + max(st - 1, 0)) * PAIRS)
                    for i in range(G8):
                        for kind, buf in ((1, kt), (2, vt)):
                            sp.dma_start(buf[u][i * TG:(i + 1) * TG].rearrange("p (r c) -> p r c", c=WW),
                                         heads_of(b, st, kind)[i]).then_inc(kv_in[u], 16)
                    if st == 1:
                        load_queries(sp, b, 0)

        @block.gpsimd
        def _(pool):
            nc.gpsimd.memset(wait_taker[:], 0.0).then_inc(taken, 1)
            with pool.Fori(0, B) as b:
                for c in range(NPC + 1):
                    if c < NPC:
                        pool.wait_ge(stored[c % 2], (b * (NPC // 2) + c // 2) * 16)
                        pool.dma_start(xr[c % 2][:], x_in[bass.ds(b, 1), :, c * PC:(c + 1) * PC]
                                       .rearrange("b (h p) n -> p (b h) n", p=PART)).then_inc(x_loaded[c % 2], 16)
                    if c > 0:
                        pool.wait_ge(taken, b * NPC + c)
                        pool.wait_ge(added, (b * NPC + c) * HALVES)
                        nc.gpsimd.tensor_tensor(wait_taker[:, 0:1], wait_taker[:, 1:2], wait_taker[:, 1:2], ALU.add)\
                            .then_inc(taken, 1)
                        pool.dma_start(x_out[bass.ds(b, 1), :, (c - 1) * PC:c * PC]
                                       .rearrange("b (h p) n -> p (b h) n", p=PART), xr[(c - 1) % 2][:])\
                            .then_inc(stored[(c - 1) % 2], 16)
            for u in range(2):
                pool.wait_ge(stored[u], B * (NPC // 2) * 16)

        @block.tensor
        def _(pe):
            pe.wait_ge(consts_in, 48)
            pe.wait_ge(ones_ready, DEEP)
            with pe.Fori(0, B) as b:
                def turn(j):
                    st, k = divmod(j, PAIRS)
                    if k == 0:
                        pe.wait_ge(kv_in[st % 2], (b * (ST // 2) + st // 2 + 1) * (2 * G8 * 16))
                    if j == 0:
                        pe.wait_ge(attended, b * NI)
                        pe.wait_ge(att_copied, b * NI)
                    if j >= DEEP:
                        pe.wait_ge(keys_copied, b * NPR + j - DEEP + 1)
                        pe.wait_ge(values_copied, b * NPR + j - DEEP + 1)
                    for e in range(2):
                        px = slice((2 * k + e) * PART, (2 * k + e + 1) * PART)
                        for v, buf in enumerate((kt, vt)):
                            last = nc.tensor.transpose(turned_bank(j, v)[:, e * PART:(e + 1) * PART], buf[st % 2][:, px], ident[:])
                    last.then_inc(turned, 1)

                def accumulate(j):
                    st, k = divmod(j, PAIRS)
                    pe.wait_ge(keys_copied, b * NPR + j + 1)
                    pe.wait_ge(values_copied, b * NPR + j + 1)
                    if j == 0:
                        pe.wait_ge(added, b * (NPC * HALVES))
                    if k == 0:
                        pe.wait_ge(sums_masked, (b * ST + st) * 2)
                    for e in range(2):
                        last = nc.tensor.matmul(pkv[:, 0:PART + 1], lhsT=kvp[j % DEEP][:, e, 0:PART],
                                                rhs=kvp[j % DEEP][:, e, PART:2 * PART + 1],
                                                start=k == 0 and e == 0, stop=k == PAIRS - 1 and e == 1)
                    last.then_inc(summed, 1)

                for j in range(NPR + DEEP - 1):
                    if j < NPR:
                        turn(j)
                    if j >= DEEP - 1:
                        accumulate(j - DEEP + 1)

                def ratio(i):
                    c, st = divmod(i, ST)
                    if c % (NPC // 2) == 0:
                        pe.wait_ge(q_positive, b * (2 * ST) + (2 * c // NPC) * ST + st + 1)
                    if c == 0:
                        pe.wait_ge(sums_masked, (b * ST + st + 1) * 2)
                    if i >= 2:
                        pe.wait_ge(attended, b * NI + i - 1)
                    else:
                        pe.wait_ge(keys_copied, (b + 1) * NPR)
                        pe.wait_ge(values_copied, (b + 1) * NPR)
                    for s in range(SUB):
                        queries = qt[:, st, c * PC + s * PART:c * PC + (s + 1) * PART]
                        nc.tensor.matmul(denom_bank(i)[:, s * TG:(s + 1) * TG], lhsT=queries, rhs=ksm[:, st],
                                         start=True, stop=True)
                        last = nc.tensor.matmul(numer_bank(i)[:, s * PART:(s + 1) * PART], lhsT=queries, rhs=kvm[:, st],
                                                start=True, stop=True)
                    last.then_inc(ratio_parts[2 * i // NI], 1)

                def back(i):
                    pe.wait_ge(attended, b * NI + i + 1)
                    if i >= 2:
                        pe.wait_ge(att_copied, b * NI + i - 1)
                    for s in range(SUB):
                        last = nc.tensor.transpose(att_bank(i)[:, s * PART:(s + 1) * PART], attp[i % 2][:, s], ident[:])
                    last.then_inc(turned_back, 1)

                def project(i):
                    c, st = divmod(i, ST)
                    pe.wait_ge(att_copied, b * NI + i + 1)
                    if st == 0:
                        pe.wait_ge(added, (b * NPC + c) * HALVES)
                    for m in range(HALVES):
                        last = nc.tensor.matmul(pp[:, m, :], lhsT=wp[:, st, m * PART:(m + 1) * PART],
                                                rhs=att[i % 2][:], start=st == 0, stop=st == ST - 1)
                    last.then_inc(projected, 1)

                for i in range(NI + 2):
                    if i < NI:
                        ratio(i)
                    if i >= 2:
                        project(i - 2)
                    if 1 <= i <= NI:
                        back(i - 1)

        @block.scalar
        def _(act):
            with act.Fori(0, B) as b:
                load_queries(act, b, 1)
                for j in range(NPR):
                    act.wait_ge(turned, b * NPR + j + 1)
                    if j >= DEEP:
                        act.wait_ge(summed, b * NPR + j - DEEP + 1)
                    nc.scalar.activation(kvp[j % DEEP][:, :, 0:PART],
                                         turned_bank(j, 0)[:, 0:2 * PART].rearrange("p (e k) -> p e k", e=2), ACT.Relu)\
                        .then_inc(keys_copied, 1)
                    if j >= NPR // 2 and j % (NPR // 16) == 0:
                        v, st = divmod((j - NPR // 2) // (NPR // 16), ST)
                        act.wait_ge(q_in[v], (b + 1) * (ST * G8 * 16))
                        part = slice(v * (NPX // 2), (v + 1) * (NPX // 2))
                        nc.scalar.activation(qt[:, st, part], qt[:, st, part], ACT.Relu).then_inc(q_positive, 1)
                for i in range(NI):
                    act.wait_ge(turned_back, b * NI + i + 1)
                    if i >= 2:
                        act.wait_ge(projected, b * NI + i - 1)
                    nc.scalar.activation(att[i % 2][:], att_bank(i), ACT.Copy).then_inc(att_copied, 1)

        @block.vector
        def _(dve):
            for u in range(DEEP):
                nc.vector.memset(kvp[u][:, :, 2 * PART:2 * PART + 1], 1.0).then_inc(ones_ready, 1)
            dve.wait_ge(consts_in, 48)
            with dve.Fori(0, B) as b:
                def mask_sums(st):
                    dve.wait_ge(summed, (b * ST + st + 1) * PAIRS)
                    nc.vector.tensor_tensor(kvm[:, st], pkv[:, 0:PART], hm[:], ALU.mult).then_inc(sums_masked, 1)
                    nc.vector.tensor_scalar(ksm[:, st], hm[:, 0:TG], pkv[:, PART:PART + 1], None, ALU.mult)\
                        .then_inc(sums_masked, 1)

                for j in range(NPR):
                    dve.wait_ge(turned, b * NPR + j + 1)
                    if j >= DEEP:
                        dve.wait_ge(summed, b * NPR + j - DEEP + 1)
                    nc.vector.tensor_copy(kvp[j % DEEP][:, :, PART:2 * PART],
                                          turned_bank(j, 1)[:, 0:2 * PART].rearrange("p (e k) -> p e k", e=2))\
                        .then_inc(values_copied, 1)
                    if j >= PAIRS and j % PAIRS == DEEP - 2:
                        mask_sums(j // PAIRS - 1)
                mask_sums(ST - 1)

                def add(c):
                    dve.wait_ge(projected, (b * NPC + c + 1) * ST)
                    dve.wait_ge(x_loaded[c % 2], (b * (NPC // 2) + c // 2 + 1) * 16)
                    for m in range(HALVES):
                        nc.vector.tensor_tensor(xr[c % 2][:, m, :], pp[:, m, :], xr[c % 2][:, m, :], ALU.add).then_inc(added, 1)

                for i in range(NI):
                    dve.wait_ge(ratio_parts[2 * i // NI], b * (NI // 2) + i % (NI // 2) + 1)
                    if i >= 2:
                        dve.wait_ge(attended, b * NI + i - 1)
                    nc.vector.tensor_scalar(den[i % 2][:].rearrange("p s g -> p (s g)"), denom_bank(i)[:, 0:SUB * TG],
                                            EPS1, None, ALU.add).then_inc(den_steps, 1)
                    dve.wait_ge(den_steps, (b * NI + i) * 2 + 1)
                    nc.vector.reciprocal(den[i % 2][:], den[i % 2][:]).then_inc(den_steps, 1)
                    dve.wait_ge(den_steps, (b * NI + i) * 2 + 2)
                    if i >= 2:
                        dve.wait_ge(turned_back, b * NI + i - 1)
                    nc.vector.tensor_tensor(attp[i % 2][:].rearrange("p s (i g) -> p s i g", g=TG),
                                            numer_bank(i).rearrange("p (s i g) -> p s i g", s=SUB, g=TG),
                                            den[i % 2][:].rearrange("p s (o g) -> p s o g", o=1)
                                            .to_broadcast([PART, SUB, G8, TG]), ALU.mult).then_inc(attended, 1)
                    if i >= 2 and (i - 2) % ST == ST - 1:
                        add((i - 2) // ST)
                add(NPC - 1)


def head_mask():
    h = np.arange(PART) % TG
    return (h[:, None] == h[None]).astype(np.float32)


def head_channels():
    return np.arange(ST * PART).reshape(ST, TG, G8).transpose(0, 2, 1).reshape(-1)


K2 = 7
R2 = 16
BPX = R2 * WW
HR = R2 + K2 - 1
HPX = HR * PW
NCK = BPX // PART
SPLIT = ((0, 3), (3, 2), (5, 2))
PER_O = len(SPLIT)
INNER = max(n for _, n in SPLIT)
GROUPS2 = [(o, i, n) for o in range(K2) for i, n in SPLIT]
NG2 = len(GROUPS2)
ON_POOL = (4, 10, 16)


def channel_attention(nc, xn, x_in, x_out, w_t, rel, ident_in):
    ctx = ExitStack()
    with ctx:
        sb = lambda n, s, dt=F32: ctx.enter_context(nc.sbuf_tensor(f"e_{n}", s, dt))
        pb = lambda n, s: ctx.enter_context(nc.psum_tensor(f"e_{n}", s, F32))
        sem = lambda n: nc.alloc_semaphore(name=f"e_{n}")
        NSE, NEV = 6, 2
        POOL_AHEAD = 3
        wt = sb("wt", [PART, 3, HALVES, C])
        rl = sb("rl", [PART, HALVES, K2])
        ident = sb("ident", [PART, PART])
        xb = sb("xb", [PART, HALVES, HPX])
        q = [sb(f"q{u}", [PART, BPX]) for u in range(2)]
        k = [sb(f"k{u}", [PART, HPX]) for u in range(2)]
        v = [sb(f"v{u}", [PART, HPX]) for u in range(2)]
        kr = [sb(f"kr{u}", [PART, HPX]) for u in range(2)]
        m2 = sb("m2", [PART, HPX])
        m4 = sb("m4", [PART, HPX])
        ext = [sb(f"ext{i}", [PART, BPX]) for i in range(2)]
        top = [sb(f"top{u}", [PART, BPX]) for u in range(2)]
        se = [sb(f"se{i}", [PART, INNER, BPX]) for i in range(NSE)]
        ev = [sb(f"ev{i}", [PART, INNER, BPX]) for i in range(NEV)]
        es = sb("es", [PART, BPX])
        rs = sb("rs", [PART, BPX])
        ws = sb("ws", [PART, BPX])
        xr = [sb(f"xr{u}", [PART, BPX]) for u in range(2)]
        pj = pb("pj", [PART, 2, 512])
        pe_sum = pb("pe_sum", [PART, NCK, PART])
        pv_sum = pb("pv_sum", [PART, NCK, PART])
        pback = pb("pback", [PART, 2, 512])
        consts_in = sem("consts_in")
        band_in = sem("band_in")
        rest_in = [sem(f"rest_in{u}") for u in range(2)]
        stored = [sem(f"stored{u}") for u in range(2)]
        projected = sem("projected")
        proj_copied = sem("proj_copied")
        rel_added = sem("rel_added")
        ext_step = sem("ext_step")
        top_products = sem("top_products")
        top_parts = sem("top_parts")
        top_ready = sem("top_ready")
        multiplied = sem("multiplied")
        pool_multiplied = sem("pool_multiplied")
        shifted = sem("shifted")
        exp_done = sem("exp_done")
        weighted = sem("weighted")
        e_summed = sem("e_summed")
        v_summed = sem("v_summed")
        e_taken = sem("e_taken")
        v_taken = sem("v_taken")
        near_steps = sem("near_steps")
        checked = sem("checked")
        inverted = sem("inverted")
        divided = sem("divided")
        turned_back = sem("turned_back")
        added = sem("added")
        RB = HH // R2
        NT = B * RB
        KCH2 = HPX // 4
        PROJ = [(1, i * KCH2, KCH2) for i in range(4)] + [(0, i * 512, 512) for i in range(BPX // 512)] \
            + [(2, i * KCH2, KCH2) for i in range(4)]
        NPJ = len(PROJ)
        NKEYS = 4
        PROJ_AT = [(0, 1), (2, 3)] + [(c,) for c in range(NKEYS, NPJ)]
        EXT = 3 + K2
        TOP_EARLY = 1
        ADD_AT = 13
        V_LAG = 1
        DIVIDE_AT = 5
        BACK_AT = 8
        EXT_FROM, EXT_TO = 6, 18
        EXT_GROUP = [EXT_FROM + s * (EXT_TO - EXT_FROM) // (2 * EXT) for s in range(2 * EXT)]
        block = ctx.enter_context(nc.Block())

        def count(n, h, per, more):
            return n * (HALVES * per) + (h * per + more)

        def window(t, h, o, i, n):
            dy, dx = (o, i) if h == 0 else (i, o)
            step = 1 if h == 0 else PW
            a = t[:, dy * PW + dx:dy * PW + dx + 1]
            return bass.AP(tensor=a.tensor, offset=a.offset, ap=[a.ap[0], [step, n], [PW, R2], [1, WW]])

        def flat(t, n):
            return t[:, 0:n].rearrange("p i (r c) -> p i r c", c=WW)

        def repeat(t, n):
            return t[:].rearrange("p (i r c) -> p i r c", i=1, c=WW).to_broadcast([PART, n, R2, WW])

        def scores(h, g):
            return se[(h * NG2 + g) % NSE]

        def keys_plus_rel(h, o):
            return kr[(h * K2 + o) % 2]

        def score_products(engine, h, g):
            o, i, taps = GROUPS2[g]
            return engine.tensor_tensor(flat(scores(h, g), taps), window(keys_plus_rel(h, o), h % 2, o, i, taps),
                                        repeat(q[h % 2], taps), ALU.mult)

        def all_half_bands(eng, half_band):
            half_band(0, 0, first=True)
            with eng.Fori(0, NT - 1) as n:
                half_band(n, 1)
                half_band(n, 2)
            half_band(NT - 1, 1, final=True)

        @block.sync
        def _(sp):
            for w in range(3):
                sp.dma_start(wt[:, w], w_t[w].rearrange("(h p) o -> p h o", p=PART)).then_inc(consts_in, 16)
            sp.dma_start(rl[:], rel.rearrange("(h p) k -> p h k", p=PART)).then_inc(consts_in, 16)
            sp.dma_start(ident[:], ident_in).then_inc(consts_in, 16)

            def band(t, n, h):
                return t[bass.ds(n // RB, 1), h * PART:(h + 1) * PART, bass.ds((n % RB) * BPX, BPX)]\
                    .rearrange("b p n -> (b p) n")

            def load_band(n):
                sp.dma_start(xb[:], xn[bass.ds(n // RB, 1), :, bass.ds((n % RB) * (R2 * PW), HPX)]
                             .rearrange("b (h p) n -> p (b h) n", p=PART)).then_inc(band_in, 16)

            def load_rest(n, h):
                sp.dma_start(xr[h][:], band(x_in, n, h)).then_inc(rest_in[h], 16)

            def store(n, h):
                sp.wait_ge(added, count(n, h, 2, 2))
                sp.dma_start(band(x_out, n, h), xr[h][:]).then_inc(stored[h], 16)

            def turn(n, final=False):
                sp.wait_ge(stored[0], n * 16)
                load_rest(n, 0)
                store(n - 1, 1)
                sp.wait_ge(stored[1], n * 16)
                load_rest(n, 1)
                if not final:
                    sp.wait_ge(projected, count(n, 2, NPJ, 0))
                    load_band(n + 1)
                store(n, 0)

            load_band(0)
            load_rest(0, 0)
            load_rest(0, 1)
            sp.wait_ge(projected, 2 * NPJ)
            load_band(1)
            store(0, 0)
            with sp.Fori(1, NT - 1) as n:
                turn(n)
            turn(NT - 1, final=True)
            store(NT - 1, 1)
            for h in range(HALVES):
                sp.wait_ge(stored[h], NT * 16)

        @block.tensor
        def _(pe):
            pe.wait_ge(consts_in, 80)

            def project(n, h, chunks):
                for c in chunks:
                    w, first, size = PROJ[c]
                    if h % 2 == 0 and c == 0:
                        pe.wait_ge(band_in, (n + h // 2 + 1) * 16)
                    if h or c >= 2:
                        pe.wait_ge(proj_copied, count(n, h, NPJ, c - 1))
                    for g in range(HALVES):
                        if w == 0:
                            rows = xb[:, g].rearrange("p (r c) -> p r c", c=PW)
                            first_row = PAD + first // WW
                            rhs = rows[:, first_row:first_row + size // WW, PAD:PAD + WW]
                            out = pj[:, c % 2, 0:size].rearrange("p (r c) -> p r c", c=WW)
                        else:
                            rhs, out = xb[:, g, first:first + size], pj[:, c % 2, 0:size]
                        last = nc.tensor.matmul(out, lhsT=wt[:, w, g, (h % 2) * PART:(h % 2 + 1) * PART], rhs=rhs,
                                                start=g == 0, stop=g == HALVES - 1)
                    last.then_inc(projected, 1)

            def add_up(g, src, acc):
                for e in range(GROUPS2[g][2]):
                    for c in range(NCK):
                        last = nc.tensor.matmul(acc[:, c, :], lhsT=src[:, e, c * PART:(c + 1) * PART], rhs=ident[:],
                                                is_transpose=True, start=g == 0 and e == 0 and c % 4 == 0,
                                                stop=g == NG2 - 1 and e == GROUPS2[g][2] - 1, skip_group_check=True)
                return last

            def sum_exponentials(n, h, g):
                pe.wait_ge(exp_done, count(n, h, NG2, g + 1))
                add_up(g, scores(h, g), pe_sum).then_inc(e_summed, 1)

            def sum_weighted(n, h, g):
                pe.wait_ge(weighted, count(n, h, NG2, g + 1))
                add_up(g, ev[(h * NG2 + g) % NEV], pv_sum).then_inc(v_summed, 1)

            def back(n, h):
                pe.wait_ge(divided, count(n, h, 1, 1))
                if h:
                    pe.wait_ge(added, count(n, h, 2, 0))
                for c in range(NCK):
                    last = nc.tensor.transpose(pback[:, c // 4, (c % 4) * PART:(c % 4 + 1) * PART],
                                               es[:, c * PART:(c + 1) * PART], ident[:])
                last.then_inc(turned_back, 1)

            def half_band(n, h, first=False, final=False):
                for g in range(NG2):
                    if g < len(PROJ_AT) and not final:
                        project(n, h + 1, PROJ_AT[g])
                    if g == 0 and not first:
                        pe.wait_ge(e_taken, count(n, h, 1, 0))
                    sum_exponentials(n, h, g)
                    if g == V_LAG and not first:
                        pe.wait_ge(v_taken, count(n, h, 1, 0))
                    if g >= V_LAG:
                        sum_weighted(n, h, g - V_LAG)
                    elif not first:
                        sum_weighted(n, h - 1, NG2 + g - V_LAG)
                    if g == BACK_AT and not first:
                        back(n, h - 1)

            project(0, 0, range(NPJ))
            all_half_bands(pe, half_band)
            for g in range(NG2 - V_LAG, NG2):
                sum_weighted(NT - 1, 1, g)
            back(NT - 1, 1)

        @block.scalar
        def _(act):
            act.wait_ge(consts_in, 80)

            def copy_projection(n, h, chunks):
                for c in chunks:
                    w, first, size = PROJ[c]
                    if h and c == 0:
                        act.wait_ge(shifted, count(n, h - 1, NG2, 0))
                    if h and w == 2 and first == 0:
                        act.wait_ge(weighted, count(n, h - 1, NG2, 0))
                    act.wait_ge(projected, count(n, h, NPJ, c + 1))
                    nc.scalar.activation((q, k, v)[w][h % 2][:, first:first + size], pj[:, c % 2, 0:size], ACT.Copy)\
                        .then_inc(proj_copied, 1)

            def add_rel(n, h, o):
                if h or o >= 2:
                    act.wait_ge(shifted, count(n, h, NG2, PER_O * (o - 1)))
                act.wait_ge(proj_copied, count(n, h, NPJ, NKEYS))
                nc.scalar.activation(keys_plus_rel(h, o)[:], k[h % 2][:], ACT.Identity, bias=rl[:, h % 2, o:o + 1])\
                    .then_inc(rel_added, 1)

            def take_e_sums(n, h):
                act.wait_ge(e_summed, count(n, h, NG2, NG2))
                if h:
                    act.wait_ge(turned_back, count(n, h, 1, 0))
                nc.scalar.activation(es[:], pe_sum[:].rearrange("p c k -> p (c k)"), ACT.Copy).then_inc(e_taken, 1)

            def nearly_invert(n, h):
                act.wait_ge(e_taken, count(n, h, 1, 1))
                nc.scalar.activation(rs[:], es[:], ACT.Ln).then_inc(near_steps, 1)
                act.wait_ge(near_steps, count(n, h, 2, 1))
                nc.scalar.activation(rs[:], rs[:], ACT.Exp, scale=-1.0).then_inc(near_steps, 1)

            def take_v_sums(n, h):
                act.wait_ge(v_summed, count(n, h, NG2, NG2))
                if h:
                    act.wait_ge(divided, count(n, h, 1, 0))
                nc.scalar.activation(ws[:], pv_sum[:].rearrange("p c k -> p (c k)"), ACT.Copy).then_inc(v_taken, 1)

            def half_band(n, h, first=False, final=False):
                for g in range(NG2):
                    taps = GROUPS2[g][2]
                    act.wait_ge(shifted, count(n, h, NG2, g + 1))
                    nc.scalar.activation(scores(h, g)[:, 0:taps], scores(h, g)[:, 0:taps], ACT.Exp).then_inc(exp_done, 1)
                    if g == 0 and not first:
                        take_e_sums(n, h - 1)
                        nearly_invert(n, h - 1)
                    if g == V_LAG and not first:
                        take_v_sums(n, h - 1)
                    if g % PER_O == PER_O - 1:
                        next_h, o = divmod(g // PER_O + 2, K2)
                        if next_h == 0 or not final:
                            add_rel(n, h + next_h, o)
                    if 1 <= g <= len(PROJ_AT) and not final:
                        copy_projection(n, h + 1, PROJ_AT[g - 1])

            copy_projection(0, 0, range(NPJ))
            add_rel(0, 0, 0)
            add_rel(0, 0, 1)
            all_half_bands(act, half_band)
            take_e_sums(NT - 1, 1)
            nearly_invert(NT - 1, 1)
            take_v_sums(NT - 1, 1)

        @block.gpsimd
        def _(pool):
            def top_product(n, h, i):
                pool.wait_ge(top_parts, count(n, h, 2, i + 1))
                pool.wait_ge(proj_copied, count(n, h, NPJ, NKEYS + BPX // 512))
                nc.gpsimd.tensor_tensor(ext[i][:], ext[i][:], q[h % 2][:], ALU.mult).then_inc(top_products, 1)

            def weigh(n, h, g):
                o, i, taps = GROUPS2[g]
                pool.wait_ge(exp_done, count(n, h, NG2, g + 1))
                if h or g >= 2:
                    pool.wait_ge(v_summed, count(n, h, NG2, g - 1))
                nc.gpsimd.tensor_tensor(flat(ev[(h * NG2 + g) % NEV], taps), flat(scores(h, g), taps),
                                        window(v[h % 2], h % 2, o, i, taps), ALU.mult).then_inc(weighted, 1)

            def multiply(n, h, g):
                pool.wait_ge(rel_added, count(n, h, K2, GROUPS2[g][0] + 1))
                if h or g >= NSE:
                    pool.wait_ge(e_summed, count(n, h, NG2, g - NSE + 1))
                    pool.wait_ge(weighted, count(n, h, NG2, g - NSE + 1))
                score_products(nc.gpsimd, h, g).then_inc(pool_multiplied, 1)

            def check_inverse(n, h):
                pool.wait_ge(near_steps, count(n, h, 2, 2))
                nc.gpsimd.tensor_tensor(es[:], es[:], rs[:], ALU.mult).then_inc(checked, 1)

            def half_band(n, h, first=False, final=False):
                for g in range(NG2):
                    if g == 2 and not first:
                        check_inverse(n, h - 1)
                    if g + POOL_AHEAD in ON_POOL:
                        multiply(n, h, g + POOL_AHEAD)
                    weigh(n, h, g)
                    if not final:
                        if g == EXT_GROUP[EXT - 1] - TOP_EARLY:
                            top_product(n, h + 1, 0)
                        if g == EXT_GROUP[2 * EXT - 1] - TOP_EARLY:
                            top_product(n, h + 1, 1)

            top_product(0, 0, 0)
            top_product(0, 0, 1)
            all_half_bands(pool, half_band)
            check_inverse(NT - 1, 1)

        @block.vector
        def _(dve):
            dve.wait_ge(consts_in, 80)

            def extreme_step(n, h, step):
                i, t = divmod(step, EXT)
                op = (ALU.max, ALU.min)[i]
                if step == 0:
                    dve.wait_ge(proj_copied, count(n, h, NPJ, NKEYS))
                if t == 0 and (h or i):
                    dve.wait_ge(top_parts, count(n, h, 2, i))
                if t > 0:
                    dve.wait_ge(ext_step, count(n, h, 2 * (EXT - 1), i * (EXT - 1) + t))
                if t < 3:
                    away = 1 if h % 2 == 0 else PW
                    size = HPX - (1, 3, 6)[t] * away
                    by = (1, 2, 3)[t] * away
                    src, dst = ((k[h % 2], m2), (m2, m4), (m4, m2))[t]
                    nc.vector.tensor_tensor(dst[:, 0:size], src[:, 0:size], src[:, by:by + size], op).then_inc(ext_step, 1)
                    return
                o = t - 3
                first = o * PW if h % 2 == 0 else o
                win = m2[:, first:first + 1]
                win = bass.AP(tensor=win.tensor, offset=win.offset, ap=[win.ap[0], [PW, R2], [1, WW]])
                to = ext[i][:].rearrange("p (r c) -> p r c", c=WW)
                r = rl[:, h % 2, o:o + 1]
                if o == 0:
                    if h:
                        dve.wait_ge(top_ready, count(n, h, 1, 0))
                    nc.vector.tensor_scalar(to, win, r, None, ALU.add).then_inc(ext_step, 1)
                else:
                    nc.vector.scalar_tensor_tensor(to, win, r, to, ALU.add, op)\
                        .then_inc(top_parts if o == K2 - 1 else ext_step, 1)

            def largest(n, h):
                dve.wait_ge(top_products, count(n, h, 2, 2))
                nc.vector.tensor_tensor(top[h % 2][:], ext[0][:], ext[1][:], ALU.max).then_inc(top_ready, 1)

            def multiply(n, h, g):
                dve.wait_ge(rel_added, count(n, h, K2, GROUPS2[g][0] + 1))
                if h or g >= NSE:
                    dve.wait_ge(e_summed, count(n, h, NG2, g - NSE + 1))
                    dve.wait_ge(weighted, count(n, h, NG2, g - NSE + 1))
                score_products(nc.vector, h, g).then_inc(multiplied, 1)

            def shift(n, h, g):
                taps = GROUPS2[g][2]
                on_pool = sum(p <= g for p in ON_POOL)
                if g in ON_POOL:
                    dve.wait_ge(pool_multiplied, count(n, h, len(ON_POOL), on_pool))
                else:
                    dve.wait_ge(multiplied, count(n, h, NG2 - len(ON_POOL), g + 1 - on_pool))
                if g == 0:
                    dve.wait_ge(top_ready, count(n, h, 1, 1))
                nc.vector.tensor_tensor(flat(scores(h, g), taps), flat(scores(h, g), taps), repeat(top[h % 2], taps),
                                        ALU.subtract).then_inc(shifted, 1)

            def invert(n, h):
                dve.wait_ge(checked, count(n, h, 1, 1))
                nc.vector.scalar_tensor_tensor(es[:], es[:], 2.0, rs[:], ALU.subtract, ALU.mult).then_inc(inverted, 1)

            def divide(n, h):
                dve.wait_ge(v_taken, count(n, h, 1, 1))
                dve.wait_ge(inverted, count(n, h, 1, 1))
                nc.vector.tensor_tensor(es[:], es[:], ws[:], ALU.mult).then_inc(divided, 1)

            def add(n, h):
                dve.wait_ge(turned_back, count(n, h, 1, 1))
                dve.wait_ge(rest_in[h % 2], (n + h // 2 + 1) * 16)
                for c in range(2):
                    s = slice(c * 512, (c + 1) * 512)
                    nc.vector.tensor_tensor(xr[h % 2][:, s], xr[h % 2][:, s], pback[:, c, :], ALU.subtract).then_inc(added, 1)

            def half_band(n, h, first=False, final=False):
                for g in range(NG2):
                    if g + 1 < NG2:
                        if g + 1 not in ON_POOL:
                            multiply(n, h, g + 1)
                    elif not final:
                        multiply(n, h + 1, 0)
                    if g == 0:
                        largest(n, h)
                    shift(n, h, g)
                    if not first:
                        if g == DIVIDE_AT:
                            invert(n, h - 1)
                            divide(n, h - 1)
                        if g == ADD_AT:
                            add(n, h - 1)
                    if not final:
                        for step in range(2 * EXT):
                            if EXT_GROUP[step] == g:
                                extreme_step(n, h + 1, step)

            for step in range(2 * EXT):
                extreme_step(0, 0, step)
            multiply(0, 0, 0)
            all_half_bands(dve, half_band)
            invert(NT - 1, 1)
            divide(NT - 1, 1)
            add(NT - 1, 1)


K3 = 4
HID = 65
TEMP = 0.5
KW3 = 3
TAPS = KW3 * KW3
R3 = 8
BPX3 = R3 * WW
HR3 = R3 + KW3 - 1


def dynamic_conv(nc, xn, pooled, x_in, x_out, w1_t, w2_t, b2, w_sets, ident_in):
    ctx = ExitStack()
    with ctx:
        sb = lambda n, s, dt=F32: ctx.enter_context(nc.sbuf_tensor(f"f_{n}", s, dt))
        pb = lambda n, s: ctx.enter_context(nc.psum_tensor(f"f_{n}", s, F32))
        sem = lambda n: nc.alloc_semaphore(name=f"f_{n}")
        KH = K3 * HALVES
        w1 = sb("w1", [PART, HALVES, HID])
        w2 = sb("w2", [HID, KH, PART])
        b2t = sb("b2t", [PART, KH])
        pl = sb("pl", [PART, HALVES, B])
        hid = sb("hid", [HID, B])
        lg = sb("lg", [PART, K3, HALVES * B])
        mx = sb("mx", [PART, HALVES * B])
        sm = sb("sm", [PART, HALVES * B])
        ident = sb("ident", [PART, PART])
        ws = sb("ws", [PART, K3, HALVES, TAPS * C])
        mw = [sb(f"mw{u}", [PART, HALVES, TAPS * C]) for u in range(2)]
        w_high = sb("w_high", [PART, HALVES, TAPS, C], F32R)
        w_low = sb("w_low", [PART, HALVES, TAPS, C], F32R)
        xb = [sb(f"xb{u}", [PART, HALVES, HR3 * PW]) for u in range(2)]
        x_high = [sb(f"x_high{u}", [PART, HALVES, HR3 * PW], F32R) for u in range(2)]
        x_low = [sb(f"x_low{u}", [PART, HALVES, HR3 * PW], F32R) for u in range(2)]
        xr = [sb(f"xr{u}", [PART, HALVES, BPX3]) for u in range(2)]
        pm = pb("pm", [PART, 2, 512])
        pw = pb("pw", [PART, 2, 512])
        pc = pb("pc", [PART, 2, HALVES, 512])
        consts_in = sem("consts_in")
        sets_in = [sem(f"sets_in{k}") for k in range(K3)]
        mlp_products = sem("mlp_products")
        hidden_ready = sem("hidden_ready")
        soft = sem("soft")
        mixed_part = sem("mixed_part")
        mixed = sem("mixed")
        turned = sem("turned")
        w_high_ready = sem("w_high_ready")
        w_low_ready = sem("w_low_ready")
        x_high_ready = sem("x_high_ready")
        x_low_ready = sem("x_low_ready")
        band_in = [sem(f"band_in{u}") for u in range(2)]
        rest_in = [sem(f"rest_in{u}") for u in range(2)]
        convolved = [sem(f"convolved{u}") for u in range(2)]
        added = [sem(f"added{u}") for u in range(2)]
        stored = [sem(f"stored{u}") for u in range(2)]
        TURNS = HH // R3 // 2
        NTURN = TAPS * HALVES * HALVES // 4
        block = ctx.enter_context(nc.Block())

        @block.sync
        def _(sp):
            slow = dict(allow_slow_non_contiguous=True)
            sp.dma_start(w1[:], w1_t.rearrange("(h p) o -> p h o", p=PART)).then_inc(consts_in, 16)
            sp.dma_start(w2[:].rearrange("p k o -> p (k o)"), w2_t).then_inc(consts_in, 16)
            sp.dma_start(b2t[:], b2.rearrange("(m p) -> p m", p=PART), **slow).then_inc(consts_in, 16)
            for b in range(B):
                sp.dma_start(pl[:, :, b], pooled[b].rearrange("(h p) -> p h", p=PART), **slow).then_inc(consts_in, 16)
            sp.dma_start(ident[:], ident_in).then_inc(consts_in, 16)
            for k in range(K3):
                sp.dma_start(ws[:, k], w_sets[k].rearrange("(h p) n -> p h n", p=PART)).then_inc(sets_in[k], 16)

            def band(t, n, u):
                return t[bass.ds(n // TURNS, 1), :, bass.ds((n % TURNS) * (2 * BPX3) + u * BPX3, BPX3)]\
                    .rearrange("b (h p) n -> p (b h) n", p=PART)

            def load_band(n, u):
                first = (PAD - KW3 // 2 + u * R3) * PW
                sp.dma_start(xb[u][:], xn[bass.ds(n // TURNS, 1), :, bass.ds((n % TURNS) * (2 * R3 * PW) + first, HR3 * PW)]
                             .rearrange("b (h p) n -> p (b h) n", p=PART)).then_inc(band_in[u], 16)

            def load_rest(n, u):
                sp.dma_start(xr[u][:], band(x_in, n, u)).then_inc(rest_in[u], 16)

            def store(n, u):
                sp.wait_ge(added[u], (n + 1) * HALVES)
                sp.dma_start(band(x_out, n, u), xr[u][:]).then_inc(stored[u], 16)

            for u in range(2):
                load_band(0, u)
                load_rest(0, u)
            with sp.Fori(1, B * TURNS) as n:
                for u in range(2):
                    sp.wait_ge(x_low_ready, n * 2 + u - 1)
                    load_band(n, u)
                for u in range(2):
                    store(n - 1, u)
                    sp.wait_ge(stored[u], n * 16)
                    load_rest(n, u)
            for u in range(2):
                store(B * TURNS - 1, u)
            for u in range(2):
                sp.wait_ge(stored[u], B * TURNS * 16)

        @block.gpsimd
        def _(pool):
            def split(n, u, first=False):
                pool.wait_ge(x_high_ready, n * 2 + u + 1)
                if not first:
                    pool.wait_ge(convolved[u], n * HALVES)
                flat = lambda t: t[:].rearrange("p h n -> p (h n)")
                nc.gpsimd.tensor_tensor(flat(x_low[u]), flat(xb[u]), flat(x_high[u]).bitcast(F32), ALU.subtract)\
                    .then_inc(x_low_ready, 1)

            for u in range(2):
                split(0, u, first=True)
            with pool.Fori(1, B * TURNS) as n:
                for u in range(2):
                    split(n, u)

        @block.tensor
        def _(pe):
            pe.wait_ge(consts_in, (4 + B) * 16)
            for h in range(HALVES):
                last = nc.tensor.matmul(pm[0:HID, 0, 0:B], lhsT=w1[:, h], rhs=pl[:, h], start=h == 0, stop=h == 1)
            last.then_inc(mlp_products, 1)
            pe.wait_ge(hidden_ready, 1)
            for m in range(KH):
                last = nc.tensor.matmul(pm[:, 1, m * B:(m + 1) * B], lhsT=w2[:, m], rhs=hid[:], start=True, stop=True)
            last.then_inc(mlp_products, 1)
            for b in range(B):
                pe.wait_ge(mixed, (b + 1) * HALVES)
                for j in range(NTURN):
                    if b or j >= 2:
                        pe.wait_ge(w_low_ready, b * NTURN + j - 1)
                    for i in range(4):
                        t, g = divmod(j * 2 + i // 2, HALVES)
                        o = i % 2
                        last = nc.tensor.transpose(pw[:, j % 2, i * PART:(i + 1) * PART],
                                                   mw[b % 2][:, o, t * C + g * PART:t * C + (g + 1) * PART], ident[:])
                    last.then_inc(turned, 1)
                pe.wait_ge(w_low_ready, (b + 1) * NTURN)
                with pe.Fori(0, TURNS) as r:
                    n = r + b * TURNS
                    for u in range(2):
                        pe.wait_ge(x_low_ready, n * 2 + u + 1)
                        pe.wait_ge(added[u], n * HALVES)
                        high, low = (t[:].rearrange("p h (r c) -> p h r c", c=PW) for t in (x_high[u], x_low[u]))
                        for m in range(HALVES):
                            for t in range(TAPS):
                                dy, dx = divmod(t, KW3)
                                for g in range(HALVES):
                                    c0 = PAD - KW3 // 2 + dx
                                    for i, (w, x) in enumerate(((w_high, high), (w_high, low), (w_low, high))):
                                        last = nc.tensor.matmul(pc[:, u, m].rearrange("p (r c) -> p r c", c=WW),
                                                                lhsT=w[:, g, t, m * PART:(m + 1) * PART],
                                                                rhs=x[:, g, dy:dy + R3, c0:c0 + WW],
                                                                start=t == 0 and g == 0 and i == 0,
                                                                stop=t == TAPS - 1 and g == 1 and i == 2)
                            last.then_inc(convolved[u], 1)

        @block.scalar
        def _(act):
            act.wait_ge(mlp_products, 1)
            nc.scalar.activation(hid[:], pm[0:HID, 0, 0:B], ACT.Relu).then_inc(hidden_ready, 1)
            act.wait_ge(soft, KH + 2)
            nc.scalar.activation(lg[:].rearrange("p k n -> p (k n)"), lg[:].rearrange("p k n -> p (k n)"), ACT.Exp,
                                 scale=1.0 / TEMP).then_inc(soft, 1)
            for b in range(B):
                for j in range(NTURN):
                    act.wait_ge(turned, b * NTURN + j + 1)
                    if b:
                        for u in range(2):
                            act.wait_ge(convolved[u], b * TURNS * HALVES)
                    src = pw[:, j % 2].rearrange("p (g o) -> p g o", g=2)
                    nc.scalar.activation(w_high[:, :, j, :], src, ACT.Copy).then_inc(w_high_ready, 1)
                with act.Fori(0, TURNS) as r:
                    n = r + b * TURNS
                    for u in range(2):
                        act.wait_ge(band_in[u], n * 16 + 16)
                        act.wait_ge(convolved[u], n * HALVES)
                        nc.scalar.activation(x_high[u][:], xb[u][:], ACT.Copy).then_inc(x_high_ready, 1)

        @block.vector
        def _(dve):
            dve.wait_ge(consts_in, (4 + B) * 16)
            dve.wait_ge(mlp_products, 2)
            flat = lg[:].rearrange("p k (h b) -> p (k h) b", b=B)
            for m in range(KH):
                nc.vector.tensor_scalar(flat[:, m], pm[:, 1, m * B:(m + 1) * B], b2t[:, m:m + 1], None, ALU.add)\
                    .then_inc(soft, 1)
            dve.wait_ge(soft, KH)
            by_k = lg[:].rearrange("p k n -> p n k")
            nc.vector.tensor_reduce(mx[:], by_k, AX.X, ALU.max).then_inc(soft, 1)
            dve.wait_ge(soft, KH + 1)
            rep = lambda t: t[:].rearrange("p (o n) -> p o n", o=1).to_broadcast([PART, K3, HALVES * B])
            nc.vector.tensor_tensor(lg[:], lg[:], rep(mx), ALU.subtract).then_inc(soft, 1)
            dve.wait_ge(soft, KH + 3)
            nc.vector.tensor_reduce(sm[:], by_k, AX.X, ALU.add).then_inc(soft, 1)
            dve.wait_ge(soft, KH + 4)
            nc.vector.reciprocal(sm[:], sm[:]).then_inc(soft, 1)
            dve.wait_ge(soft, KH + 5)
            nc.vector.tensor_tensor(lg[:], lg[:], rep(sm), ALU.mult).then_inc(soft, 1)
            dve.wait_ge(soft, KH + 6)

            def mix(b):
                if b >= 2:
                    dve.wait_ge(turned, (b - 1) * NTURN)
                for k in range(K3):
                    dve.wait_ge(sets_in[k], 16)
                    for o in range(HALVES):
                        s = lg[:, k, o * B + b:o * B + b + 1]
                        to = mw[b % 2][:, o]
                        if k == 0:
                            ins = nc.vector.tensor_scalar(to, ws[:, k, o], s, None, ALU.mult)
                        else:
                            dve.wait_ge(mixed_part, (b * (K3 - 1) + k - 1) * HALVES + o + 1)
                            ins = nc.vector.scalar_tensor_tensor(to, ws[:, k, o], s, to, ALU.mult, ALU.add)
                        ins.then_inc(mixed if k == K3 - 1 else mixed_part, 1)

            mix(0)
            for b in range(B):
                for j in range(NTURN):
                    dve.wait_ge(w_high_ready, b * NTURN + j + 1)
                    nc.vector.tensor_tensor(w_low[:, :, j, :], pw[:, j % 2].rearrange("p (g o) -> p g o", g=2),
                                            w_high[:, :, j, :].bitcast(F32), ALU.subtract).then_inc(w_low_ready, 1)
                if b + 1 < B:
                    mix(b + 1)
                with dve.Fori(0, TURNS) as r:
                    n = r + b * TURNS
                    for u in range(2):
                        dve.wait_ge(rest_in[u], n * 16 + 16)
                        for m in range(HALVES):
                            dve.wait_ge(convolved[u], n * HALVES + m + 1)
                            nc.vector.tensor_tensor(xr[u][:, m], pc[:, u, m], xr[u][:, m], ALU.add).then_inc(added[u], 1)


def four_layers(nc, x, out, w):
    def scratch(name, shape):
        return nc.dram_tensor(name, shape, F32, kind="Internal").ap()

    xn = [scratch(f"xn{i}", [B, C, PPX]) for i in range(4)]
    xs = [x] + [scratch(f"x{i}", [B, C, NPX]) for i in (1, 2, 3)] + [out]
    qkv = scratch("qkv", [B, GROUPS, GPX])
    agg = scratch("agg", [B, GROUPS, GPX])
    pooled = scratch("pooled", [B, C])

    norm_sems = norm_semaphores(nc)
    group_norm(nc, norm_sems, 0, xs[0], xn[0], w["group_mean"])
    window_attention(nc, xn[0], xs[0], xs[1], w["L0_w_qkv_t"], w["L0_b_qkv"], w["attention_masks"], w["identity"])
    group_norm(nc, norm_sems, 1, xs[1], xn[1], w["group_mean"])
    qkv_project(nc, xn[1], qkv, w["L1_w_qkv_t"])
    grouped_conv(nc, qkv, agg, w["L1_w_dw"], w["L1_w_pw"], w["row_masks"])
    linear_attention(nc, [qkv, agg], xs[1], xs[2], w["L1_w_proj_t"], w["head_mask"], w["identity"])
    group_norm(nc, norm_sems, 2, xs[2], xn[2], w["group_mean"])
    channel_attention(nc, xn[2], xs[2], xs[3], w["L2_w_t"], w["L2_rel"], w["identity"])
    group_norm(nc, norm_sems, 3, xs[3], xn[3], w["group_mean"], pooled=pooled)
    dynamic_conv(nc, xn[3], pooled, xs[3], xs[4], w["L3_w1_t"], w["L3_w2_t"], w["L3_b2"], w["L3_w_sets"], w["identity"])


def laid_out(i):
    a = {k: np.asarray(v) for k, v in i.items()}
    return {
        "L0_w_qkv_t": a["L0_conv_w_qkv"].T,
        "L0_b_qkv": a["L0_conv_b_qkv"],
        "L1_w_qkv_t": a["L1_conv_w_qkv"].reshape(C3, C)[permuted_channels()].T,
        "L1_w_dw": a["L1_conv_w_dw"].reshape(GROUPS, G8, K1 * K1).transpose(1, 0, 2).reshape(G8, -1),
        "L1_w_pw": a["L1_conv_w_pw"].reshape(GROUPS, G8, G8).transpose(2, 0, 1).reshape(G8, -1),
        "L1_w_proj_t": a["L1_conv_w_proj"].reshape(C, ST * PART).T[head_channels()],
        "L2_w_t": np.stack([a[f"L2_conv_w_{c}"].T for c in "qkv"]),
        "L2_rel": np.concatenate([a["L2_conv_rel_h"].reshape(C // 2, K2), a["L2_conv_rel_w"].reshape(C // 2, K2)]),
        "L3_w1_t": a["L3_conv_w1"].T,
        "L3_w2_t": a["L3_conv_w2"].T,
        "L3_b2": a["L3_conv_b2"],
        "L3_w_sets": a["L3_conv_weight"].reshape(K3, C, C, TAPS).transpose(0, 1, 3, 2).reshape(K3, C, TAPS * C),
        "group_mean": group_mean(),
        "attention_masks": attention_masks(),
        "row_masks": row_masks(),
        "head_mask": head_mask(),
        "identity": np.eye(PART, dtype=np.float32),
    }


def kernel(**inputs):
    import concourse.bacc as _bacc
    from concourse.bass_utils import run_bass_kernel_spmd as _run

    x = np.asarray(inputs["x"])
    arrays = {"x": np.ascontiguousarray(x.reshape(B, C, NPX))}
    arrays.update((k, np.ascontiguousarray(v)) for k, v in laid_out(inputs).items())
    nc = _bacc.Bacc("TRN2", target_bir_lowering=False, num_devices=1)
    aps = {k: nc.dram_tensor(f"in_{k}", v.shape, mybir.dt.from_np(v.dtype), kind="ExternalInput").ap()
           for k, v in arrays.items()}
    out = nc.dram_tensor("out_x", (B, C, NPX), F32, kind="ExternalOutput").ap()
    four_layers(nc, aps["x"], out, aps)
    r = _run(nc, [{f"in_{k}": v for k, v in arrays.items()}], core_ids=[0])
    return r.results[0]["out_x"].reshape(x.shape)
```
